# Optimizing a Trainium2 kernel written in Bass

```python
import numpy as np
import jax
import jax.numpy as jnp

def _softmax(x, axis=-1):
    return jax.nn.softmax(x, axis=axis)

def _gelu(x):
    return jax.nn.gelu(x, approximate=True)

def _silu(x):
    return jax.nn.silu(x)

def _sigmoid(x):
    return jax.nn.sigmoid(x)

def _layernorm(x, axis=-1, eps=1e-05):
    m = jnp.mean(x, axis=axis, keepdims=True)
    v = jnp.var(x, axis=axis, keepdims=True)
    return (x - m) / jnp.sqrt(v + eps)

def _scatter_add(tgt, idx, src, axis=0):
    return tgt.at[idx].add(src)

def _segment_sum(src, seg, n):
    return jax.ops.segment_sum(src, seg, n)
kernel_name = 'mk_gnn_resnorm_d2_gnn_r8_1626a9'

def setup_inputs(seed: int=0):
    np.random.seed(seed)
    _w = jnp.asarray

    def _rec_inputs():
        import jax
        import jax.numpy as jnp
        _gk = jax.random.key(seed)
        x = -0.0001126 + 1 * jax.random.normal(jax.random.fold_in(_gk, 1), (1250, 768), jnp.float32)
        _s = jax.random.randint(jax.random.fold_in(_gk, 2), (20000,), 0, 1250, jnp.int32)
        _d = jax.random.randint(jax.random.fold_in(_gk, 3), (20000,), 0, 1250, jnp.int32)
        _loop = jnp.arange(1250, dtype=jnp.int32)
        src = jnp.concatenate([_s, _d, _loop])
        dst = jnp.concatenate([_d, _s, _loop])
        _o = jnp.argsort(dst, stable=True)
        src = src[_o]
        dst = dst[_o]
        edge_weight1 = -0.00472126 + 0.997171 * jax.random.normal(jax.random.fold_in(_gk, 13), (41250, 1), jnp.float32)
        return (x, src, dst, edge_weight1)
    x, src, dst, edge_weight1 = _rec_inputs()

    def _L0_gnn_setup():
        import jax, jax.numpy as jnp
        import numpy as np
        N, E, D, H, C = (1250, 12500, 768, 4, 192)
        NEG_SLOPE = 0.2

        def gat_conv(x, src, dst, W, a_src, a_dst, b):
            h = (x @ W).reshape(N, H, C)
            as_n = (h * a_src).sum(-1)
            ad_n = (h * a_dst).sum(-1)
            e = jax.nn.leaky_relu(as_n[src] + ad_n[dst], NEG_SLOPE)
            m = jax.ops.segment_max(e, dst, num_segments=N)
            p = jnp.exp(e - m[dst])
            s = jax.ops.segment_sum(p, dst, num_segments=N)
            alpha = p / (s[dst] + 1e-16)
            out = jax.ops.segment_sum(alpha[:, :, None] * h[src], dst, num_segments=N)
            return out.reshape(N, H * C) + b
        key = jax.random.key(seed)
        ks = jax.random.split(key, 16)
        w = lambda k, shape: jax.random.normal(k, shape, dtype=jnp.float32) * 0.02
        inp = {}
        inp['x'] = jax.random.normal(ks[0], (N, D), dtype=jnp.float32)
        inp['edge_index'] = jax.random.randint(ks[1], (2, E), 0, N, dtype=jnp.int32)
        inp['batch'] = jnp.zeros((N,), dtype=jnp.int32)
        inp['edge_attr'] = jax.random.normal(ks[2], (E, 1), dtype=jnp.float32)
        inp['W_ah'] = w(ks[3], (D, D))
        inp['b_ah'] = jnp.zeros((D,), jnp.float32)
        for i in range(3):
            inp[f'W{i}'] = w(ks[4 + 3 * i], (D, H * C))
            inp[f'a_src{i}'] = w(ks[5 + 3 * i], (H, C))
            inp[f'a_dst{i}'] = w(ks[6 + 3 * i], (H, C))
            inp[f'b{i}'] = jnp.zeros((H * C,), jnp.float32)
        inp['W_out'] = w(ks[13], (3 * D, D))
        inp['b_out'] = jnp.zeros((D,), jnp.float32)
        return inp
    _L0_gnn_all = _L0_gnn_setup()
    _L0_gnn_in = {k: v for k, v in _L0_gnn_all.items() if k in ('W_ah', 'b_ah', 'W0', 'a_src0', 'a_dst0', 'b0', 'W1', 'a_src1', 'a_dst1', 'b1', 'W2', 'a_src2', 'a_dst2', 'b2', 'W_out', 'b_out')}
    del _L0_gnn_all

    def _L1_gnn_setup():
        import jax, jax.numpy as jnp
        import numpy as np
        N_NODES = 1250
        D = 768
        N_EDGES = 20000

        def gcn_conv(x, W, b, src, dst, n_nodes):
            h = x @ W
            deg = jax.ops.segment_sum(jnp.ones_like(dst, dtype=h.dtype), dst, num_segments=n_nodes)
            dinv = jnp.where(deg > 0, jax.lax.rsqrt(deg), 0.0)
            norm = dinv[src] * dinv[dst]
            msgs = h[src] * norm[:, None]
            out = jax.ops.segment_sum(msgs, dst, num_segments=n_nodes)
            return out + b

        def add_self_loops(edge_index, n_nodes):
            loop = jnp.arange(n_nodes, dtype=edge_index.dtype)
            src = jnp.concatenate([edge_index[0], loop])
            dst = jnp.concatenate([edge_index[1], loop])
            return (src, dst)
        key = jax.random.key(seed)
        k1, k2, k3, k4 = jax.random.split(key, 4)
        x = jax.random.normal(k1, (N_NODES, D), dtype=jnp.float32)
        edge_index = jax.random.randint(k2, (2, N_EDGES), 0, N_NODES, dtype=jnp.int32)
        glorot = float(np.sqrt(6.0 / (D + D)))
        W1 = jax.random.uniform(k3, (D, D), jnp.float32, -glorot, glorot)
        W2 = jax.random.uniform(k4, (D, D), jnp.float32, -glorot, glorot)
        b1 = jnp.zeros((D,), jnp.float32)
        b2 = jnp.zeros((D,), jnp.float32)
        return {'x': x, 'W1': W1, 'b1': b1, 'W2': W2, 'b2': b2, 'edge_index': edge_index}
    _L1_gnn_all = _L1_gnn_setup()
    _L1_gnn_in = {k: v for k, v in _L1_gnn_all.items() if k in ('W1', 'b1', 'W2', 'b2')}
    del _L1_gnn_all
    return {'x': x, 'src': src, 'dst': dst, 'edge_weight1': edge_weight1, 'L0_gnn_W_ah': _L0_gnn_in['W_ah'], 'L0_gnn_b_ah': _L0_gnn_in['b_ah'], 'L0_gnn_W0': _L0_gnn_in['W0'], 'L0_gnn_a_src0': _L0_gnn_in['a_src0'], 'L0_gnn_a_dst0': _L0_gnn_in['a_dst0'], 'L0_gnn_b0': _L0_gnn_in['b0'], 'L0_gnn_W1': _L0_gnn_in['W1'], 'L0_gnn_a_src1': _L0_gnn_in['a_src1'], 'L0_gnn_a_dst1': _L0_gnn_in['a_dst1'], 'L0_gnn_b1': _L0_gnn_in['b1'], 'L0_gnn_W2': _L0_gnn_in['W2'], 'L0_gnn_a_src2': _L0_gnn_in['a_src2'], 'L0_gnn_a_dst2': _L0_gnn_in['a_dst2'], 'L0_gnn_b2': _L0_gnn_in['b2'], 'L0_gnn_W_out': _L0_gnn_in['W_out'], 'L0_gnn_b_out': _L0_gnn_in['b_out'], 'L1_gnn_W1': _L1_gnn_in['W1'], 'L1_gnn_b1': _L1_gnn_in['b1'], 'L1_gnn_W2': _L1_gnn_in['W2'], 'L1_gnn_b2': _L1_gnn_in['b2']}

def reference(x, src, dst, edge_weight1, L0_gnn_W_ah, L0_gnn_b_ah, L0_gnn_W0, L0_gnn_a_src0, L0_gnn_a_dst0, L0_gnn_b0, L0_gnn_W1, L0_gnn_a_src1, L0_gnn_a_dst1, L0_gnn_b1, L0_gnn_W2, L0_gnn_a_src2, L0_gnn_a_dst2, L0_gnn_b2, L0_gnn_W_out, L0_gnn_b_out, L1_gnn_W1, L1_gnn_b1, L1_gnn_W2, L1_gnn_b2):
    import jax
    import jax.numpy as jnp

    def _L0_gnn_ref(x, edge_index, batch, edge_attr, W_ah, b_ah, W0, a_src0, a_dst0, b0, W1, a_src1, a_dst1, b1, W2, a_src2, a_dst2, b2, W_out, b_out):
        import jax, jax.numpy as jnp
        import numpy as np
        N, E, D, H, C = (1250, 12500, 768, 4, 192)
        NEG_SLOPE = 0.2

        def gat_conv(x, src, dst, W, a_src, a_dst, b):
            h = (x @ W).reshape(N, H, C)
            as_n = (h * a_src).sum(-1)
            ad_n = (h * a_dst).sum(-1)
            e = jax.nn.leaky_relu(as_n[src] + ad_n[dst], NEG_SLOPE)
            m = jax.ops.segment_max(e, dst, num_segments=N)
            p = jnp.exp(e - m[dst])
            s = jax.ops.segment_sum(p, dst, num_segments=N)
            alpha = p / (s[dst] + 1e-16)
            out = jax.ops.segment_sum(alpha[:, :, None] * h[src], dst, num_segments=N)
            return out.reshape(N, H * C) + b
        loops = jnp.arange(N, dtype=edge_index.dtype)
        src = jnp.concatenate([edge_index[0], loops])
        dst = jnp.concatenate([edge_index[1], loops])
        x1 = jax.nn.relu(x @ W_ah + b_ah)
        xs = [jax.nn.relu(gat_conv(x1, src, dst, W, a_s, a_d, b)) for W, a_s, a_d, b in ((W0, a_src0, a_dst0, b0), (W1, a_src1, a_dst1, b1), (W2, a_src2, a_dst2, b2))]
        node_emb = jnp.concatenate(xs, axis=1)
        return jax.nn.relu(node_emb @ W_out + b_out)

    def _L1_gnn_ref(x, W1, b1, W2, b2, edge_index):
        import jax, jax.numpy as jnp
        import numpy as np
        N_NODES = 1250
        D = 768
        N_EDGES = 20000

        def gcn_conv(x, W, b, src, dst, n_nodes):
            h = x @ W
            deg = jax.ops.segment_sum(jnp.ones_like(dst, dtype=h.dtype), dst, num_segments=n_nodes)
            dinv = jnp.where(deg > 0, jax.lax.rsqrt(deg), 0.0)
            norm = dinv[src] * dinv[dst]
            msgs = h[src] * norm[:, None]
            out = jax.ops.segment_sum(msgs, dst, num_segments=n_nodes)
            return out + b

        def add_self_loops(edge_index, n_nodes):
            loop = jnp.arange(n_nodes, dtype=edge_index.dtype)
            src = jnp.concatenate([edge_index[0], loop])
            dst = jnp.concatenate([edge_index[1], loop])
            return (src, dst)
        n = x.shape[0]
        src, dst = add_self_loops(edge_index, n)
        h = gcn_conv(x, W1, b1, src, dst, n)
        h = jax.nn.relu(h)
        out = gcn_conv(h, W2, b2, src, dst, n)
        return out
    edge_index = jnp.stack([src, dst])
    batch0 = jnp.zeros((1250,), jnp.int32)
    x = _layernorm(x + _L0_gnn_ref(x, edge_index, batch0, edge_weight1, L0_gnn_W_ah, L0_gnn_b_ah, L0_gnn_W0, L0_gnn_a_src0, L0_gnn_a_dst0, L0_gnn_b0, L0_gnn_W1, L0_gnn_a_src1, L0_gnn_a_dst1, L0_gnn_b1, L0_gnn_W2, L0_gnn_a_src2, L0_gnn_a_dst2, L0_gnn_b2, L0_gnn_W_out, L0_gnn_b_out), axis=-1)
    x = _layernorm(x + _L1_gnn_ref(x, L1_gnn_W1, L1_gnn_b1, L1_gnn_W2, L1_gnn_b2, edge_index), axis=-1)
    return x

_drawn_inputs = setup_inputs


def setup_inputs(seed=0):
    import zlib

    import numpy as np

    out = dict(_drawn_inputs(seed))
    spreads = {'L0_gnn_b_ah': (0.0, 0.587),
     'L0_gnn_b0': (0.0, 0.281),
     'L0_gnn_b1': (0.0, 0.3),
     'L0_gnn_b2': (0.0, 0.297),
     'L0_gnn_b_out': (0.0, 0.1),
     'L1_gnn_b1': (0.0, 0.1),
     'L1_gnn_b2': (0.0, 0.1)}
    factors = {'L0_gnn_W_ah': 3.924,
     'L0_gnn_a_src0': 8.0,
     'L0_gnn_a_dst0': 29.472,
     'L0_gnn_a_src1': 8.0,
     'L0_gnn_a_dst1': 29.483,
     'L0_gnn_a_src2': 8.0,
     'L0_gnn_a_dst2': 34.984}
    for name, (base, spread) in spreads.items():
        noise = np.random.default_rng([zlib.crc32(name.encode()), seed]).standard_normal(out[name].shape)
        drawn = base * np.exp(spread * noise) if base else spread * noise
        out[name] = jnp.asarray(drawn.astype(out[name].dtype))
    for name, factor in factors.items():
        out[name] = (out[name] * factor).astype(out[name].dtype)
    return out
```

```python
from contextlib import ExitStack

import concourse.bass as bass
from concourse import mybir

F32 = mybir.dt.float32
F32R = mybir.dt.float32r
BF16 = mybir.dt.bfloat16
F16 = mybir.dt.float16
I32 = mybir.dt.int32
ALU = mybir.AluOpType
ACT = mybir.ActivationFunctionType
AX_X = mybir.AxisListType.X

N = 1250
T = 125
NT = N // T
PAIRS = NT // 2
D = 768
KF = D // 128
LAYERS = 3
HEADS = 4
C = D // HEADS
HALL = LAYERS * HEADS
DA = D + 2 * HEADS
KO = LAYERS * D // 128
E = 41250
CHUNKS = -(-E // 128)
FULL = E // 128
CROWS = 3
CCOLS = CROWS * 128
PAD_NODE = 2000
CSTEP = 3
SW = 417
FAR = 1e30
NO_MAX = -3e38
EXP_CAP = 1e30
SLOPE = 0.2
LN_EPS = 1e-5
WP = 2
HALF = N // 2
GT = NT // 2
RING = 4


def three_passes(nc, out, lhs, rhs, first, last):
    nc.tensor.matmul(out, lhs[0], rhs[0], start=first, stop=False)
    nc.tensor.matmul(out, lhs[0], rhs[1], start=False, stop=False)
    return nc.tensor.matmul(out, lhs[1], rhs[0], start=False, stop=last)


def hold(eng, held, semaphore, value):
    eng.wait_ge(semaphore, value)
    eng.sem_inc(held, 1)


class Core:

    def __init__(self, nc, ctx):
        self.nc, self.ctx = nc, ctx

    def sem(self, name):
        return self.ctx.enter_context(self.nc.semaphore(name))

    def dram(self, name, shape, dt=F32):
        return self.nc.dram_tensor(name, shape, dt, kind="Internal").ap()


def nodes_in(nc, k, a):
    with ExitStack() as mem:
        def sb(name, shape, dt=F32):
            return mem.enter_context(nc.sbuf_tensor(name, shape, dt))

        ones = sb("ones", [128, NT])
        tile_lo_i = sb("tile_lo_i", [NT, 1], I32)
        tile_lo = sb("tile_lo", [NT, 2])
        chunk_no = sb("chunk_no", [NT, 2, CCOLS])
        edge_i = sb("edge_i", [128, 2, CROWS, 128], I32)
        edge_f = sb("edge_f", [128, 2, CROWS, 128])
        span = sb("span", [128, 2, CROWS])
        span_diag = sb("span_diag", [128, 2, CROWS, 128])
        meets = sb("meets", [NT, 2, CCOLS])
        ranges = sb("ranges", [NT, 2])
        ranges_i = sb("ranges_i", [NT, 2], I32)
        w_raw = sb("wah_raw", [128, KF, D])
        w_hi = sb("wah_hi", [128, KF, D], F32R)
        w_lo = sb("wah_lo", [128, KF, D], F32R)
        bias = sb("bah_col", [128, KF])
        x_in = sb("x_in", [T, 2, D])
        xT_hi = sb("xT_hi", [128, KF, 2 * T], F32R)
        xT_lo = sb("xT_lo", [128, KF, 2 * T], F32R)
        x1 = sb("x1_pair", [128, KF, 2 * T])
        ps = k.ps

        pads_set = k.sem("pads_set")
        fills = k.sem("fills")
        iota_ready = k.sem("iota_ready")
        consts_ready = k.sem("consts_ready")
        edges_loaded = k.sem("edges_loaded")
        weights_loaded = k.sem("weights_loaded")
        bias_loaded = k.sem("bias_loaded")
        x_loaded = k.sem("x_loaded")
        vec_step = k.sem("vec_step")
        edges_float = k.sem("edges_float")
        edges_turned = k.sem("edges_turned")
        diag_ready = k.sem("diag_ready")
        span_spread = k.sem("span_spread")
        ranges_ready = k.sem("ranges_ready")
        ranges_moved = k.sem("ranges_moved")
        wah_hi_ready = k.sem("wah_hi_ready")
        wah_lo_ready = k.sem("wah_lo_ready")
        x_turned = k.sem("x_turned")
        xT_hi_ready = k.sem("xT_hi_ready")
        xT_lo_ready = k.sem("xT_lo_ready")
        x1_summed = k.sem("x1_summed")
        x1_copied = k.sem("x1_copied")
        x1_hi_ready = k.sem("x1_hi_ready")
        x1_lo_ready = k.sem("x1_lo_ready")

        turned = ps[:, 3:6, 0:4 * T]
        summed = ps[:, 0:3, :].rearrange("p b (m n) -> p (b m) n", m=2)

        block = mem.enter_context(nc.Block())
        x_pairs = a["x"].rearrange("(i j p) f -> p i j f", j=2, p=T)

        @block.sync
        def _(sp):
            sp.wait_ge(pads_set, 1)
            for which, arr in ((0, a["src"]), (1, a["dst"])):
                rows = arr[0:FULL * 128].rearrange("(r f) -> r f", f=128)
                sp.dma_start(edge_i[:, which, 0:2, :],
                             rows[0:256, :].rearrange("(c p) f -> p c f", p=128)).then_inc(edges_loaded, 16)
                sp.dma_start(edge_i[0:FULL - 256, which, 2, :], rows[256:FULL, :]).then_inc(edges_loaded, 16)
                sp.dma_start(edge_i[FULL - 256:FULL - 255, which, 2, 0:E - FULL * 128],
                             arr[FULL * 128:E].rearrange("(r f) -> r f", r=1)).then_inc(edges_loaded, 16)
            sp.dma_start(x_in[:, :, :], x_pairs[:, 0, :, :]).then_inc(x_loaded, 16)
            with sp.Fori(1, PAIRS) as i:
                sp.wait_ge(x_turned, i)
                sp.dma_start(x_in[:, :, :], x_pairs[:, bass.ds(i, 1), :, :].rearrange("p i j f -> p (i j) f")
                             ).then_inc(x_loaded, 16)
            sp.wait_ge(ranges_ready, 1)
            for n in range(2):
                sp.dma_start(k.ranges_row[0:1, n * NT:(n + 1) * NT], ranges_i[:, n:n + 1]).then_inc(ranges_moved, 16)
            sp.wait_ge(ranges_moved, 32)

        @block.gpsimd
        def _(pool):
            nc.gpsimd.memset(edge_i[:, :, :, :], PAD_NODE).then_inc(pads_set, 1)
            nc.gpsimd.memset(k.ident[:, :], 0.0).then_inc(fills, 1)
            nc.gpsimd.memset(k.loop_strip[:, :], 0.0).then_inc(fills, 1)
            nc.gpsimd.iota(k.iota_i[:, :], pattern=[[1, 3 * SW]], base=0, channel_multiplier=0).then_inc(iota_ready, 1)
            nc.gpsimd.iota(tile_lo_i[:, :], pattern=[[0, 1]], base=0, channel_multiplier=T).then_inc(iota_ready, 1)
            pool.wait_ge(fills, 2)
            nc.gpsimd.affine_select(out=k.ident[:, :], in_=k.ident[:, :], compare_op=ALU.not_equal, fill=1.0, base=0,
                                    pattern=[[-1, 128]], channel_multiplier=1).then_inc(consts_ready, 1)
            nc.gpsimd.affine_select(out=k.loop_strip[:, N:N + T], in_=k.loop_strip[:, N:N + T],
                                    compare_op=ALU.not_equal, fill=1.0, base=0, pattern=[[-1, T]],
                                    channel_multiplier=1).then_inc(consts_ready, 1)
            nc.gpsimd.memset(ones[:, :], 1.0).then_inc(consts_ready, 1)
            nc.gpsimd.memset(k.zeros[:, :], 0.0).then_inc(consts_ready, 1)
            nc.gpsimd.memset(k.far[:, :], FAR).then_inc(consts_ready, 1)
            nc.gpsimd.memset(k.eps[:, :], LN_EPS).then_inc(consts_ready, 1)
            nc.gpsimd.memset(k.neg_half[:, :], -0.5).then_inc(consts_ready, 1)
            with pool.Fori(0, PAIRS) as i:
                hold(pool, k.held, x1_copied, (i + 1) * KF)
                nc.gpsimd.tensor_copy(k.x1_hi[:, :, bass.ds(2 * T * i, 2 * T)], x1[:, :, :]).then_inc(x1_hi_ready, 1)

        @block.vector
        def _(dve):
            done = [0]

            def link(ins):
                done[0] += 1
                ins.then_inc(vec_step, 1)
                dve.wait_ge(vec_step, done[0])

            dve.wait_ge(iota_ready, 2)
            nc.vector.tensor_copy(k.iota_h[:, :], k.iota_i[:, :])
            link(nc.vector.tensor_copy(tile_lo[:, 0:1], tile_lo_i[:, :]))
            nc.vector.tensor_scalar(tile_lo[:, 1:2], tile_lo[:, 0:1], float(T), None, ALU.add)
            link(nc.vector.tensor_copy(chunk_no[:, 0, :], k.iota_i[0:NT, 0:CCOLS]))
            link(nc.vector.tensor_scalar(chunk_no[:, 1, :], chunk_no[:, 0, :], -1.0, CCOLS - 1.0, ALU.mult, ALU.add))
            dve.wait_ge(edges_loaded, 96)
            nc.vector.tensor_copy(edge_f[:, :, :, :], edge_i[:, :, :, :]).then_inc(edges_float, 1)
            dve.wait_ge(edges_float, 1)
            link(nc.vector.tensor_reduce(span[:, 0, :], edge_f[:, 1, :, :], op=ALU.min, axis=AX_X))
            link(nc.vector.tensor_reduce(span[:, 1, :], edge_f[:, 1, :, :], op=ALU.max, axis=AX_X))
            dve.wait_ge(consts_ready, 7)
            for n in range(2):
                for c in range(CROWS):
                    last = nc.vector.tensor_scalar(span_diag[:, n, c, :], k.ident[:, :], span[:, n, c:c + 1], None,
                                                   ALU.mult)
            last.then_inc(diag_ready, 1)
            dve.wait_ge(edges_turned, 1)
            nc.vector.tensor_copy(k.src_col[:, :], ps[:, 6, 0:CCOLS])
            nc.vector.tensor_copy(k.dst_col[:, :], ps[:, 7, 0:CCOLS])
            dve.wait_ge(span_spread, 1)
            link(nc.vector.tensor_scalar(meets[:, 0, :], ps[0:NT, 3, 0:CCOLS], tile_lo[:, 1:2], None, ALU.is_lt))
            link(nc.vector.scalar_tensor_tensor(out=meets[:, 0, :], in0=ps[0:NT, 4, 0:CCOLS], scalar=tile_lo[:, 0:1],
                                                in1=meets[:, 0, :], op0=ALU.is_ge, op1=ALU.mult))
            link(nc.vector.tensor_tensor(meets[:, 1, :], meets[:, 0, :], chunk_no[:, 1, :], ALU.mult))
            link(nc.vector.tensor_tensor(meets[:, 0, :], meets[:, 0, :], chunk_no[:, 0, :], ALU.mult))
            link(nc.vector.tensor_reduce(ranges[:, 0:1], meets[:, 1, :], op=ALU.max, axis=AX_X))
            link(nc.vector.tensor_reduce(ranges[:, 1:2], meets[:, 0, :], op=ALU.max, axis=AX_X))
            link(nc.vector.tensor_scalar(ranges[:, 0:1], ranges[:, 0:1], -1.0, CCOLS - 1.0, ALU.mult, ALU.add))
            link(nc.vector.tensor_scalar(ranges[:, 0:1], ranges[:, 0:1], float(CHUNKS - 1), None, ALU.min))
            link(nc.vector.tensor_tensor(ranges[:, 1:2], ranges[:, 1:2], ranges[:, 0:1], ALU.max))
            link(nc.vector.tensor_scalar(ranges[:, 1:2], ranges[:, 1:2], 1.0, None, ALU.add))
            nc.vector.tensor_copy(ranges_i[:, :], ranges[:, :]).then_inc(ranges_ready, 1)
            dve.wait_ge(wah_hi_ready, 1)
            nc.vector.tensor_tensor(w_lo[:, :, :], w_raw[:, :, :], w_hi[:, :, :].bitcast(F32),
                                    ALU.subtract).then_inc(wah_lo_ready, 1)
            with dve.Fori(0, PAIRS) as i:
                dve.wait_ge(xT_hi_ready, i + 1)
                nc.vector.tensor_tensor(xT_lo[:, :, :].rearrange("p (b k) n -> p b (k n)", k=2), turned,
                                        xT_hi[:, :, :].bitcast(F32).rearrange("p (b k) n -> p b (k n)", k=2),
                                        ALU.subtract).then_inc(xT_lo_ready, 1)
                dve.wait_ge(x1_hi_ready, i + 1)
                nc.vector.tensor_tensor(k.x1_lo[:, :, bass.ds(2 * T * i, 2 * T)], x1[:, :, :],
                                        k.x1_hi[:, :, bass.ds(2 * T * i, 2 * T)].bitcast(F32),
                                        ALU.subtract).then_inc(x1_lo_ready, 1)

        @block.tensor
        def _(pe):
            pe.wait_ge(consts_ready, 7)
            pe.wait_ge(edges_float, 1)
            for n in range(2):
                for c in range(CROWS):
                    last = nc.tensor.transpose(ps[:, 6 + n, c * 128:(c + 1) * 128], edge_f[:, n, c, :], k.ident[:, :])
            last.then_inc(edges_turned, 1)
            pe.wait_ge(diag_ready, 1)
            for n in range(2):
                for c in range(CROWS):
                    last = nc.tensor.matmul(ps[0:NT, 3 + n, c * 128:(c + 1) * 128], ones[:, :], span_diag[:, n, c, :],
                                            start=True, stop=True)
            last.then_inc(span_spread, 1)
            pe.wait_ge(ranges_ready, 1)
            pe.wait_ge(wah_lo_ready, 1)
            with pe.Fori(0, PAIRS) as i:
                pe.wait_ge(x_loaded, (i + 1) * 16)
                for f in range(KF):
                    for j in range(2):
                        last = nc.tensor.transpose(ps[:, 3 + f // 2, (f % 2) * 2 * T + j * T:(f % 2) * 2 * T + (j + 1) * T],
                                                   x_in[:, j, f * 128:(f + 1) * 128], k.ident[0:T, 0:T])
                last.then_inc(x_turned, 1)
                pe.wait_ge(xT_lo_ready, i + 1)
                for m in range(KF):
                    for f in range(KF):
                        cols = slice(m * 128, (m + 1) * 128)
                        last = three_passes(nc, summed[:, m, 0:2 * T], (w_hi[:, f, cols], w_lo[:, f, cols]),
                                            (xT_hi[:, f, :], xT_lo[:, f, :]), f == 0, f == KF - 1)
                    last.then_inc(x1_summed, 1)

        @block.scalar
        def _(act):
            act.dma_start(w_raw[:, :, :], a["W_ah"].rearrange("(k p) n -> p k n", p=128)).then_inc(weights_loaded, 16)
            act.dma_start(bias[:, :], a["b_ah_cols"]).then_inc(bias_loaded, 16)
            act.wait_ge(weights_loaded, 16)
            nc.scalar.activation(w_hi[:, :, :], w_raw[:, :, :], ACT.Copy).then_inc(wah_hi_ready, 1)
            act.wait_ge(bias_loaded, 16)
            with act.Fori(0, PAIRS) as i:
                act.wait_ge(x_turned, i + 1)
                nc.scalar.activation(xT_hi[:, :, :].rearrange("p (b k) n -> p b (k n)", k=2), turned,
                                     ACT.Copy).then_inc(xT_hi_ready, 1)
                for m in range(KF):
                    act.wait_ge(x1_summed, i * KF + 2 * (m // 2) + 2)
                    nc.scalar.activation(x1[:, m, :], summed[:, m, 0:2 * T], ACT.Relu,
                                         bias=bias[:, m:m + 1]).then_inc(x1_copied, 1)


def counts(nc, k, a):
    with ExitStack() as mem:
        def sb(name, shape, dt=F32):
            return mem.enter_context(nc.sbuf_tensor(name, shape, dt))

        src_hot = sb("src_hot", [128, CSTEP, 3 * SW], BF16)
        dst_hot = sb("dst_hot", [128, CSTEP, T], BF16)
        count_tile = sb("count_tile", [T, 3, SW])
        count_T = sb("count_T", [T, NT, N])
        wt = sb("w_turned", [128, KF, WP * 128])
        att = sb("att_cols", [128, LAYERS, KF, 2 * HEADS])
        ps = k.ps
        summed = ps[0:T, 0:3, 0:SW]

        hots_ready = k.sem("hots_ready")
        hots_used = k.sem("hots_used")
        counts_summed = k.sem("counts_summed")
        counts_copied = k.sem("counts_copied")
        no_edge_ready = k.sem("no_edge_ready")
        counts_turned = k.sem("counts_turned")
        turned_copied = k.sem("turned_copied")
        dst_shifted = k.sem("dst_shifted")
        counts_stored = k.sem("counts_stored")
        deg_root = k.sem("deg_root")
        dinv_ready = k.sem("dinv_ready")
        root = sb("root", [T, NT])
        att_loaded = k.sem("att_loaded")
        wt_loaded = k.sem("wt_loaded")
        terms_summed = k.sem("terms_summed")
        terms_copied = k.sem("terms_copied")
        most = NT * (CHUNKS + CSTEP)
        pieces = LAYERS * KF // WP

        def piece(t):
            return (t * pieces) // NT

        block = mem.enter_context(nc.Block())

        def chunk_range(eng, t):
            first = eng.value_load(k.ranges_row[0:1, bass.ds(t, 1)], min_val=0, max_val=CHUNKS)
            end = eng.value_load(k.ranges_row[0:1, bass.ds(t + NT, 1)], min_val=1, max_val=CHUNKS + 1)
            return first, end

        @block.sync
        def _(sp):
            sp.dma_start(att[:, :, :, :], a["att"]).then_inc(att_loaded, 16)
            sp.sem_inc(terms_copied, 1)
            with sp.Fori(0, NT) as t:
                sp.wait_ge(terms_copied, t + 1)
                sp.dma_start(wt[:, :, :], a["W_gat_turned"][bass.ds(piece(t), 1), :, :, :].rearrange(
                    "o p c f -> p (o c) f")).then_inc(wt_loaded, 16)
            sp.wait_ge(turned_copied, NT + 1)
            sp.dma_start(k.count_d, count_T[:, :, :]).then_inc(counts_stored, 16)
            sp.wait_ge(counts_stored, 16)

        @block.vector
        def _(dve):
            made = nc.vector.alloc_register("made")
            nc.vector.reg_mov(made, 1)
            dve.sem_inc(hots_used, CSTEP)
            with dve.Fori(0, NT) as t:
                first, end = chunk_range(nc.vector, t)
                with dve.Fori(first, end, CSTEP) as c:
                    n = nc.vector.snap(made, min_val=1, max_val=most)
                    for j in range(CSTEP):
                        dve.wait_ge(hots_used, n + j)
                        nc.vector.tensor_scalar(src_hot[:, j, :], k.iota_h[:, :], k.src_col[:, bass.ds(c + j, 1)], None,
                                                ALU.is_equal)
                        nc.vector.tensor_scalar(dst_hot[:, j, :], k.iota_h[:, 0:T], k.dst_col[:, bass.ds(c + j, 1)],
                                                None, ALU.is_equal).then_inc(hots_ready, 1)
                    nc.vector.reg_add(made, made, CSTEP)
                dve.wait_ge(hots_ready, nc.vector.snap(made, min_val=2, max_val=most) - 1)
                nc.vector.tensor_scalar(k.dst_col[:, :], k.dst_col[:, :], float(T), None,
                                        ALU.subtract).then_inc(dst_shifted, 1)
                dve.wait_ge(dst_shifted, t + 1)
            dve.wait_ge(deg_root, 1)
            nc.vector.reciprocal(k.dinv[:, :], root[:, :]).then_inc(dinv_ready, 1)

        @block.tensor
        def _(pe):
            pe.wait_ge(att_loaded, 16)
            taken = nc.tensor.alloc_register("taken")
            nc.tensor.reg_mov(taken, 1)
            with pe.Fori(0, NT) as t:
                first, end = chunk_range(nc.tensor, t)
                for s in range(3):
                    nc.tensor.matmul(summed[:, s, :], k.loop_strip[:, N:N + T],
                                     k.loop_strip[:, bass.ds(N - T * t + SW * s, SW)], start=True, stop=False)
                with pe.Fori(first, end, CSTEP) as c:
                    n = nc.tensor.snap(taken, min_val=1, max_val=most)
                    for j in range(CSTEP):
                        pe.wait_ge(hots_ready, n + j)
                        for s in range(3):
                            last = nc.tensor.matmul(summed[:, s, :], dst_hot[:, j, :], src_hot[:, j, s * SW:(s + 1) * SW],
                                                    start=False, stop=False)
                        last.then_inc(hots_used, 1)
                    nc.tensor.reg_add(taken, taken, CSTEP)
                for s in range(3):
                    last = nc.tensor.matmul(summed[:, s, :], k.zeros[0:T, 0:T], k.zeros[0:T, :], start=False, stop=True)
                last.then_inc(counts_summed, 1)
                pe.wait_ge(wt_loaded, 16 * t + 16)
                for f in range(WP):
                    for c in range(KF):
                        last = nc.tensor.matmul(ps[:, 7, f * 2 * HEADS:(f + 1) * 2 * HEADS],
                                                wt[:, c, f * 128:(f + 1) * 128],
                                                att[:, bass.ds(piece(t) // (KF // WP), 1), c, :].rearrange(
                                                    "p o h -> p (o h)"), start=c == 0, stop=c == KF - 1)
                last.then_inc(terms_summed, 1)
                pe.wait_ge(counts_copied, t + 1)
                pe.wait_ge(turned_copied, t + 1)
                flat = count_tile[:, :, :].rearrange("p a b -> p (a b)")
                for s in range(NT):
                    last = nc.tensor.transpose(ps[0:T, 3 + s // 4, (s % 4) * T:(s % 4 + 1) * T],
                                               flat[:, s * T:(s + 1) * T], k.ident[0:T, 0:T])
                last.then_inc(counts_turned, 1)

        @block.scalar
        def _(act):
            act.sem_inc(turned_copied, 1)
            act.sem_inc(no_edge_ready, 1)
            with act.Fori(0, NT) as t:
                act.wait_ge(counts_summed, t + 1)
                hold(act, k.held, no_edge_ready, t + 1)
                nc.scalar.activation(count_tile[:, :, :], summed, ACT.Copy,
                                     accum_out=k.deg[:, bass.ds(t, 1)]).then_inc(counts_copied, 1)
                hold(act, k.held, counts_copied, t + 1)
                nc.scalar.activation(k.no_edge[:, bass.ds(t, 1), :].rearrange("p a (b c) -> p (a b) c", c=SW),
                                     count_tile[:, :, :], ACT.Relu, bias=k.far[0:T, :],
                                     scale=-FAR).then_inc(no_edge_ready, 1)
                act.wait_ge(terms_summed, t + 1)
                hold(act, k.held, terms_copied, t + 1)
                nc.scalar.activation(k.w_att[:, bass.ds(piece(t) * WP * 2 * HEADS, WP * 2 * HEADS)],
                                     ps[:, 7, 0:WP * 2 * HEADS], ACT.Copy).then_inc(terms_copied, 1)
                hold(act, k.held, counts_turned, t + 1)
                for g, w in ((0, 4), (1, 4), (2, 2)):
                    last = nc.scalar.activation(
                        count_T[:, 4 * g:4 * g + w, bass.ds(T * t, T)],
                        ps[0:T, 3 + g, 0:w * T].rearrange("p (a b) -> p a b", b=T), ACT.Copy)
                last.then_inc(turned_copied, 1)
            act.wait_ge(turned_copied, NT + 1)
            nc.scalar.activation(root[:, :], k.deg[:, :], ACT.Sqrt).then_inc(deg_root, 1)


def heads_in(nc, k, a):
    with ExitStack() as mem:
        def sb(name, shape, dt=F32):
            return mem.enter_context(nc.sbuf_tensor(name, shape, dt))

        w_raw = sb("w_raw", [128, KF, DA])
        w_hi = sb("w_hi", [128, KF, DA], F32R)
        w_lo = sb("w_lo", [128, KF, DA], F32R)
        h_out = [sb(f"h_out{b}", [T, 2, DA // 2]) for b in range(2)]
        terms = sb("terms", [T, NT, 2 * HEADS])
        dst_term = sb("dst_term", [T, NT, HEADS])
        src_row = sb("src_row", [HEADS, N])
        src_spread = sb("src_spread", [T, HEADS, N])
        scores = [sb(f"scores{b}", [T, N], BF16) for b in range(2)]
        top = sb("top", [T, NT, HEADS])
        low = sb("low", [T, NT, HEADS])
        lifts = sb("lifts", [T, NT, 2 * HALL])
        lift_rows = sb("lift_rows", [2 * HALL, N])
        deg_row = sb("deg_row", [NT, T])
        ps = k.ps

        raw_loaded = k.sem("raw_loaded")
        raw_ready = k.sem("raw_ready")
        w_hi_ready = k.sem("w_hi_ready")
        w_lo_ready = k.sem("w_lo_ready")
        h_summed = k.sem("h_summed")
        h_copied = k.sem("h_copied")
        h_stored = [k.sem(f"h_stored{b}") for b in range(2)]
        rows_turned = k.sem("rows_turned")
        rows_copied = k.sem("rows_copied")
        rows_stored = k.sem("rows_stored")
        spread_loaded = k.sem("spread_loaded")
        terms_taken = k.sem("terms_taken")
        maxima_step = k.sem("maxima_step")
        lift_step = k.sem("lift_step")
        lifts_turned = k.sem("lifts_turned")
        lifts_copied = k.sem("lifts_copied")
        lifts_stored = k.sem("lifts_stored")

        block = mem.enter_context(nc.Block())
        w_all = a["W_gat"].rearrange("l (k p) n -> p l k n", p=128)
        spread_steps = NT * HEADS

        @block.gpsimd
        def _(pool):
            pool.sem_inc(w_lo_ready, 2)
            with pool.Fori(0, LAYERS) as l:
                hold(pool, k.held, w_lo_ready, 2 * l + 2)
                pool.dma_start(w_raw[:, :, 0:D], w_all[:, bass.ds(l, 1), :, :].rearrange("p l k n -> p (l k) n")
                               ).then_inc(raw_loaded, 16)
                pool.wait_ge(raw_loaded, (l + 1) * 16)
                nc.gpsimd.tensor_copy(w_raw[:, :, D:DA], k.w_att[:, bass.ds(l * KF * 2 * HEADS, KF * 2 * HEADS)].rearrange(
                    "p (k h) -> p k h", h=2 * HEADS)).then_inc(raw_ready, 1)
                for part in range(2):
                    ks = slice(3 * part, 3 * part + 3)
                    pool.wait_ge(w_hi_ready, 2 * l + part + 1)
                    nc.gpsimd.tensor_tensor(w_lo[:, ks, :], w_raw[:, ks, :], w_hi[:, ks, :].bitcast(F32),
                                            ALU.subtract).then_inc(w_lo_ready, 1)

        @block.scalar
        def _(act):
            act.sem_inc(h_copied, 2)
            with act.Fori(0, LAYERS) as l:
                act.wait_ge(raw_ready, l + 1)
                for part in range(2):
                    ks = slice(3 * part, 3 * part + 3)
                    nc.scalar.activation(w_hi[:, ks, :], w_raw[:, ks, :], ACT.Copy).then_inc(w_hi_ready, 1)
                for t in range(NT):
                    act.wait_ge(h_summed, l * NT + t + 1)
                    act.wait_ge(h_stored[t % 2], (l * (NT // 2) + t // 2 + 1) * 16)
                    nc.scalar.activation(h_out[t % 2][:, :, :], ps[0:T, 2 * (t % 2):2 * (t % 2) + 2, 0:DA // 2], ACT.Copy)
                    if t == 0:
                        act.wait_ge(terms_taken, l + 1)
                    nc.scalar.activation(terms[:, t, :], ps[0:T, 2 * (t % 2) + 1, DA // 2 - 2 * HEADS:DA // 2],
                                         ACT.Copy).then_inc(h_copied, 1)
                act.wait_ge(rows_turned, l + 1)
                act.wait_ge(rows_stored, l * 16 + 16)
                for g, w in ((0, 4), (1, 4), (2, 2)):
                    last = nc.scalar.activation(src_row[:, 4 * g * T:(4 * g + w) * T], ps[0:HEADS, 4 + g, 0:w * T],
                                                ACT.Copy)
                last.then_inc(rows_copied, 1)
            act.wait_ge(lifts_turned, 1)
            for g, w in ((0, 4), (1, 4), (2, 2)):
                nc.scalar.activation(lift_rows[:, 4 * g * T:(4 * g + w) * T], ps[0:2 * HALL, 4 + g, 0:w * T],
                                     ACT.Copy).then_inc(lifts_copied, 1)
            nc.scalar.activation(deg_row[:, :], ps[0:NT, 7, 0:T], ACT.Copy).then_inc(lifts_copied, 1)

        @block.sync
        def _(sp):
            sp.sem_inc(h_stored[0], 16)
            sp.sem_inc(h_stored[1], 16)
            sp.sem_inc(rows_stored, 16)
            with sp.Fori(0, LAYERS) as l:
                for t in range(NT):
                    sp.wait_ge(h_copied, l * NT + t + 3)
                    sp.dma_start(k.h_d[:, bass.ds(l * HEADS, HEADS), t, :],
                                 h_out[t % 2][:, :, :].rearrange("p a b -> p (a b)")[:, 0:D].rearrange(
                                     "p (h c) -> p h c", c=C)).then_inc(h_stored[t % 2], 16)
                sp.wait_ge(rows_copied, l + 1)
                sp.dma_start(k.src_row_d[bass.ds(l, 1), :, :].rearrange("l h n -> (l h) n"),
                             src_row[:, :]).then_inc(rows_stored, 16)
                sp.wait_ge(rows_stored, l * 16 + 32)
                sp.wait_ge(maxima_step, l * spread_steps + 1)
                sp.dma_start(src_spread[:, :, :],
                             k.src_row_d[bass.ds(l, 1), :, :].to_broadcast([T, HEADS, N])).then_inc(spread_loaded, 16)
            sp.wait_ge(lifts_copied, 4)
            sp.dma_start(k.lift_d, lift_rows[:, :]).then_inc(lifts_stored, 16)
            sp.dma_start(k.dinv_d.rearrange("(t p) -> t p", p=T), deg_row[:, :]).then_inc(lifts_stored, 16)
            sp.wait_ge(lifts_stored, 32)
            sp.wait_ge(h_stored[0], (LAYERS * (NT // 2) + 1) * 16)
            sp.wait_ge(h_stored[1], (LAYERS * (NT // 2) + 1) * 16)

        @block.vector
        def _(dve):
            dve.sem_inc(terms_taken, 1)
            dve.sem_inc(maxima_step, 1)
            with dve.Fori(0, LAYERS) as l:
                heads = bass.ds(l * HEADS, HEADS)
                dve.wait_ge(h_copied, l * NT + NT + 2)
                src_terms = terms[:, :, 0:HEADS].rearrange("p t h -> p h t")
                nc.vector.tensor_copy(k.src_term[:, heads, :], src_terms)
                nc.vector.tensor_scalar(k.src_drop[:, heads, :], src_terms, SLOPE - 1.0, None, ALU.mult)
                nc.vector.tensor_copy(dst_term[:, :, :], terms[:, :, HEADS:2 * HEADS]).then_inc(terms_taken, 1)
                dve.wait_ge(spread_loaded, (l + 1) * 16)
                for t in range(NT):
                    for h in range(HEADS):
                        n = t * HEADS + h
                        hold(dve, k.held, maxima_step, l * spread_steps + n + 1 - (1 if n else 0))
                        nc.vector.tensor_tensor_reduce(
                            out=scores[n % 2][:, :], in0=src_spread[:, h, :], in1=k.no_edge[:, t, 0:N], scale=1.0,
                            scalar=NO_MAX, op0=ALU.subtract, op1=ALU.max,
                            accum_out=top[:, t, h:h + 1]).then_inc(maxima_step, 1)
                dve.wait_ge(maxima_step, (l + 1) * spread_steps + 1)
                dve.wait_ge(terms_taken, l + 2)
                chain = [0]

                def link(ins):
                    chain[0] += 1
                    ins.then_inc(lift_step, 1)
                    dve.wait_ge(lift_step, l * 5 + chain[0])

                link(nc.vector.tensor_tensor(top[:, :, :], top[:, :, :], dst_term[:, :, :], ALU.add))
                link(nc.vector.tensor_scalar(low[:, :, :], top[:, :, :], SLOPE, None, ALU.mult))
                link(nc.vector.tensor_tensor(top[:, :, :], top[:, :, :], low[:, :, :], ALU.max))
                pairs = lifts[:, :, bass.ds(l * 2 * HEADS, 2 * HEADS)].rearrange("p t (h u) -> p t h u", u=2)
                link(nc.vector.tensor_tensor(pairs[:, :, :, 0], dst_term[:, :, :], top[:, :, :], ALU.subtract))
                link(nc.vector.scalar_tensor_tensor(out=pairs[:, :, :, 1], in0=dst_term[:, :, :], scalar=SLOPE,
                                                    in1=top[:, :, :], op0=ALU.mult, op1=ALU.subtract))

        @block.tensor
        def _(pe):
            with pe.Fori(0, LAYERS) as l:
                for t in range(NT):
                    pe.wait_ge(h_copied, l * NT + t + 1)
                    for s in range(2):
                        for f in range(KF):
                            if t == 0 and s == 0 and f % 3 == 0:
                                pe.wait_ge(w_lo_ready, 2 * l + f // 3 + 3)
                            nodes = slice(t * T, (t + 1) * T)
                            cols = slice(s * DA // 2, (s + 1) * DA // 2)
                            last = three_passes(nc, ps[0:T, 2 * (t % 2) + s, 0:DA // 2],
                                                (k.x1_hi[:, f, nodes], k.x1_lo[:, f, nodes]),
                                                (w_hi[:, f, cols], w_lo[:, f, cols]), f == 0, f == KF - 1)
                    last.then_inc(h_summed, 1)
                pe.wait_ge(h_copied, l * NT + NT + 2)
                for t in range(NT):
                    last = nc.tensor.transpose(ps[0:HEADS, 4 + t // 4, (t % 4) * T:(t % 4 + 1) * T],
                                               terms[:, t, 0:HEADS], k.ident[0:T, 0:T])
                last.then_inc(rows_turned, 1)
            pe.wait_ge(rows_copied, LAYERS)
            pe.wait_ge(lift_step, 5 * LAYERS)
            for t in range(NT):
                nc.tensor.transpose(ps[0:2 * HALL, 4 + t // 4, (t % 4) * T:(t % 4 + 1) * T], lifts[:, t, :],
                                    k.ident[0:T, 0:T])
            nc.tensor.transpose(ps[0:NT, 7, 0:T], k.dinv[:, :], k.ident[0:T, 0:T]).then_inc(lifts_turned, 1)


def attend(nc, k, a):
    with ExitStack() as mem:
        def sb(name, shape, dt=F32):
            return mem.enter_context(nc.sbuf_tensor(name, shape, dt))

        count_T = sb("count_T_att", [T, NT, N])
        lift = [sb(f"lift{q}", [T, 2, N]) for q in range(2)]
        h_in = [sb(f"h_in{q}", [T, NT, C + 1]) for q in range(2)]
        score = [sb(f"score{r}", [T, HALF]) for r in range(RING)]
        weight = [sb(f"weight{r}", [T, HALF]) for r in range(RING)]
        sums = [sb(f"sums{g}", [T, GT, C + 1]) for g in range(2)]
        inverse = [sb(f"inverse{g}", [T, GT, 1]) for g in range(2)]
        normed = [sb(f"normed{g}", [T, GT, C]) for g in range(2)]
        bias = sb("gat_bias", [T, HALL + 1, C])
        ps = k.ps
        banks = [ps[0:T, 3 * g:3 * g + 3, :].rearrange("p b (m n) -> p (b m) n", m=2) for g in range(2)]

        counts_loaded = [k.sem(f"counts_loaded{n}") for n in range(NT // 2)]
        bias_loaded = k.sem("gat_bias_loaded")
        head_loaded = [k.sem(f"head_loaded{q}") for q in range(2)]
        ones_set = k.sem("ones_set")
        score_ready = k.sem("score_ready")
        exp_ready = k.sem("exp_ready")
        weight_ready = k.sem("weight_ready")
        weight_used = k.sem("weight_used")
        sums_copied = k.sem("sums_copied")
        norm_step = k.sem("norm_step")
        biased = k.sem("biased")
        cat_stored = [k.sem(f"cat_stored{g}") for g in range(2)]

        PAIR = 4 * NT
        GROUPS = 4
        block = mem.enter_context(nc.Block())

        def group_of(i):
            return i // NT % 2, i % NT, i // (2 * NT)

        @block.sync
        def _(sp):
            def load_head(head, q):
                sp.dma_start(lift[q][:, :, :], k.lift_d[bass.ds(2 * head, 2), :].rearrange(
                    "(o u) n -> o u n", o=1).to_broadcast([T, 2, N])).then_inc(head_loaded[q], 16)
                sp.dma_start(h_in[q][:, :, 0:C], k.h_d[:, bass.ds(head, 1), :, :].rearrange(
                    "p o t c -> p (o t) c")).then_inc(head_loaded[q], 16)

            load_head(0, 0)
            for n in range(NT // 2):
                sp.dma_start(count_T[:, 2 * n:2 * n + 2, :], k.count_d[:, 2 * n:2 * n + 2, :]
                             ).then_inc(counts_loaded[n], 16)
                if n == 0:
                    load_head(1, 1)
            sp.dma_start(bias[:, 1:, :], a["b_gat"].rearrange("(o h c) -> o h c", o=1, c=C).to_broadcast([T, HALL, C])
                         ).then_inc(bias_loaded, 16)
            sp.sem_inc(cat_stored[0], 16)
            sp.sem_inc(cat_stored[1], 16)

            def store(n, g, slot):
                sp.wait_ge(biased, n + 1)
                sp.dma_start(k.cat_d[:, g * GT:(g + 1) * GT, bass.ds(slot, 1), :].rearrange("p t o c -> p t (o c)"),
                             normed[g][:, :, :]).then_inc(cat_stored[g], 16)

            with sp.Fori(0, HALL // 2) as p:
                for gg in range(GROUPS):
                    store(p * GROUPS + gg, (gg + 1) % 2, 2 * p + (gg + 1) // 2)
                    if gg >= 2:
                        q = gg - 2
                        sp.wait_ge(weight_used, p * PAIR + 2 * NT * (q + 1) + RING)
                        load_head(2 * ((p + 1) % (HALL // 2)) + q, q)
            store(2 * HALL, 1, HALL)
            for g in range(2):
                sp.wait_ge(cat_stored[g], (HALL + 1 + g) * 16)
                sp.wait_ge(head_loaded[g], (HALL // 2 + 1) * 32)

        @block.vector
        def _(dve):
            dve.sem_inc(weight_ready, RING)
            dve.sem_inc(weight_used, RING - 1)
            dve.sem_inc(norm_step, 6)

            def make_score(p, i):
                g, s, q = group_of(i)
                cols = slice(g * HALF, (g + 1) * HALF)
                if i % (2 * NT) == 0:
                    dve.wait_ge(head_loaded[q], (p + 1) * 32)
                dve.wait_ge(weight_ready, p * PAIR + i + 1)
                nc.vector.scalar_tensor_tensor(out=score[i % RING][:, :], in0=lift[q][:, 1, cols],
                                               scalar=k.src_drop[:, bass.ds(2 * p + q, 1), s], in1=lift[q][:, 0, cols],
                                               op0=ALU.add, op1=ALU.max).then_inc(score_ready, 1)

            def normalise(n, g, before):
                dve.wait_ge(sums_copied, n + 2)
                base = 6 + 3 * n
                nc.vector.tensor_scalar(inverse[g][:, :, :], sums[g][:, :, C:C + 1], 1e-16, None,
                                        ALU.add).then_inc(norm_step, 1)
                dve.wait_ge(norm_step, base + 1)
                nc.vector.reciprocal(inverse[g][:, :, :], inverse[g][:, :, :]).then_inc(norm_step, 1)
                dve.wait_ge(norm_step, base + 2)
                dve.wait_ge(cat_stored[g], before * 16 + 16)
                nc.vector.tensor_tensor(normed[g][:, :, :], sums[g][:, :, 0:C],
                                        inverse[g][:, :, :].to_broadcast([T, GT, C]), ALU.mult).then_inc(norm_step, 1)

            with dve.Fori(0, HALL // 2) as p:
                make_score(p, 0)
                for i in range(PAIR):
                    g, s, q = group_of(i)
                    if i < PAIR - 1:
                        make_score(p, i + 1)
                    dve.wait_ge(exp_ready, p * PAIR + i + 1)
                    dve.wait_ge(weight_used, p * PAIR + i + 1)
                    if i < NT:
                        dve.wait_ge(counts_loaded[s // 2], 16)
                    nc.vector.scalar_tensor_tensor(out=weight[i % RING][:, :], in0=score[i % RING][:, :], scalar=EXP_CAP,
                                                   in1=count_T[:, s, g * HALF:(g + 1) * HALF], op0=ALU.min,
                                                   op1=ALU.mult).then_inc(weight_ready, 1)
                    if s == 6:
                        gg = i // NT
                        normalise(p * GROUPS + gg, (gg + 1) % 2, 2 * p + gg // 2)
            normalise(2 * HALL, 1, HALL)

        @block.scalar
        def _(act):
            act.sem_inc(sums_copied, 1)

            def copy_sums(n, g):
                act.wait_ge(weight_used, n * NT + RING)
                act.wait_ge(norm_step, 3 * n + 3)
                nc.scalar.activation(sums[g][:, :, :], banks[g][:, 0:GT, 0:C + 1], ACT.Copy).then_inc(sums_copied, 1)

            with act.Fori(0, HALL // 2) as p:
                for i in range(PAIR):
                    g, s, q = group_of(i)
                    hold(act, k.held, score_ready, p * PAIR + i + 1)
                    nc.scalar.activation(score[i % RING][:, :], score[i % RING][:, :], ACT.Exp,
                                         bias=k.src_term[:, bass.ds(2 * p + q, 1), s]).then_inc(exp_ready, 1)
                    if s == 3:
                        gg = i // NT
                        copy_sums(p * GROUPS + gg, (gg + 1) % 2)
            copy_sums(2 * HALL, 1)

        @block.tensor
        def _(pe):
            for b in range(3):
                for half in range(2):
                    last = nc.tensor.matmul(ps[0:T, 3 + b, half * 256:(half + 1) * 256], k.zeros[0:T, 0:T],
                                            k.zeros[0:T, 0:256], start=True, stop=True)
            last.then_inc(weight_used, 1)
            pe.wait_ge(ones_set, 4)
            with pe.Fori(0, HALL // 2) as p:
                for i in range(PAIR):
                    g, s, q = group_of(i)
                    if s == 0:
                        pe.wait_ge(sums_copied, p * GROUPS + i // NT + 1)
                    pe.wait_ge(weight_ready, p * PAIR + i + 1 + RING)
                    for t in range(GT):
                        last = nc.tensor.matmul(banks[g][:, t, 0:C + 1], weight[i % RING][:, t * T:(t + 1) * T],
                                                h_in[q][:, s, :], start=(s == 0 and t % 2 == 0), stop=(s == NT - 1),
                                                skip_group_check=True)
                    last.then_inc(weight_used, 1)

        @block.gpsimd
        def _(pool):
            for q in range(2):
                nc.gpsimd.memset(h_in[q][:, :, C:C + 1], 1.0).then_inc(ones_set, 1)
            nc.gpsimd.memset(bias[:, 0:1, :], 0.0).then_inc(ones_set, 1)
            pool.wait_ge(bias_loaded, 16)
            pool.sem_inc(ones_set, 1)

            def add_bias(n, g, slot):
                hold(pool, k.held, norm_step, 3 * n + 9)
                nc.gpsimd.tensor_tensor(normed[g][:, :, :], normed[g][:, :, :],
                                        bias[:, bass.ds(slot, 1), :].to_broadcast([T, GT, C]), ALU.add
                                        ).then_inc(biased, 1)

            with pool.Fori(0, HALL // 2) as p:
                for gg in range(GROUPS):
                    add_bias(p * GROUPS + gg, (gg + 1) % 2, 2 * p + (gg + 1) // 2)
            add_bias(2 * HALL, 1, HALL)


def split_weights(nc, mem, k, name, kt):
    hi = mem.enter_context(nc.sbuf_tensor(f"{name}_hi", [128, kt, D], F32R))
    lo = mem.enter_context(nc.sbuf_tensor(f"{name}_lo", [128, kt, D], F32R))
    return hi, lo


STAGE = 3


def combine(nc, k, a):
    with ExitStack() as mem:
        def sb(name, shape, dt=F32):
            return mem.enter_context(nc.sbuf_tensor(name, shape, dt))

        SG = 1
        wo = split_weights(nc, mem, k, "wo", KO)
        w1 = split_weights(nc, mem, k, "w1", KF)
        stage = [sb(f"stage{b}", [128, SG, D]) for b in range(2)]
        cat = sb("cat", [T, HALL * C])
        catT_hi = sb("catT_hi", [128, KO, T], F32R)
        catT_lo = sb("catT_lo", [128, KO, T], F32R)
        x_in = sb("x_res", [T, D])
        y = sb("y_pre", [T, D])
        x2 = sb("x2", [T, D])
        stats = sb("stats", [T, 2, 6])
        mean_var = sb("mean_var", [T, 2])
        rstd = sb("rstd", [T, 1])
        x2T_hi = sb("x2T_hi", [128, KF, 128], F32R)
        x2T_lo = sb("x2T_lo", [128, KF, 128], F32R)
        hs_hi = sb("hs_hi_out", [T, D], F32R)
        hs_lo = sb("hs_lo_out", [T, D], F32R)
        b_row = sb("b_out_row", [T, D])
        ps = k.ps

        staged = [k.sem(f"wo_staged{b}") for b in range(2)]
        split_hi = k.sem("wo_split_hi")
        split_lo = k.sem("wo_split_lo")
        row_loaded = k.sem("b_out_loaded")
        cat_loaded = k.sem("cat_loaded")
        x_loaded = k.sem("x_res_loaded")
        cat_turned = k.sem("cat_turned")
        catT_hi_ready = k.sem("catT_hi_ready")
        catT_lo_ready = k.sem("catT_lo_ready")
        out_summed = k.sem("out_summed")
        ln_step = k.sem("ln_step")
        rstd_step = k.sem("rstd_step")
        x2_ready = k.sem("x2_ready")
        x2_turned = k.sem("x2_turned")
        x2T_hi_ready = k.sem("x2T_hi_ready")
        x2T_lo_ready = k.sem("x2T_lo_ready")
        h1_summed = k.sem("h1_summed")
        hs_hi_ready = k.sem("hs_hi_ready")
        hs_lo_ready = k.sem("hs_lo_ready")
        stored = k.sem("combine_stored")
        pieces = [(wo, a["W_out"], f) for f in range(0, KO, SG)] + [(w1, a["W1"], f) for f in range(0, KF, SG)]
        groups = [(f, min(4, KO - f)) for f in range(0, KO, 4)]
        NG = len(groups)
        LN = 5
        block = mem.enter_context(nc.Block())

        def turned(f, w, bank):
            return ps[:, bank, 0:w * T].rearrange("p (k n) -> p k n", n=T)

        @block.sync
        def _(sp):
            for n, (_, w, f) in enumerate(pieces):
                if n >= 2:
                    sp.wait_ge(split_lo, n - 1)
                sp.dma_start(stage[n % 2][:, :, :], w[f * 128:(f + SG) * 128, :].rearrange("(k p) n -> p k n", p=128)
                             ).then_inc(staged[n % 2], 16)
                if n == 1:
                    sp.dma_start(b_row[:, :], a["b_out"].rearrange("(o n) -> o n", o=1).to_broadcast([T, D])
                                 ).then_inc(row_loaded, 16)
            sp.sem_inc(stored, 48)

            def load_cat(t):
                sp.dma_start(cat[:, :], k.cat_d[:, bass.ds(t, 1), 1:, :].rearrange("p o h c -> p (o h c)")
                             ).then_inc(cat_loaded, 16)

            def load_x(t):
                sp.dma_start(x_in[:, :], a["x"][bass.ds(t * T, T), :]).then_inc(x_loaded, 16)

            load_cat(0)
            load_x(0)
            with sp.Fori(0, NT) as t:
                after = (t + 1) % NT
                sp.wait_ge(cat_turned, t * NG + NG)
                load_cat(after)
                sp.wait_ge(ln_step, t * LN + 2)
                load_x(after)
                sp.wait_ge(x2_ready, t + 1)
                sp.dma_start(k.x2_d[:, bass.ds(t, 1), :].rearrange("p o n -> p (o n)"), x2[:, :]).then_inc(stored, 16)
                sp.wait_ge(hs_lo_ready, 2 * t + 4)
                for n, hs in enumerate((hs_hi, hs_lo)):
                    sp.dma_start(k.hs1_d[n, :, bass.ds(t, 1), :].rearrange("p o n -> p (o n)"), hs[:, :].bitcast(F32)
                                 ).then_inc(stored, 16)
            sp.wait_ge(stored, NT * 48 + 48)
            sp.wait_ge(cat_loaded, NT * 16 + 16)
            sp.wait_ge(x_loaded, NT * 16 + 16)

        @block.gpsimd
        def _(pool):
            with pool.Fori(0, NT) as t:
                pool.wait_ge(ln_step, t * LN + LN)
                nc.gpsimd.tensor_tensor(rstd[:, :], mean_var[:, 1:2], k.eps[0:T, :], ALU.add).then_inc(rstd_step, 1)
                pool.wait_ge(rstd_step, 2 * t + 1)
                nc.gpsimd.tensor_tensor(rstd[:, :], rstd[:, :], k.neg_half[0:T, :], ALU.pow).then_inc(rstd_step, 1)

        @block.scalar
        def _(act):
            for n, (w, _, f) in enumerate(pieces):
                act.wait_ge(staged[n % 2], 16 * (n // 2 + 1))
                nc.scalar.activation(w[0][:, f:f + SG, :], stage[n % 2][:, :, :], ACT.Copy).then_inc(split_hi, 1)
            with act.Fori(0, NT) as t:
                for g, (f, w) in enumerate(groups):
                    act.wait_ge(cat_turned, t * NG + g + 1)
                    nc.scalar.activation(catT_hi[:, f:f + w, :], turned(f, w, g % 3), ACT.Relu).then_inc(catT_hi_ready, 1)
                act.wait_ge(x2_turned, t + 1)
                nc.scalar.activation(x2T_hi[:, 0:4, 0:T], turned(0, 4, 5), ACT.Copy)
                nc.scalar.activation(x2T_hi[:, 4:6, 0:T], turned(4, 2, 6), ACT.Copy).then_inc(x2T_hi_ready, 1)
                act.wait_ge(h1_summed, t + 1)
                hold(act, k.held, stored, t * 48 + 48)
                for s, bank in ((0, 7), (1, 4)):
                    nc.scalar.activation(hs_hi[:, s * 384:(s + 1) * 384], ps[0:T, bank, 0:384], ACT.Copy,
                                         scale=k.dinv[:, bass.ds(t, 1)]).then_inc(hs_hi_ready, 1)

        @block.vector
        def _(dve):
            for n, (w, _, f) in enumerate(pieces):
                dve.wait_ge(split_hi, n + 1)
                nc.vector.tensor_tensor(w[1][:, f:f + SG, :], stage[n % 2][:, :, :], w[0][:, f:f + SG, :].bitcast(F32),
                                        ALU.subtract).then_inc(split_lo, 1)
            dve.wait_ge(row_loaded, 16)
            dve.sem_inc(hs_lo_ready, 2)
            with dve.Fori(0, NT) as t:
                for g, (f, w) in enumerate(groups):
                    dve.wait_ge(catT_hi_ready, t * NG + g + 1)
                    nc.vector.scalar_tensor_tensor(out=catT_lo[:, f:f + w, :], in0=turned(f, w, g % 3), scalar=0.0,
                                                   in1=catT_hi[:, f:f + w, :].bitcast(F32), op0=ALU.max,
                                                   op1=ALU.subtract).then_inc(catT_lo_ready, 1)
                dve.wait_ge(out_summed, t + 1)
                step = [0]

                def link(ins):
                    step[0] += 1
                    ins.then_inc(ln_step, 1)
                    hold(dve, k.held, ln_step, t * LN + step[0])

                link(nc.vector.tensor_tensor(y[:, :].rearrange("p (s n) -> p s n", s=2), ps[0:T, 3:5, 0:384],
                                             b_row[:, :].rearrange("p (s n) -> p s n", s=2), ALU.add))
                dve.wait_ge(x_loaded, 16 * t + 16)
                link(nc.vector.scalar_tensor_tensor(out=y[:, :], in0=y[:, :], scalar=0.0, in1=x_in[:, :], op0=ALU.max,
                                                    op1=ALU.add))
                link(nc.vector.bn_stats(stats[:, 0, :], y[:, 0:384]))
                link(nc.vector.bn_stats(stats[:, 1, :], y[:, 384:768]))
                link(nc.vector.bn_aggr(mean_var[:, :], stats[:, :, :]))
                dve.wait_ge(rstd_step, 2 * t + 2)
                dve.wait_ge(stored, t * 48 + 48)
                nc.vector.tensor_scalar(x2[:, :], y[:, :], mean_var[:, 0:1], rstd[:, :], ALU.subtract, ALU.mult
                                        ).then_inc(x2_ready, 1)
                dve.wait_ge(x2T_hi_ready, t + 1)
                nc.vector.tensor_tensor(x2T_lo[:, 0:4, 0:T], turned(0, 4, 5), x2T_hi[:, 0:4, 0:T].bitcast(F32),
                                        ALU.subtract)
                nc.vector.tensor_tensor(x2T_lo[:, 4:6, 0:T], turned(4, 2, 6), x2T_hi[:, 4:6, 0:T].bitcast(F32),
                                        ALU.subtract).then_inc(x2T_lo_ready, 1)
                for s, bank in ((0, 7), (1, 4)):
                    cols = slice(s * 384, (s + 1) * 384)
                    dve.wait_ge(hs_hi_ready, 2 * t + s + 1)
                    nc.vector.scalar_tensor_tensor(out=hs_lo[:, cols], in0=ps[0:T, bank, 0:384],
                                                   scalar=k.dinv[:, bass.ds(t, 1)], in1=hs_hi[:, cols].bitcast(F32),
                                                   op0=ALU.mult, op1=ALU.subtract).then_inc(hs_lo_ready, 1)

        @block.tensor
        def _(pe):
            pe.wait_ge(split_lo, len(pieces))
            with pe.Fori(0, NT) as t:
                pe.wait_ge(cat_loaded, 16 * t + 16)
                for g, (f, w) in enumerate(groups):
                    if g >= 3:
                        pe.wait_ge(catT_lo_ready, t * NG + g - 2)
                    for j in range(w):
                        last = nc.tensor.transpose(ps[:, g % 3, j * T:(j + 1) * T], cat[:, (f + j) * 128:(f + j + 1) * 128],
                                                   k.ident[0:T, 0:T])
                    last.then_inc(cat_turned, 1)
                pe.wait_ge(hs_lo_ready, 2 * t + 2)
                for g, (f0, w) in enumerate(groups):
                    pe.wait_ge(catT_lo_ready, t * NG + g + 1)
                    for f in range(f0, f0 + w):
                        for s in range(2):
                            cols = slice(s * 384, (s + 1) * 384)
                            last = three_passes(nc, ps[0:T, 3 + s, 0:384], (catT_hi[:, f, :], catT_lo[:, f, :]),
                                                (wo[0][:, f, cols], wo[1][:, f, cols]), f == 0, f == KO - 1)
                last.then_inc(out_summed, 1)
                pe.wait_ge(x2_ready, t + 1)
                for f in range(KF):
                    last = nc.tensor.transpose(ps[:, 5 + f // 4, (f % 4) * T:(f % 4 + 1) * T],
                                               x2[:, f * 128:(f + 1) * 128], k.ident[0:T, 0:T])
                last.then_inc(x2_turned, 1)
                pe.wait_ge(x2T_lo_ready, t + 1)
                for f in range(KF):
                    for s, bank in ((0, 7), (1, 4)):
                        cols = slice(s * 384, (s + 1) * 384)
                        last = three_passes(nc, ps[0:T, bank, 0:384], (x2T_hi[:, f, 0:T], x2T_lo[:, f, 0:T]),
                                            (w1[0][:, f, cols], w1[1][:, f, cols]), f == 0, f == KF - 1)
                last.then_inc(h1_summed, 1)


def spread(nc, k, a, count_R):
    with ExitStack() as mem:
        def sb(name, shape, dt=F32):
            return mem.enter_context(nc.sbuf_tensor(name, shape, dt))

        hs = [sb(f"hs1_{n}", [T, NT, D], F32R) for n in range(2)]
        w2 = split_weights(nc, mem, k, "w2", KF)
        stage = [sb(f"w2_stage{b}", [128, 1, D]) for b in range(2)]
        dinv_row = sb("dinv_row", [128, N])
        b1_col = sb("b1_col", [128, KF])
        scaled = sb("scaled", [128, KF, 2 * T])
        r_hi = sb("r_hi", [128, KF, 2 * T], F32R)
        r_lo = sb("r_lo", [128, KF, 2 * T], F32R)
        out_hi = sb("hs2_hi_out", [T, 2, D], F32R)
        out_lo = sb("hs2_lo_out", [T, 2, D], F32R)
        ps = k.ps
        summed = ps[:, 0:3, :].rearrange("p b (m n) -> p (b m) n", m=2)

        staged = [k.sem(f"w2_staged{b}") for b in range(2)]
        split_hi = k.sem("w2_split_hi")
        split_lo = k.sem("w2_split_lo")
        rows_loaded = k.sem("spread_rows_loaded")
        counts_in = k.sem("counts_in")
        hs_loaded = k.sem("hs1_loaded")
        agg_summed = k.sem("agg_summed")
        agg_scaled = k.sem("agg_scaled")
        r_ready = k.sem("r_ready")
        r_hi_ready = k.sem("r_hi_ready")
        r_lo_ready = k.sem("r_lo_ready")
        h2_summed = k.sem("h2_summed")
        hs2_hi_ready = k.sem("hs2_hi_ready")
        hs2_lo_ready = k.sem("hs2_lo_ready")
        stored = k.sem("spread_stored")
        block = mem.enter_context(nc.Block())

        @block.sync
        def _(sp):
            sp.dma_start(count_R[:, :, :].bitcast(F32), k.count_d).then_inc(counts_in, 16)
            for n in range(2):
                sp.dma_start(hs[n][:, :, :].bitcast(F32), k.hs1_d[n, :, :, :]).then_inc(hs_loaded, 16)
            for f in range(KF):
                if f >= 2:
                    sp.wait_ge(split_lo, f - 1)
                sp.dma_start(stage[f % 2][:, :, :], a["W2"][f * 128:(f + 1) * 128, :].rearrange("(k p) n -> p k n", p=128)
                             ).then_inc(staged[f % 2], 16)
            sp.sem_inc(stored, 32)
            with sp.Fori(0, PAIRS) as c:
                sp.wait_ge(hs2_lo_ready, 2 * c + 2)
                sp.dma_start(k.hs2_d[0, :, bass.ds(2 * c, 2), :], out_hi[:, :, :].bitcast(F32)).then_inc(stored, 16)
                sp.dma_start(k.hs2_d[1, :, bass.ds(2 * c, 2), :], out_lo[:, :, :].bitcast(F32)).then_inc(stored, 16)
            sp.wait_ge(stored, PAIRS * 32 + 32)

        @block.scalar
        def _(act):
            act.dma_start(dinv_row[:, :], k.dinv_d.rearrange("(o n) -> o n", o=1).to_broadcast([128, N])
                          ).then_inc(rows_loaded, 16)
            act.dma_start(b1_col[:, :], a["b1_cols"]).then_inc(rows_loaded, 16)
            for f in range(KF):
                act.wait_ge(staged[f % 2], 16 * (f // 2 + 1))
                nc.scalar.activation(w2[0][:, f:f + 1, :], stage[f % 2][:, :, :], ACT.Copy).then_inc(split_hi, 1)
            act.wait_ge(rows_loaded, 32)
            with act.Fori(0, PAIRS) as c:
                for b in range(3):
                    act.wait_ge(agg_scaled, 3 * c + b + 1)
                    for m in (2 * b, 2 * b + 1):
                        nc.scalar.activation(r_hi[:, m, :], scaled[:, m, :], ACT.Relu, bias=b1_col[:, m:m + 1]
                                             ).then_inc(r_hi_ready, 1)
                        act.wait_ge(r_hi_ready, KF * c + m + 1)
                        nc.scalar.activation(scaled[:, m, :], scaled[:, m, :], ACT.Relu, bias=b1_col[:, m:m + 1]
                                             ).then_inc(r_ready, 1)
                act.wait_ge(stored, 32 * c + 32)
                for j in range(2):
                    hold(act, k.held, h2_summed, 2 * c + j + 1)
                    nc.scalar.activation(out_hi[:, j, :].rearrange("p (s n) -> p s n", s=2),
                                         ps[0:T, 3 + 2 * j:5 + 2 * j, 0:384], ACT.Copy,
                                         scale=k.dinv[:, bass.ds(2 * c + j, 1)]).then_inc(hs2_hi_ready, 1)

        @block.vector
        def _(dve):
            for f in range(KF):
                dve.wait_ge(split_hi, f + 1)
                nc.vector.tensor_tensor(w2[1][:, f:f + 1, :], stage[f % 2][:, :, :], w2[0][:, f:f + 1, :].bitcast(F32),
                                        ALU.subtract).then_inc(split_lo, 1)
            dve.wait_ge(rows_loaded, 32)
            with dve.Fori(0, PAIRS) as c:
                for b in range(3):
                    ms = slice(2 * b, 2 * b + 2)
                    dve.wait_ge(agg_summed, KF * c + 2 * b + 2)
                    nc.vector.tensor_tensor(scaled[:, ms, :], summed[:, ms, 0:2 * T],
                                            dinv_row[:, bass.ds(2 * T * c, 2 * T)].unsqueeze(1).to_broadcast(
                                                [128, 2, 2 * T]), ALU.mult).then_inc(agg_scaled, 1)
                for b in range(3):
                    ms = slice(2 * b, 2 * b + 2)
                    dve.wait_ge(r_ready, KF * c + 2 * b + 2)
                    nc.vector.tensor_tensor(r_lo[:, ms, :], scaled[:, ms, :], r_hi[:, ms, :].bitcast(F32),
                                            ALU.subtract).then_inc(r_lo_ready, 1)
                dve.wait_ge(stored, 32 * c + 32)
                for j in range(2):
                    dve.wait_ge(hs2_hi_ready, 2 * c + j + 1)
                    nc.vector.scalar_tensor_tensor(
                        out=out_lo[:, j, :].rearrange("p (s n) -> p s n", s=2), in0=ps[0:T, 3 + 2 * j:5 + 2 * j, 0:384],
                        scalar=k.dinv[:, bass.ds(2 * c + j, 1)],
                        in1=out_hi[:, j, :].rearrange("p (s n) -> p s n", s=2).bitcast(F32),
                        op0=ALU.mult, op1=ALU.subtract).then_inc(hs2_lo_ready, 1)

        @block.tensor
        def _(pe):
            pe.wait_ge(counts_in, 16)
            pe.wait_ge(hs_loaded, 32)
            with pe.Fori(0, PAIRS) as c:
                for m in range(KF):
                    cols = slice(m * 128, (m + 1) * 128)
                    for s in range(NT):
                        for n in range(2):
                            last = nc.tensor.matmul(summed[:, m, 0:2 * T], hs[n][:, s, cols],
                                                    count_R[:, s, bass.ds(2 * T * c, 2 * T)],
                                                    start=(s == 0 and n == 0), stop=(s == NT - 1 and n == 1))
                    last.then_inc(agg_summed, 1)
                pe.wait_ge(split_lo, KF)
                for j in range(2):
                    nodes = slice(j * T, (j + 1) * T)
                    for f in range(KF):
                        if j == 0 and f % 2 == 0:
                            pe.wait_ge(r_lo_ready, 3 * c + f // 2 + 1)
                        for s in range(2):
                            wc = slice(s * 384, (s + 1) * 384)
                            last = three_passes(nc, ps[0:T, 3 + 2 * j + s, 0:384], (r_hi[:, f, nodes], r_lo[:, f, nodes]),
                                                (w2[0][:, f, wc], w2[1][:, f, wc]), f == 0, f == KF - 1)
                    last.then_inc(h2_summed, 1)


def finish(nc, k, a, count_R, out):
    with ExitStack() as mem:
        def sb(name, shape, dt=F32):
            return mem.enter_context(nc.sbuf_tensor(name, shape, dt))

        hs = [sb(f"hs2_{n}", [T, NT, D], F32R) for n in range(2)]
        cols_tile = [sb(f"count_cols{j}", [T, NT, T], F32R) for j in range(2)]
        x2 = [sb(f"x2_in{j}", [T, D]) for j in range(2)]
        y = [sb(f"y_out{j}", [T, D]) for j in range(2)]
        b_row = sb("b2_row", [T, D])
        stats = [sb(f"stats_out{j}", [T, 2, 6]) for j in range(2)]
        mean_var = [sb(f"mean_var_out{j}", [T, 2]) for j in range(2)]
        rstd = [sb(f"rstd_out{j}", [T, 1]) for j in range(2)]
        result = [sb(f"result{j}", [T, D]) for j in range(2)]
        ps = k.ps

        hs_loaded = k.sem("hs2_loaded")
        row_loaded = k.sem("b2_loaded")
        x2_loaded = [k.sem(f"x2_loaded{j}") for j in range(2)]
        cols_ready = k.sem("cols_ready")
        x2_biased = k.sem("x2_biased")
        out_summed = k.sem("final_summed")
        ln_step = k.sem("final_ln_step")
        rstd_step = k.sem("final_rstd_step")
        result_ready = k.sem("result_ready")
        out_stored = [k.sem(f"out_stored{j}") for j in range(2)]
        LN = 4
        block = mem.enter_context(nc.Block())

        @block.sync
        def _(sp):
            for n in range(2):
                sp.dma_start(hs[n][:, :, :].bitcast(F32), k.hs2_d[n, :, :, :]).then_inc(hs_loaded, 16)
            sp.dma_start(b_row[:, :], a["b2"].rearrange("(o n) -> o n", o=1).to_broadcast([T, D])).then_inc(row_loaded, 16)
            sp.sem_inc(out_stored[0], 16)
            sp.sem_inc(out_stored[1], 16)
            sp.sem_inc(ln_step, LN)
            with sp.Fori(0, PAIRS) as u:
                for j in range(2):
                    sp.wait_ge(ln_step, 2 * LN * u + LN)
                    sp.dma_start(x2[j][:, :], k.x2_d[:, bass.ds(2 * u + j, 1), :].rearrange("p o n -> p (o n)")
                                 ).then_inc(x2_loaded[j], 16)
                for j in range(2):
                    sp.wait_ge(result_ready, 2 * u + j + 1)
                    sp.dma_start(out[bass.ds(2 * T * u + j * T, T), :], result[j][:, :]).then_inc(out_stored[j], 16)
            sp.wait_ge(out_stored[0], 16 * PAIRS + 16)
            sp.wait_ge(out_stored[1], 16 * PAIRS + 16)

        @block.gpsimd
        def _(pool):
            pool.wait_ge(row_loaded, 16)
            pool.sem_inc(out_summed, 1)
            with pool.Fori(0, PAIRS) as u:
                for j in range(2):
                    pool.wait_ge(out_summed, 2 * u + 1)
                    nc.gpsimd.tensor_copy(cols_tile[j][:, :, :],
                                          count_R[:, :, bass.ds(2 * T * u + j * T, T)].bitcast(F32)).then_inc(cols_ready, 1)
                for j in range(2):
                    pool.wait_ge(x2_loaded[j], 16 * u + 16)
                    nc.gpsimd.tensor_tensor(x2[j][:, :], x2[j][:, :], b_row[:, :], ALU.add).then_inc(x2_biased, 1)
                for j in range(2):
                    n = 2 * u + j
                    pool.wait_ge(ln_step, LN * n + 2 * LN)
                    nc.gpsimd.tensor_tensor(rstd[j][:, :], mean_var[j][:, 1:2], k.eps[0:T, :], ALU.add
                                            ).then_inc(rstd_step, 1)
                    pool.wait_ge(rstd_step, 2 * n + 1)
                    nc.gpsimd.tensor_tensor(rstd[j][:, :], rstd[j][:, :], k.neg_half[0:T, :], ALU.pow
                                            ).then_inc(rstd_step, 1)

        @block.tensor
        def _(pe):
            pe.wait_ge(hs_loaded, 32)
            with pe.Fori(0, PAIRS) as u:
                for j in range(2):
                    pe.wait_ge(cols_ready, 2 * u + j + 1)
                    pe.wait_ge(ln_step, 2 * LN * u + LN)
                    for s in range(NT):
                        for n in range(2):
                            for h in range(2):
                                last = nc.tensor.matmul(ps[0:T, 2 * j + h, 0:384], cols_tile[j][:, s, :],
                                                        hs[n][:, s, h * 384:(h + 1) * 384],
                                                        start=(s == 0 and n == 0), stop=(s == NT - 1 and n == 1))
                    last.then_inc(out_summed, 1)

        @block.vector
        def _(dve):
            with dve.Fori(0, PAIRS) as u:
                for j in range(2):
                    n = 2 * u + j
                    step = [0]

                    def link(ins):
                        step[0] += 1
                        ins.then_inc(ln_step, 1)
                        hold(dve, k.held, ln_step, LN * n + LN + step[0])

                    dve.wait_ge(out_summed, n + 2)
                    dve.wait_ge(x2_biased, n + 1)
                    link(nc.vector.scalar_tensor_tensor(
                        out=y[j][:, :].rearrange("p (s n) -> p s n", s=2), in0=ps[0:T, 2 * j:2 * j + 2, 0:384],
                        scalar=k.dinv[:, bass.ds(n, 1)], in1=x2[j][:, :].rearrange("p (s n) -> p s n", s=2),
                        op0=ALU.mult, op1=ALU.add))
                    link(nc.vector.bn_stats(stats[j][:, 0, :], y[j][:, 0:384]))
                    link(nc.vector.bn_stats(stats[j][:, 1, :], y[j][:, 384:768]))
                    link(nc.vector.bn_aggr(mean_var[j][:, :], stats[j][:, :, :]))
                    dve.wait_ge(rstd_step, 2 * n + 2)
                    dve.wait_ge(out_stored[j], 16 * u + 16)
                    nc.vector.tensor_scalar(result[j][:, :], y[j][:, :], mean_var[j][:, 0:1], rstd[j][:, :],
                                            ALU.subtract, ALU.mult).then_inc(result_ready, 1)


def program(nc, a, out, stages=7):
    with ExitStack() as ctx:
        k = Core(nc, ctx)

        def sb(name, shape, dt=F32, stack=ctx):
            return stack.enter_context(nc.sbuf_tensor(name, shape, dt))

        k.held = k.sem("held")
        k.ps = ctx.enter_context(nc.psum_tensor("ps", [128, 8, 512], F32))
        k.ident = sb("ident", [128, 128])
        k.zeros = sb("zeros", [128, SW], BF16)
        k.far = sb("far", [128, 1])
        k.eps = sb("eps", [128, 1])
        k.neg_half = sb("neg_half", [128, 1])
        k.deg = sb("deg", [T, NT])
        k.dinv = sb("dinv", [T, NT])
        k.src_term = sb("src_term", [T, HALL, NT])
        k.src_drop = sb("src_drop", [T, HALL, NT])
        k.w_att = sb("w_att", [128, LAYERS * KF * 2 * HEADS])
        k.ranges_row = sb("ranges_row", [1, 2 * NT], I32)
        k.count_d = k.dram("count_d", (T, NT, N))
        k.h_d = k.dram("h_d", (T, HALL, NT, C))
        k.src_row_d = k.dram("src_row_d", (LAYERS, HEADS, N))
        k.lift_d = k.dram("lift_d", (2 * HALL, N))
        k.dinv_d = k.dram("dinv_d", (N,))
        k.cat_d = k.dram("cat_d", (T, NT, HALL + 1, C))
        k.x2_d = k.dram("x2_d", (T, NT, D))
        k.hs1_d = k.dram("hs1_d", (2, T, NT, D))
        k.hs2_d = k.dram("hs2_d", (2, T, NT, D))
        with ExitStack() as early:
            k.x1_hi = sb("x1_hi", [128, KF, N], F32R, early)
            k.x1_lo = sb("x1_lo", [128, KF, N], F32R, early)
            k.no_edge = sb("no_edge", [T, NT, 3 * SW], BF16, early)
            with ExitStack() as edges:
                k.loop_strip = sb("loop_strip", [T, 2 * N + 2], BF16, edges)
                k.iota_i = sb("iota_i", [128, 3 * SW], I32, edges)
                k.iota_h = sb("iota_h", [128, 3 * SW], F16, edges)
                k.src_col = sb("src_col", [128, CCOLS], F32, edges)
                k.dst_col = sb("dst_col", [128, CCOLS], F32, edges)
                nodes_in(nc, k, a)
                if stages >= 2:
                    counts(nc, k, a)
            if stages >= 3:
                heads_in(nc, k, a)
        if stages >= 4:
            attend(nc, k, a)
        if stages >= 5:
            combine(nc, k, a)
        with ExitStack() as late:
            count_R = sb("count_R", [T, NT, N], F32R, late)
            if stages >= 6:
                spread(nc, k, a, count_R)
            if stages >= 7:
                finish(nc, k, a, count_R, out)
        return k


def kernel(**inputs):
    import numpy as np
    import concourse.bacc as bacc
    from concourse.bass_utils import run_bass_kernel_spmd

    given = {n: np.asarray(v) for n, v in inputs.items()}
    gat = "L0_gnn_"
    turned = np.stack([given[f"{gat}W{i}"].T.reshape(KF, 128, KF // WP, WP * 128).transpose(2, 1, 0, 3)
                       for i in range(LAYERS)]).reshape(LAYERS * KF // WP, 128, KF, WP * 128)
    att = np.zeros((LAYERS, D, 2 * HEADS), np.float32)
    for i in range(LAYERS):
        for h in range(HEADS):
            att[i, h * C:(h + 1) * C, h] = given[f"{gat}a_src{i}"][h]
            att[i, h * C:(h + 1) * C, HEADS + h] = given[f"{gat}a_dst{i}"][h]
    arrays = {
        "x": given["x"], "src": given["src"], "dst": given["dst"],
        "W_ah": given[gat + "W_ah"], "b_ah_cols": given[gat + "b_ah"].reshape(KF, 128).T,
        "W_gat": np.stack([given[f"{gat}W{i}"] for i in range(LAYERS)]),
        "W_gat_turned": turned, "att": att.reshape(LAYERS, KF, 128, 2 * HEADS).transpose(2, 0, 1, 3),
        "b_gat": np.concatenate([given[f"{gat}b{i}"] for i in range(LAYERS)]),
        "W_out": given[gat + "W_out"], "b_out": given[gat + "b_out"],
        "W1": given["L1_gnn_W1"], "b1_cols": given["L1_gnn_b1"].reshape(KF, 128).T,
        "W2": given["L1_gnn_W2"], "b2": given["L1_gnn_b2"],
    }
    nc = bacc.Bacc("TRN2", target_bir_lowering=False, num_devices=1)
    aps = {}
    for name, value in arrays.items():
        arrays[name] = np.ascontiguousarray(value)
        aps[name] = nc.dram_tensor(name, value.shape, mybir.dt.from_np(value.dtype), kind="ExternalInput").ap()
    out = nc.dram_tensor("out", (N, D), F32, kind="ExternalOutput").ap()
    program(nc, aps, out)
    return run_bass_kernel_spmd(nc, [arrays], core_ids=[0]).results[0]["out"]
```

```python
from contextlib import ExitStack

import concourse.bass as bass
from concourse import mybir

F32 = mybir.dt.float32
F32R = mybir.dt.float32r
BF16 = mybir.dt.bfloat16
F16 = mybir.dt.float16
I32 = mybir.dt.int32
U16 = mybir.dt.uint16
ALU = mybir.AluOpType
ACT = mybir.ActivationFunctionType
AX_X = mybir.AxisListType.X

N = 1250
T = 125
NT = N // T
PAIRS = NT // 2
D = 768
KF = D // 128
LAYERS = 3
HEADS = 4
C = D // HEADS
HALL = LAYERS * HEADS
TERMS = 2 * HALL
PARTS = 3
KO = LAYERS * D // 128
E = 41250
CHUNKS = -(-E // 128)
FULL = E // 128
CROWS = 3
CCOLS = CROWS * 128
PAD_NODE = 2000
CSTEP = 3
SW = 417
FAR = 1e30
NO_MAX = -3e38
EXP_CAP = 1e30
SLOPE = 0.2
LN_EPS = 1e-5
WP = 2
HALF = N // 2
GT = NT // 2
RING = 4


def three_passes(nc, out, lhs, rhs, first, last):
    nc.tensor.matmul(out, lhs[0], rhs[0], start=first, stop=False)
    nc.tensor.matmul(out, lhs[0], rhs[1], start=False, stop=False)
    return nc.tensor.matmul(out, lhs[1], rhs[0], start=False, stop=last)


def hold(eng, held, semaphore, value):
    eng.wait_ge(semaphore, value)
    eng.sem_inc(held, 1)


class Core:

    def __init__(self, nc, ctx):
        self.nc, self.ctx = nc, ctx

    def sem(self, name):
        return self.ctx.enter_context(self.nc.semaphore(name))

    def dram(self, name, shape, dt=F32):
        return self.nc.dram_tensor(name, shape, dt, kind="Internal").ap()



def split_low(nc, out, whole, high):
    return nc.vector.tensor_tensor(out, whole, high.bitcast(F32), ALU.subtract)


def raw_and_low(nc, mem, name, feature_tiles):
    raw = mem.enter_context(nc.sbuf_tensor(f"{name}_raw", [128, feature_tiles, D], F32))
    low = nc.alloc_sbuf_tensor_at(f"{name}_lo", [128, feature_tiles, D], F32R,
                                  offset=nc.sbuf_base - feature_tiles * D * 4)
    return raw, low


def nodes_in(nc, k, a):
    with ExitStack() as mem:
        def sb(name, shape, dt=F32):
            return mem.enter_context(nc.sbuf_tensor(name, shape, dt))

        ones = sb("ones", [128, NT])
        tile_lo_i = sb("tile_lo_i", [NT, 1], I32)
        tile_lo = sb("tile_lo", [NT, 2])
        chunk_no = sb("chunk_no", [NT, 2, CCOLS])
        edge_i = sb("edge_i", [128, 2, CROWS, 128], I32)
        edge_f = sb("edge_f", [128, 2, CROWS, 128])
        span = sb("span", [128, 2, CROWS])
        span_diag = sb("span_diag", [128, 2, CROWS, 128])
        meets = sb("meets", [NT, 2, CCOLS])
        ranges = sb("ranges", [NT, 2])
        ranges_i = sb("ranges_i", [NT, 2], I32)
        w_raw = sb("wah_raw", [128, KF, D])
        w_hi = sb("wah_hi", [128, KF, D], F32R)
        w_lo = sb("wah_lo", [128, KF, D], F32R)
        bias = sb("bah_col", [128, KF])
        x_in = sb("x_in", [T, 2, D])
        xT_hi = sb("xT_hi", [128, KF, 4 * T], F32R)
        xT_lo = sb("xT_lo", [128, KF, 4 * T], F32R)
        x1 = sb("x1_pair", [128, KF, 2 * T])
        ps = k.ps

        pads_set = k.sem("pads_set")
        fills = k.sem("fills")
        iota_ready = k.sem("iota_ready")
        consts_ready = k.sem("consts_ready")
        edges_loaded = k.sem("edges_loaded")
        weights_loaded = k.sem("weights_loaded")
        bias_loaded = k.sem("bias_loaded")
        x_loaded = k.sem("x_loaded")
        vec_step = k.sem("vec_step")
        edges_float = k.sem("edges_float")
        edges_turned = k.sem("edges_turned")
        diag_ready = k.sem("diag_ready")
        span_spread = k.sem("span_spread")
        ranges_ready = k.sem("ranges_ready")
        ranges_moved = k.sem("ranges_moved")
        wah_hi_ready = k.sem("wah_hi_ready")
        wah_lo_ready = k.sem("wah_lo_ready")
        x_turned = k.sem("x_turned")
        xT_hi_ready = k.sem("xT_hi_ready")
        xT_lo_ready = k.sem("xT_lo_ready")
        x1_summed = k.sem("x1_summed")
        x1_copied = k.sem("x1_copied")
        x1_lo_ready = k.sem("x1_lo_ready")

        turned = ps[:, 3:6, 0:4 * T]
        summed = ps[:, 0:3, :].rearrange("p b (m n) -> p (b m) n", m=2)

        block = mem.enter_context(nc.Block())
        x_pairs = a["x"].rearrange("(i j p) f -> p i j f", j=2, p=T)

        def slot(x, i):
            return x[:, :, bass.ds(2 * T * (i % 2), 2 * T)].rearrange("p (b k) n -> p b k n", k=2)

        def load_pair(sp, i):
            sp.dma_start(x_in[:, :, :], x_pairs[:, bass.ds(i, 1), :, :].rearrange("p i j f -> p (i j) f")
                         ).then_inc(x_loaded, 16)

        @block.sync
        def _(sp):
            load_pair(sp, 0)
            sp.wait_ge(pads_set, 1)
            for which, arr in ((0, a["src"]), (1, a["dst"])):
                rows = arr[0:FULL * 128].rearrange("(r f) -> r f", f=128)
                sp.dma_start(edge_i[:, which, 0:2, :],
                             rows[0:256, :].rearrange("(c p) f -> p c f", p=128)).then_inc(edges_loaded, 16)
                sp.dma_start(edge_i[0:FULL - 256, which, 2, :], rows[256:FULL, :]).then_inc(edges_loaded, 16)
                sp.dma_start(edge_i[FULL - 256:FULL - 255, which, 2, 0:E - FULL * 128],
                             arr[FULL * 128:E].rearrange("(r f) -> r f", r=1)).then_inc(edges_loaded, 16)
            with sp.Fori(1, PAIRS) as i:
                sp.wait_ge(x_turned, i)
                load_pair(sp, i)
            sp.wait_ge(ranges_ready, 1)
            for n in range(2):
                sp.dma_start(k.ranges_row[0:1, n * NT:(n + 1) * NT], ranges_i[:, n:n + 1]).then_inc(ranges_moved, 16)
            sp.wait_ge(ranges_moved, 32)

        @block.gpsimd
        def _(pool):
            nc.gpsimd.memset(edge_i[:, :, :, :], PAD_NODE).then_inc(pads_set, 1)
            nc.gpsimd.memset(k.ident[:, :], 0.0).then_inc(fills, 1)
            pool.wait_ge(fills, 1)
            nc.gpsimd.affine_select(out=k.ident[:, :], in_=k.ident[:, :], compare_op=ALU.not_equal, fill=1.0, base=0,
                                    pattern=[[-1, 128]], channel_multiplier=1).then_inc(consts_ready, 1)
            nc.gpsimd.memset(ones[:, :], 1.0).then_inc(consts_ready, 1)
            nc.gpsimd.iota(k.iota_i[:, :], pattern=[[1, 3 * SW]], base=0, channel_multiplier=0).then_inc(iota_ready, 1)
            nc.gpsimd.iota(tile_lo_i[:, :], pattern=[[0, 1]], base=0, channel_multiplier=T).then_inc(iota_ready, 1)
            nc.gpsimd.memset(k.loop_strip[:, :], 0.0).then_inc(fills, 1)
            pool.wait_ge(fills, 2)
            nc.gpsimd.affine_select(out=k.loop_strip[:, N:N + T], in_=k.loop_strip[:, N:N + T],
                                    compare_op=ALU.not_equal, fill=1.0, base=0, pattern=[[-1, T]],
                                    channel_multiplier=1)
            nc.gpsimd.memset(k.zeros[:, :], 0.0)
            nc.gpsimd.memset(k.far[:, :], FAR)
            nc.gpsimd.memset(k.eps[:, :], LN_EPS)
            nc.gpsimd.memset(k.neg_half[:, :], -0.5)

        @block.vector
        def _(dve):
            done = [0]

            def link(ins):
                done[0] += 1
                ins.then_inc(vec_step, 1)
                dve.wait_ge(vec_step, done[0])

            dve.wait_ge(edges_loaded, 96)
            nc.vector.tensor_copy(edge_f[:, :, :, :], edge_i[:, :, :, :]).then_inc(edges_float, 1)
            dve.wait_ge(edges_float, 1)
            link(nc.vector.tensor_reduce(span[:, 0, :], edge_f[:, 1, :, :], op=ALU.min, axis=AX_X))
            link(nc.vector.tensor_reduce(span[:, 1, :], edge_f[:, 1, :, :], op=ALU.max, axis=AX_X))
            dve.wait_ge(consts_ready, 2)
            for n in range(2):
                for c in range(CROWS):
                    last = nc.vector.tensor_scalar(span_diag[:, n, c, :], k.ident[:, :], span[:, n, c:c + 1], None,
                                                   ALU.mult)
            last.then_inc(diag_ready, 1)
            dve.wait_ge(iota_ready, 2)
            nc.vector.tensor_copy(k.iota_h[:, :], k.iota_i[:, :])
            link(nc.vector.tensor_copy(tile_lo[:, 0:1], tile_lo_i[:, :]))
            nc.vector.tensor_scalar(tile_lo[:, 1:2], tile_lo[:, 0:1], float(T), None, ALU.add)
            link(nc.vector.tensor_copy(chunk_no[:, 0, :], k.iota_i[0:NT, 0:CCOLS]))
            link(nc.vector.tensor_scalar(chunk_no[:, 1, :], chunk_no[:, 0, :], -1.0, CCOLS - 1.0, ALU.mult, ALU.add))
            dve.wait_ge(edges_turned, 1)
            nc.vector.tensor_copy(k.src_col[:, :], ps[:, 6, 0:CCOLS])
            nc.vector.tensor_copy(k.dst_col[:, :], ps[:, 7, 0:CCOLS])
            dve.wait_ge(span_spread, 1)
            link(nc.vector.tensor_scalar(meets[:, 0, :], ps[0:NT, 3, 0:CCOLS], tile_lo[:, 1:2], None, ALU.is_lt))
            link(nc.vector.scalar_tensor_tensor(out=meets[:, 0, :], in0=ps[0:NT, 4, 0:CCOLS], scalar=tile_lo[:, 0:1],
                                                in1=meets[:, 0, :], op0=ALU.is_ge, op1=ALU.mult))
            link(nc.vector.tensor_tensor(meets[:, 1, :], meets[:, 0, :], chunk_no[:, 1, :], ALU.mult))
            link(nc.vector.tensor_tensor(meets[:, 0, :], meets[:, 0, :], chunk_no[:, 0, :], ALU.mult))
            link(nc.vector.tensor_reduce(ranges[:, 0:1], meets[:, 1, :], op=ALU.max, axis=AX_X))
            link(nc.vector.tensor_reduce(ranges[:, 1:2], meets[:, 0, :], op=ALU.max, axis=AX_X))
            link(nc.vector.tensor_scalar(ranges[:, 0:1], ranges[:, 0:1], -1.0, CCOLS - 1.0, ALU.mult, ALU.add))
            link(nc.vector.tensor_scalar(ranges[:, 0:1], ranges[:, 0:1], float(CHUNKS - 1), None, ALU.min))
            link(nc.vector.tensor_tensor(ranges[:, 1:2], ranges[:, 1:2], ranges[:, 0:1], ALU.max))
            link(nc.vector.tensor_scalar(ranges[:, 1:2], ranges[:, 1:2], 1.0, None, ALU.add))
            nc.vector.tensor_copy(ranges_i[:, :], ranges[:, :]).then_inc(ranges_ready, 1)
            for f in range(KF):
                dve.wait_ge(wah_hi_ready, f + 1)
                split_low(nc, w_lo[:, f, :], w_raw[:, f, :], w_hi[:, f, :]).then_inc(wah_lo_ready, 1)

            def split_x(i):
                dve.wait_ge(xT_hi_ready, i + 1)
                nc.vector.tensor_tensor(slot(xT_lo, i), turned.rearrange("p b (k n) -> p b k n", k=2),
                                        slot(xT_hi, i).bitcast(F32), ALU.subtract).then_inc(xT_lo_ready, 1)

            def split_x1(i):
                dve.wait_ge(x1_copied, (i + 2) * KF)
                nc.vector.tensor_tensor(k.x1_lo[:, :, bass.ds(2 * T * i, 2 * T)], x1[:, :, :],
                                        k.x1_hi[:, :, bass.ds(2 * T * i, 2 * T)].bitcast(F32),
                                        ALU.subtract).then_inc(x1_lo_ready, 1)

            split_x(0)
            with dve.Fori(0, PAIRS - 1) as i:
                split_x(i + 1)
                split_x1(i)
            split_x1(PAIRS - 1)

        @block.tensor
        def _(pe):
            pe.wait_ge(consts_ready, 2)
            pe.wait_ge(edges_float, 1)
            for n in range(2):
                for c in range(CROWS):
                    last = nc.tensor.transpose(ps[:, 6 + n, c * 128:(c + 1) * 128], edge_f[:, n, c, :], k.ident[:, :])
            last.then_inc(edges_turned, 1)
            pe.wait_ge(diag_ready, 1)
            for n in range(2):
                for c in range(CROWS):
                    last = nc.tensor.matmul(ps[0:NT, 3 + n, c * 128:(c + 1) * 128], ones[:, :], span_diag[:, n, c, :],
                                            start=True, stop=True)
            last.then_inc(span_spread, 1)
            pe.wait_ge(ranges_ready, 1)

            def turn_x(i):
                pe.wait_ge(x_loaded, (i + 1) * 16)
                for f in range(KF):
                    for j in range(2):
                        at = (f % 2) * 2 * T + j * T
                        last = nc.tensor.transpose(ps[:, 3 + f // 2, at:at + T], x_in[:, j, f * 128:(f + 1) * 128],
                                                   k.ident[0:T, 0:T])
                last.then_inc(x_turned, 1)

            def multiply(i):
                pair = bass.ds(2 * T * (i % 2), 2 * T)
                for m in range(KF):
                    cols = slice(m * 128, (m + 1) * 128)
                    if m % 2 == 0:
                        pe.wait_ge(x1_copied, i * KF + m + 2)
                    for f in range(KF):
                        last = three_passes(nc, summed[:, m, 0:2 * T], (w_hi[:, f, cols], w_lo[:, f, cols]),
                                            (xT_hi[:, f, pair], xT_lo[:, f, pair]), f == 0, f == KF - 1)
                    last.then_inc(x1_summed, 1)

            turn_x(0)
            pe.wait_ge(wah_lo_ready, KF)
            pe.sem_inc(x1_copied, KF)
            with pe.Fori(0, PAIRS - 1) as i:
                pe.wait_ge(xT_lo_ready, i + 1)
                turn_x(i + 1)
                multiply(i)
            pe.wait_ge(xT_lo_ready, PAIRS)
            multiply(PAIRS - 1)

        @block.scalar
        def _(act):
            for f in range(KF):
                act.dma_start(w_raw[:, f, :], a["W_ah"][f * 128:(f + 1) * 128, :]).then_inc(weights_loaded, 16)
            act.dma_start(bias[:, :], a["b_ah_cols"]).then_inc(bias_loaded, 16)
            act.wait_ge(weights_loaded, 16 * KF)
            for f in range(KF):
                nc.scalar.activation(w_hi[:, f, :], w_raw[:, f, :], ACT.Copy).then_inc(wah_hi_ready, 1)
            act.wait_ge(bias_loaded, 16)

            def high_x(i):
                hold(act, k.held, x_turned, i + 1)
                nc.scalar.activation(slot(xT_hi, i), turned.rearrange("p b (k n) -> p b k n", k=2), ACT.Copy
                                     ).then_inc(xT_hi_ready, 1)

            def take_x1(i):
                for m in range(KF):
                    if m % 2 == 0:
                        act.wait_ge(x1_summed, i * KF + m + 2)
                    if m == 0:
                        act.wait_ge(x1_lo_ready, i + 1)
                    nc.scalar.activation(x1[:, m, :], summed[:, m, 0:2 * T], ACT.Relu, bias=bias[:, m:m + 1])
                    nc.scalar.activation(k.x1_hi[:, m, bass.ds(2 * T * i, 2 * T)], summed[:, m, 0:2 * T], ACT.Relu,
                                         bias=bias[:, m:m + 1]).then_inc(x1_copied, 1)

            act.sem_inc(x1_lo_ready, 1)
            high_x(0)
            with act.Fori(0, PAIRS - 1) as i:
                high_x(i + 1)
                take_x1(i)
            take_x1(PAIRS - 1)


def counts(nc, k, a, count_T):
    with ExitStack() as mem:
        def sb(name, shape, dt=F32):
            return mem.enter_context(nc.sbuf_tensor(name, shape, dt))

        src_hot = sb("src_hot", [128, CSTEP, 3 * SW], BF16)
        dst_hot = sb("dst_hot", [128, CSTEP, T], BF16)
        count_tile = sb("count_tile", [T, 2, 3, SW])
        wt = sb("w_turned", [128, KF, WP * 128])
        att = sb("att_cols", [128, LAYERS, KF, 2 * HEADS])
        root = sb("root", [T, NT])
        ps = k.ps
        acc = ps[0:T, 0:6, 0:SW]

        hots_ready = k.sem("hots_ready")
        hots_used = k.sem("hots_used")
        counts_summed = k.sem("counts_summed")
        counts_copied = k.sem("counts_copied")
        no_edge_ready = k.sem("no_edge_ready")
        counts_turned = k.sem("counts_turned")
        turned_copied = k.sem("turned_copied")
        dst_shifted = k.sem("dst_shifted")
        deg_root = k.sem("deg_root")
        att_loaded = k.sem("att_loaded")
        wt_loaded = k.sem("wt_loaded")
        most = NT * (CHUNKS + CSTEP)
        pieces = LAYERS * KF // WP
        GROUPS = ((0, 4, 6), (4, 4, 7), (8, 2, 6))
        TERM_AT = 2 * T

        def piece(t):
            return (t * pieces) // NT

        block = mem.enter_context(nc.Block())

        def chunk_range(eng, t):
            first = eng.value_load(k.ranges_row[0:1, bass.ds(t, 1)], min_val=0, max_val=CHUNKS)
            end = eng.value_load(k.ranges_row[0:1, bass.ds(t + NT, 1)], min_val=1, max_val=CHUNKS + 1)
            return first, end

        @block.sync
        def _(sp):
            sp.dma_start(att[:, :, :, :], a["att"]).then_inc(att_loaded, 16)
            with sp.Fori(0, NT) as t:
                sp.wait_ge(counts_turned, 3 * t + 1)
                sp.dma_start(wt[:, :, :], a["W_gat_turned"][bass.ds(piece(t), 1), :, :, :].rearrange(
                    "o p c f -> p (o c) f")).then_inc(wt_loaded, 16)

        @block.vector
        def _(dve):
            made = nc.vector.alloc_register("made")
            nc.vector.reg_mov(made, 1)
            dve.sem_inc(hots_used, CSTEP)
            with dve.Fori(0, NT) as t:
                first, end = chunk_range(nc.vector, t)
                with dve.Fori(first, end, CSTEP) as c:
                    n = nc.vector.snap(made, min_val=1, max_val=most)
                    for j in range(CSTEP):
                        dve.wait_ge(hots_used, n + j)
                        nc.vector.tensor_scalar(src_hot[:, j, :], k.iota_h[:, :], k.src_col[:, bass.ds(c + j, 1)], None,
                                                ALU.is_equal)
                        nc.vector.tensor_scalar(dst_hot[:, j, :], k.iota_h[:, 0:T], k.dst_col[:, bass.ds(c + j, 1)],
                                                None, ALU.is_equal).then_inc(hots_ready, 1)
                    nc.vector.reg_add(made, made, CSTEP)
                dve.wait_ge(hots_ready, nc.vector.snap(made, min_val=2, max_val=most) - 1)
                nc.vector.tensor_scalar(k.dst_col[:, :], k.dst_col[:, :], float(T), None,
                                        ALU.subtract).then_inc(dst_shifted, 1)
                dve.wait_ge(dst_shifted, t + 1)
            dve.wait_ge(deg_root, 1)
            nc.vector.reciprocal(k.dinv[:, :], root[:, :])

        @block.tensor
        def _(pe):
            pe.sem_inc(counts_copied, 2)
            pe.sem_inc(turned_copied, 3)
            pe.sem_inc(counts_turned, 1)
            pe.wait_ge(att_loaded, 16)
            taken = nc.tensor.alloc_register("taken")
            nc.tensor.reg_mov(taken, 1)

            def sum_tile(t, j):
                summed = acc[:, 3 * j:3 * j + 3, :]
                first, end = chunk_range(nc.tensor, t)
                pe.wait_ge(counts_copied, t + 1)
                for s in range(3):
                    nc.tensor.matmul(summed[:, s, :], k.loop_strip[:, N:N + T],
                                     k.loop_strip[:, bass.ds(N - T * t + SW * s, SW)], start=True, stop=False)
                with pe.Fori(first, end, CSTEP) as c:
                    n = nc.tensor.snap(taken, min_val=1, max_val=most)
                    for i in range(CSTEP):
                        pe.wait_ge(hots_ready, n + i)
                        for s in range(3):
                            last = nc.tensor.matmul(summed[:, s, :], dst_hot[:, i, :], src_hot[:, i, s * SW:(s + 1) * SW],
                                                    start=False, stop=False)
                        last.then_inc(hots_used, 1)
                    nc.tensor.reg_add(taken, taken, CSTEP)
                for s in range(3):
                    last = nc.tensor.matmul(summed[:, s, :], k.zeros[0:T, 0:T], k.zeros[0:T, :], start=False, stop=True)
                last.then_inc(counts_summed, 1)

            def turn_tile(t, j):
                flat = count_tile[:, j, :, :].rearrange("p a b -> p (a b)")
                pe.wait_ge(counts_copied, t + 3)
                for g, (s0, w, bank) in enumerate(GROUPS):
                    pe.wait_ge(turned_copied, 3 * t + (g + 1 if g < 2 else 4))
                    for s in range(w):
                        last = nc.tensor.transpose(ps[0:T, bank, s * T:(s + 1) * T],
                                                   flat[:, (s0 + s) * T:(s0 + s + 1) * T], k.ident[0:T, 0:T])
                    if g == 2:
                        pe.wait_ge(wt_loaded, 16 * t + 16)
                        for f in range(WP):
                            at = TERM_AT + f * 2 * HEADS
                            for c in range(KF):
                                last = nc.tensor.matmul(ps[:, bank, at:at + 2 * HEADS], wt[:, c, f * 128:(f + 1) * 128],
                                                        att[:, bass.ds(piece(t) // (KF // WP), 1), c, :].rearrange(
                                                            "p o h -> p (o h)"), start=c == 0, stop=c == KF - 1)
                    last.then_inc(counts_turned, 1)

            sum_tile(0, 0)
            with pe.Fori(0, NT // 2 - 1) as u:
                sum_tile(2 * u + 1, 1)
                turn_tile(2 * u, 0)
                sum_tile(2 * u + 2, 0)
                turn_tile(2 * u + 1, 1)
            sum_tile(NT - 1, 1)
            turn_tile(NT - 2, 0)
            turn_tile(NT - 1, 1)

        @block.scalar
        def _(act):
            act.sem_inc(no_edge_ready, 1)
            with act.Fori(0, NT) as t:
                mine = count_tile[:, bass.ds(t % 2, 1), :, :].rearrange("p o a b -> p (o a) b")
                act.wait_ge(counts_summed, t + 1)
                hold(act, k.held, no_edge_ready, t + 1)
                nc.scalar.activation(mine, acc[:, bass.ds(3 * (t % 2), 3), :], ACT.Copy,
                                     accum_out=k.deg[:, bass.ds(t, 1)]).then_inc(counts_copied, 1)
                hold(act, k.held, counts_copied, t + 3)
                nc.scalar.activation(k.no_edge[:, bass.ds(t, 1), :].rearrange("p a (b c) -> p (a b) c", c=SW),
                                     mine, ACT.Relu, bias=k.far[0:T, :], scale=-FAR).then_inc(no_edge_ready, 1)
                for g, (s0, w, bank) in enumerate(GROUPS):
                    hold(act, k.held, counts_turned, 3 * t + g + 2)
                    last = nc.scalar.activation(count_T[:, s0:s0 + w, bass.ds(T * t, T)],
                                                ps[0:T, bank, 0:w * T].rearrange("p (a b) -> p a b", b=T), ACT.Copy)
                    if g == 2:
                        last = nc.scalar.activation(
                            k.w_att[:, bass.ds(piece(t) * WP, WP), :], ps[:, bank, TERM_AT:TERM_AT + WP * 2 * HEADS
                                                                          ].rearrange("p (f h) -> p f h", h=2 * HEADS),
                            ACT.Copy)
                    last.then_inc(turned_copied, 1)
            nc.scalar.activation(root[:, :], k.deg[:, :], ACT.Sqrt).then_inc(deg_root, 1)


def heads_in(nc, k, a):
    with ExitStack() as mem:
        def sb(name, shape, dt=F32):
            return mem.enter_context(nc.sbuf_tensor(name, shape, dt))

        w_raw = sb("w_raw", [128, KF, D])
        w_hi = sb("w_hi", [128, KF, D], F32R)
        w_lo = sb("w_lo", [128, KF, D], F32R)
        wa_hi = sb("wa_hi", [128, LAYERS, KF, 2 * HEADS], F32R)
        wa_lo = sb("wa_lo", [128, LAYERS, KF, 2 * HEADS], F32R)
        h_out = [sb(f"h_out{b}", [T, D]) for b in range(2)]
        terms = sb("terms", [T, NT, TERMS])
        dst_term = sb("dst_term", [T, HALL, NT])
        rows = sb("term_rows", [TERMS, N])
        src_spread = [sb(f"src_spread{h}", [T, N]) for h in range(HEADS)]
        scores = [sb(f"scores{b}", [T, N], BF16) for b in range(2)]
        top = sb("top", [T, HEADS, NT])
        low = sb("low", [T, HEADS, NT])
        lifts = sb("lifts", [T, NT, TERMS])
        ps = k.ps

        wa_split = k.sem("wa_split")
        terms_summed = k.sem("terms_summed")
        terms_copied = k.sem("terms_copied")
        rows_turned = k.sem("rows_turned")
        rows_copied = k.sem("rows_copied")
        rows_stored = k.sem("rows_stored")
        spread_loaded = [k.sem(f"spread_loaded{h}") for h in range(HEADS)]
        raw_loaded = k.sem("raw_loaded")
        w_hi_ready = k.sem("w_hi_ready")
        w_lo_ready = k.sem("w_lo_ready")
        h_summed = k.sem("h_summed")
        h_copied = k.sem("h_copied")
        h_stored = [k.sem(f"h_stored{b}") for b in range(2)]
        terms_taken = k.sem("terms_taken")
        maxima_step = k.sem("maxima_step")
        lift_step = k.sem("lift_step")
        LIFT = 5

        block = mem.enter_context(nc.Block())
        w_all = a["W_gat"].rearrange("l (k p) n -> p l k n", p=128)
        layer_maxima = NT * HEADS
        part_k = KF // PARTS

        @block.gpsimd
        def _(pool):
            with pool.Fori(0, LAYERS) as l:
                for part in range(PARTS):
                    ks = slice(part_k * part, part_k * (part + 1))
                    pool.wait_ge(w_hi_ready, PARTS * l + part + 1)
                    nc.gpsimd.tensor_tensor(w_lo[:, ks, :], w_raw[:, ks, :], w_hi[:, ks, :].bitcast(F32),
                                            ALU.subtract).then_inc(w_lo_ready, 1)

        @block.sync
        def _(sp):
            def load_weights(l):
                sp.dma_start(w_raw[:, :, :], w_all[:, bass.ds(l, 1), :, :].rearrange("p l k n -> p (l k) n")
                             ).then_inc(raw_loaded, 16)

            def load_spread(l, h):
                sp.dma_start(src_spread[h][:, :], k.src_row_d[bass.ds(l * 2 * HEADS + h, 1), :].to_broadcast([T, N])
                             ).then_inc(spread_loaded[h], 16)

            load_weights(0)
            sp.wait_ge(rows_stored, 16)
            for h in range(HEADS):
                load_spread(0, h)
            with sp.Fori(0, LAYERS - 1) as l:
                sp.wait_ge(w_lo_ready, PARTS * (l + 1))
                load_weights(l + 1)
                for h in range(HEADS):
                    sp.wait_ge(maxima_step, l * layer_maxima + (h + 1) * NT + 1)
                    load_spread(l + 1, h)

        @block.scalar
        def _(act):
            nc.scalar.activation(wa_hi[:, :, :, :], k.w_att[:, :, :].rearrange("p (l f) h -> p l f h", l=LAYERS), ACT.Copy
                                 ).then_inc(wa_split, 1)
            act.sem_inc(h_copied, 2)
            act.wait_ge(terms_summed, 1)
            nc.scalar.activation(terms[:, :, :], ps[0:T, 7, 0:NT * TERMS].rearrange("p (t h) -> p t h", h=TERMS),
                                 ACT.Copy).then_inc(terms_copied, 1)
            act.wait_ge(rows_turned, 1)
            for g, w in ((0, 4), (1, 4), (2, 2)):
                nc.scalar.activation(rows[:, 4 * g * T:(4 * g + w) * T], ps[0:TERMS, 4 + g, 0:w * T],
                                     ACT.Copy).then_inc(rows_copied, 1)
            act.wait_ge(rows_copied, 3)
            act.dma_start(k.src_row_d, rows[:, :]).then_inc(rows_stored, 16)
            act.sem_inc(h_stored[0], 16)
            act.sem_inc(h_stored[1], 16)
            with act.Fori(0, LAYERS) as l:
                act.wait_ge(raw_loaded, (l + 1) * 16)
                act.wait_ge(h_copied, l * NT + 2)
                for part in range(PARTS):
                    ks = slice(part_k * part, part_k * (part + 1))
                    nc.scalar.activation(w_hi[:, ks, :], w_raw[:, ks, :], ACT.Copy).then_inc(w_hi_ready, 1)
                for t in range(NT):
                    act.wait_ge(h_summed, l * NT + t + 1)
                    act.wait_ge(h_stored[t % 2], (l * (NT // 2) + t // 2 + 1) * 16)
                    nc.scalar.activation(h_out[t % 2][:, :].rearrange("p (s n) -> p s n", s=2),
                                         ps[0:T, 2 * (t % 2):2 * (t % 2) + 2, 0:D // 2], ACT.Copy).then_inc(h_copied, 1)
                    act.wait_ge(h_copied, l * NT + t + 3)
                    act.dma_start(k.h_d[:, bass.ds(l * HEADS, HEADS), t, :],
                                  h_out[t % 2][:, :].rearrange("p (h c) -> p h c", c=C)).then_inc(h_stored[t % 2], 16)
            act.wait_ge(rows_turned, 2)
            for g, w in ((0, 4), (1, 4), (2, 2)):
                nc.scalar.activation(rows[:, 4 * g * T:(4 * g + w) * T], ps[0:TERMS, 4 + g, 0:w * T],
                                     ACT.Copy).then_inc(rows_copied, 1)
            act.wait_ge(rows_copied, 6)
            act.dma_start(k.lift_d, rows[:, :]).then_inc(rows_stored, 16)
            act.wait_ge(rows_stored, 32)
            for b in range(2):
                act.wait_ge(h_stored[b], (LAYERS * (NT // 2) + 1) * 16)

        @block.vector
        def _(dve):
            dve.wait_ge(wa_split, 1)
            nc.vector.tensor_tensor(wa_lo[:, :, :, :], k.w_att[:, :, :].rearrange("p (l f) h -> p l f h", l=LAYERS),
                                    wa_hi[:, :, :, :].bitcast(F32), ALU.subtract).then_inc(wa_split, 1)
            dve.wait_ge(terms_copied, 1)
            by_head = terms[:, :, :].rearrange("p t (l s h) -> p l s h t", l=LAYERS, s=2)

            def all_heads(x):
                return x.rearrange("p (l h) t -> p l h t", l=LAYERS)

            nc.vector.tensor_copy(all_heads(k.src_term[:, :, :]), by_head[:, :, 0, :, :])
            nc.vector.tensor_scalar(all_heads(k.src_drop[:, :, :]), by_head[:, :, 0, :, :], SLOPE - 1.0, None, ALU.mult)
            nc.vector.tensor_copy(all_heads(dst_term[:, :, :]), by_head[:, :, 1, :, :]).then_inc(terms_taken, 1)
            dve.sem_inc(maxima_step, 1)
            dve.wait_ge(terms_taken, 1)
            with dve.Fori(0, LAYERS) as l:
                for h in range(HEADS):
                    dve.wait_ge(spread_loaded[h], (l + 1) * 16)
                    for t in range(NT):
                        n = h * NT + t
                        hold(dve, k.held, maxima_step, l * layer_maxima + max(n, 1))
                        nc.vector.tensor_tensor_reduce(
                            out=scores[n % 2][:, :], in0=src_spread[h][:, :], in1=k.no_edge[:, t, 0:N], scale=1.0,
                            scalar=NO_MAX, op0=ALU.subtract, op1=ALU.max,
                            accum_out=top[:, h, t:t + 1]).then_inc(maxima_step, 1)
                dve.wait_ge(maxima_step, (l + 1) * layer_maxima + 1)
                chain = [0]

                def link(ins):
                    chain[0] += 1
                    ins.then_inc(lift_step, 1)
                    dve.wait_ge(lift_step, l * LIFT + chain[0])

                mine = dst_term[:, bass.ds(l * HEADS, HEADS), :]
                link(nc.vector.tensor_tensor(top[:, :, :], top[:, :, :], mine, ALU.add))
                link(nc.vector.tensor_scalar(low[:, :, :], top[:, :, :], SLOPE, None, ALU.mult))
                link(nc.vector.tensor_tensor(top[:, :, :], top[:, :, :], low[:, :, :], ALU.max))
                pairs = lifts[:, :, bass.ds(l * 2 * HEADS, 2 * HEADS)].rearrange("p t (h u) -> p h u t", u=2)
                link(nc.vector.tensor_tensor(pairs[:, :, 0, :], mine, top[:, :, :], ALU.subtract))
                link(nc.vector.scalar_tensor_tensor(out=pairs[:, :, 1, :], in0=mine, scalar=SLOPE,
                                                    in1=top[:, :, :], op0=ALU.mult, op1=ALU.subtract))

        @block.tensor
        def _(pe):
            pe.wait_ge(wa_split, 2)
            for t in range(NT):
                nodes = slice(t * T, (t + 1) * T)
                for f in range(KF):
                    last = three_passes(nc, ps[0:T, 7, t * TERMS:(t + 1) * TERMS].rearrange("p (l h) -> p l h", l=LAYERS),
                                        (k.x1_hi[:, f, nodes], k.x1_lo[:, f, nodes]),
                                        (wa_hi[:, :, f, :], wa_lo[:, :, f, :]), f == 0, f == KF - 1)
            last.then_inc(terms_summed, 1)

            def turn_rows(x):
                for t in range(NT):
                    last = nc.tensor.transpose(ps[0:TERMS, 4 + t // 4, (t % 4) * T:(t % 4 + 1) * T], x[:, t, :],
                                               k.ident[0:T, 0:T])
                last.then_inc(rows_turned, 1)

            pe.wait_ge(terms_copied, 1)
            turn_rows(terms)
            with pe.Fori(0, LAYERS) as l:
                for t in range(NT):
                    pe.wait_ge(h_copied, l * NT + t + 1)
                    for f in range(KF):
                        if t == 0 and f % part_k == 0:
                            pe.wait_ge(w_lo_ready, PARTS * l + f // part_k + 1)
                        for s in range(2):
                            nodes = slice(t * T, (t + 1) * T)
                            cols = slice(s * D // 2, (s + 1) * D // 2)
                            last = three_passes(nc, ps[0:T, 2 * (t % 2) + s, 0:D // 2],
                                                (k.x1_hi[:, f, nodes], k.x1_lo[:, f, nodes]),
                                                (w_hi[:, f, cols], w_lo[:, f, cols]), f == 0, f == KF - 1)
                    last.then_inc(h_summed, 1)
            pe.wait_ge(rows_copied, 3)
            pe.wait_ge(lift_step, LIFT * LAYERS)
            turn_rows(lifts)


def attend(nc, k, a, count_T, wo_raw):
    with ExitStack() as mem:
        def sb(name, shape, dt=F32):
            return mem.enter_context(nc.sbuf_tensor(name, shape, dt))

        lift = [sb(f"lift{q}", [T, 2, N]) for q in range(2)]
        h_in = [sb(f"h_in{q}", [T, NT, C + 1]) for q in range(2)]
        score = [sb(f"score{r}", [T, HALF]) for r in range(RING)]
        weight = [sb(f"weight{r}", [T, HALF]) for r in range(RING)]
        sums = [sb(f"sums{g}", [T, GT, C + 1]) for g in range(2)]
        inverse = [sb(f"inverse{g}", [T, GT, 1]) for g in range(2)]
        normed = [sb(f"normed{g}", [T, GT, C]) for g in range(2)]
        bias = sb("gat_bias", [T, HALL + 1, C])
        ps = k.ps
        banks = [ps[0:T, 3 * g:3 * g + 3, :].rearrange("p b (m n) -> p (b m) n", m=2) for g in range(2)]

        wo_loaded = k.sem("wo_loaded")
        bias_loaded = k.sem("gat_bias_loaded")
        head_loaded = [k.sem(f"head_loaded{q}") for q in range(2)]
        ones_set = k.sem("ones_set")
        score_ready = k.sem("score_ready")
        exp_ready = k.sem("exp_ready")
        weight_ready = k.sem("weight_ready")
        weight_used = k.sem("weight_used")
        sums_copied = k.sem("sums_copied")
        norm_step = k.sem("norm_step")
        biased = k.sem("biased")
        cat_stored = [k.sem(f"cat_stored{g}") for g in range(2)]

        PAIR = 4 * NT
        GROUPS = 4
        block = mem.enter_context(nc.Block())

        def group_of(i):
            return i // NT % 2, i % NT, i // (2 * NT)

        @block.sync
        def _(sp):
            def load_head(head, q):
                sp.dma_start(lift[q][:, :, :], k.lift_d[bass.ds(2 * head, 2), :].rearrange(
                    "(o u) n -> o u n", o=1).to_broadcast([T, 2, N])).then_inc(head_loaded[q], 16)
                sp.dma_start(h_in[q][:, :, 0:C], k.h_d[:, bass.ds(head, 1), :, :].rearrange(
                    "p o t c -> p (o t) c")).then_inc(head_loaded[q], 16)

            load_head(0, 0)
            load_head(1, 1)
            sp.dma_start(bias[:, 1:, :], a["b_gat"].rearrange("(o h c) -> o h c", o=1, c=C).to_broadcast([T, HALL, C])
                         ).then_inc(bias_loaded, 16)
            sp.dma_start(wo_raw[:, :, :], a["W_out"].rearrange("(k p) n -> p k n", p=128)).then_inc(wo_loaded, 16)
            sp.sem_inc(cat_stored[0], 16)
            sp.sem_inc(cat_stored[1], 16)

            def store(n, g, slot):
                sp.wait_ge(biased, n + 1)
                sp.dma_start(k.cat_d[:, g * GT:(g + 1) * GT, bass.ds(slot, 1), :].rearrange("p t o c -> p t (o c)"),
                             normed[g][:, :, :]).then_inc(cat_stored[g], 16)

            with sp.Fori(0, HALL // 2) as p:
                for gg in range(GROUPS):
                    store(p * GROUPS + gg, (gg + 1) % 2, 2 * p + (gg + 1) // 2)
                    if gg >= 2:
                        q = gg - 2
                        sp.wait_ge(weight_used, p * PAIR + 2 * NT * (q + 1) + RING)
                        load_head(2 * ((p + 1) % (HALL // 2)) + q, q)
            store(2 * HALL, 1, HALL)
            sp.wait_ge(wo_loaded, 16)
            for g in range(2):
                sp.wait_ge(cat_stored[g], (HALL + 1 + g) * 16)
                sp.wait_ge(head_loaded[g], (HALL // 2 + 1) * 32)

        @block.vector
        def _(dve):
            dve.sem_inc(weight_ready, RING)
            dve.sem_inc(weight_used, RING - 1)
            dve.sem_inc(norm_step, 6)

            def make_score(p, i):
                g, s, q = group_of(i)
                cols = slice(g * HALF, (g + 1) * HALF)
                if i % (2 * NT) == 0:
                    dve.wait_ge(head_loaded[q], (p + 1) * 32)
                dve.wait_ge(weight_ready, p * PAIR + i + 1)
                nc.vector.scalar_tensor_tensor(out=score[i % RING][:, :], in0=lift[q][:, 1, cols],
                                               scalar=k.src_drop[:, bass.ds(2 * p + q, 1), s], in1=lift[q][:, 0, cols],
                                               op0=ALU.add, op1=ALU.max).then_inc(score_ready, 1)

            def normalise(n, g, before):
                dve.wait_ge(sums_copied, n + 2)
                base = 6 + 3 * n
                nc.vector.tensor_scalar(inverse[g][:, :, :], sums[g][:, :, C:C + 1], 1e-16, None,
                                        ALU.add).then_inc(norm_step, 1)
                dve.wait_ge(norm_step, base + 1)
                nc.vector.reciprocal(inverse[g][:, :, :], inverse[g][:, :, :]).then_inc(norm_step, 1)
                dve.wait_ge(norm_step, base + 2)
                dve.wait_ge(cat_stored[g], before * 16 + 16)
                nc.vector.tensor_tensor(normed[g][:, :, :], sums[g][:, :, 0:C],
                                        inverse[g][:, :, :].to_broadcast([T, GT, C]), ALU.mult).then_inc(norm_step, 1)

            with dve.Fori(0, HALL // 2) as p:
                make_score(p, 0)
                for i in range(PAIR):
                    g, s, q = group_of(i)
                    if i < PAIR - 1:
                        make_score(p, i + 1)
                    dve.wait_ge(exp_ready, p * PAIR + i + 1)
                    dve.wait_ge(weight_used, p * PAIR + i + 1)
                    nc.vector.scalar_tensor_tensor(out=weight[i % RING][:, :], in0=score[i % RING][:, :], scalar=EXP_CAP,
                                                   in1=count_T[:, s, g * HALF:(g + 1) * HALF], op0=ALU.min,
                                                   op1=ALU.mult).then_inc(weight_ready, 1)
                    if s == 6:
                        gg = i // NT
                        normalise(p * GROUPS + gg, (gg + 1) % 2, 2 * p + gg // 2)
            normalise(2 * HALL, 1, HALL)

        @block.scalar
        def _(act):
            act.sem_inc(sums_copied, 1)

            def copy_sums(n, g):
                act.wait_ge(weight_used, n * NT + RING)
                act.wait_ge(norm_step, 3 * n + 3)
                nc.scalar.activation(sums[g][:, :, :], banks[g][:, 0:GT, 0:C + 1], ACT.Copy).then_inc(sums_copied, 1)

            with act.Fori(0, HALL // 2) as p:
                for i in range(PAIR):
                    g, s, q = group_of(i)
                    hold(act, k.held, score_ready, p * PAIR + i + 1)
                    nc.scalar.activation(score[i % RING][:, :], score[i % RING][:, :], ACT.Exp,
                                         bias=k.src_term[:, bass.ds(2 * p + q, 1), s]).then_inc(exp_ready, 1)
                    if s == 3:
                        gg = i // NT
                        copy_sums(p * GROUPS + gg, (gg + 1) % 2)
            copy_sums(2 * HALL, 1)

        @block.tensor
        def _(pe):
            for b in range(3):
                for half in range(2):
                    last = nc.tensor.matmul(ps[0:T, 3 + b, half * 256:(half + 1) * 256], k.zeros[0:T, 0:T],
                                            k.zeros[0:T, 0:256], start=True, stop=True)
            last.then_inc(weight_used, 1)
            pe.wait_ge(ones_set, 4)
            with pe.Fori(0, HALL // 2) as p:
                for i in range(PAIR):
                    g, s, q = group_of(i)
                    if s == 0:
                        pe.wait_ge(sums_copied, p * GROUPS + i // NT + 1)
                    pe.wait_ge(weight_ready, p * PAIR + i + 1 + RING)
                    for t in range(GT):
                        last = nc.tensor.matmul(banks[g][:, t, 0:C + 1], weight[i % RING][:, t * T:(t + 1) * T],
                                                h_in[q][:, s, :], start=(s == 0 and t % 2 == 0), stop=(s == NT - 1),
                                                skip_group_check=True)
                    last.then_inc(weight_used, 1)

        @block.gpsimd
        def _(pool):
            for q in range(2):
                nc.gpsimd.memset(h_in[q][:, :, C:C + 1], 1.0).then_inc(ones_set, 1)
            nc.gpsimd.memset(bias[:, 0:1, :], 0.0).then_inc(ones_set, 1)
            pool.wait_ge(bias_loaded, 16)
            pool.sem_inc(ones_set, 1)

            def add_bias(n, g, slot):
                hold(pool, k.held, norm_step, 3 * n + 9)
                nc.gpsimd.tensor_tensor(normed[g][:, :, :], normed[g][:, :, :],
                                        bias[:, bass.ds(slot, 1), :].to_broadcast([T, GT, C]), ALU.add
                                        ).then_inc(biased, 1)

            with pool.Fori(0, HALL // 2) as p:
                for gg in range(GROUPS):
                    add_bias(p * GROUPS + gg, (gg + 1) % 2, 2 * p + (gg + 1) // 2)
            add_bias(2 * HALL, 1, HALL)


def combine(nc, k, a, wo_raw, wo_lo, xs_raw):
    with ExitStack() as mem:
        def sb(name, shape, dt=F32):
            return mem.enter_context(nc.sbuf_tensor(name, shape, dt))

        groups = [(f, min(4, KO - f)) for f in range(0, KO, 4)]
        NG = len(groups)
        BANKS = (0, 1, 2, 7, 0)
        AHEAD = 2
        LN = 5
        wo_hi = sb("wo_hi", [128, KO, D], F32R)
        cat = [sb(f"cat{g}", [T, w * 128]) for g, (f, w) in enumerate(groups)]
        catT_hi = [sb(f"catT_hi{g}", [128, w, T], F32R) for g, (f, w) in enumerate(groups)]
        catT_lo = [sb(f"catT_lo{g}", [128, w, T], F32R) for g, (f, w) in enumerate(groups)]
        x_in = sb("x_res", [T, D])
        y = sb("y_pre", [T, D])
        stats = sb("stats", [T, 2, 6])
        mean_var = sb("mean_var", [T, 2])
        rstd = sb("rstd", [T, 1])
        b_row = sb("b_out_row", [T, D])
        ps = k.ps

        wo_hi_ready = k.sem("wo_hi_ready")
        wo_lo_ready = k.sem("wo_lo_ready")
        row_loaded = k.sem("b_out_loaded")
        cat_loaded = [k.sem(f"cat_loaded{g}") for g in range(NG)]
        x_loaded = k.sem("x_res_loaded")
        cat_turned = k.sem("cat_turned")
        catT_hi_ready = k.sem("catT_hi_ready")
        catT_lo_ready = k.sem("catT_lo_ready")
        out_summed = k.sem("out_summed")
        ln_step = k.sem("ln_step")
        rstd_step = k.sem("rstd_step")
        x2_ready = k.sem("x2_ready")
        x2_scaled = k.sem("x2_scaled")
        x2_stored = k.sem("x2_stored")
        block = mem.enter_context(nc.Block())

        def turned(g):
            w = groups[g][1]
            return ps[:, BANKS[g], 0:w * T].rearrange("p (k n) -> p k n", n=T)

        @block.sync
        def _(sp):
            def load_cat(t, g):
                f, w = groups[g]
                sp.dma_start(cat[g][:, :], k.cat_d[:, bass.ds(t, 1), 1:, :].rearrange("p o h c -> p (o h c)")[
                    :, f * 128:(f + w) * 128]).then_inc(cat_loaded[g], 16)

            def load_x(t):
                sp.dma_start(x_in[:, :], a["x"][bass.ds(t * T, T), :]).then_inc(x_loaded, 16)

            for g in range(NG):
                load_cat(0, g)
            load_x(0)
            sp.dma_start(b_row[:, :], a["b_out"].rearrange("(o n) -> o n", o=1).to_broadcast([T, D])
                         ).then_inc(row_loaded, 16)
            sp.sem_inc(x2_stored, 16)
            with sp.Fori(0, NT) as t:
                after = (t + 1) % NT
                for g in range(NG):
                    sp.wait_ge(cat_turned, t * NG + g + 1)
                    load_cat(after, g)
                sp.wait_ge(ln_step, (t + 2) * LN + 2)
                load_x(after)
                sp.wait_ge(x2_ready, t + 1)
                sp.dma_start(k.x2_d[:, bass.ds(t, 1), :].rearrange("p o n -> p (o n)"), y[:, :]).then_inc(x2_stored, 16)
            sp.wait_ge(x2_stored, NT * 16 + 16)
            for g in range(NG):
                sp.wait_ge(cat_loaded[g], NT * 16 + 16)
            sp.wait_ge(x_loaded, NT * 16 + 16)

        @block.gpsimd
        def _(pool):
            with pool.Fori(0, NT) as t:
                pool.wait_ge(ln_step, (t + 2) * LN + LN)
                nc.gpsimd.tensor_tensor(rstd[:, :], mean_var[:, 1:2], k.eps[0:T, :], ALU.add).then_inc(rstd_step, 1)
                pool.wait_ge(rstd_step, 2 * t + 1)
                nc.gpsimd.tensor_tensor(rstd[:, :], rstd[:, :], k.neg_half[0:T, :], ALU.pow).then_inc(rstd_step, 1)
                hold(pool, k.held, x2_ready, t + 1)
                nc.gpsimd.tensor_tensor(xs_raw[:, bass.ds(t, 1), :].rearrange("p o n -> p (o n)"), y[:, :],
                                        k.dinv[:, bass.ds(t, 1)].to_broadcast([T, D]), ALU.mult).then_inc(x2_scaled, 1)

        @block.scalar
        def _(act):
            def high_group(t, g):
                act.wait_ge(cat_turned, t * NG + g + 1)
                nc.scalar.activation(catT_hi[g][:, :, :], turned(g), ACT.Relu).then_inc(catT_hi_ready, 1)

            for g in range(AHEAD):
                high_group(0, g)
            for f in range(KO):
                nc.scalar.activation(wo_hi[:, f, :], wo_raw[:, f, :], ACT.Copy).then_inc(wo_hi_ready, 1)
            with act.Fori(0, NT) as t:
                for g in range(NG):
                    high_group(t + (g + AHEAD) // NG, (g + AHEAD) % NG)

        @block.vector
        def _(dve):
            def low_group(t, g):
                dve.wait_ge(catT_hi_ready, t * NG + g + 1)
                nc.vector.scalar_tensor_tensor(out=catT_lo[g][:, :, :], in0=turned(g), scalar=0.0,
                                               in1=catT_hi[g][:, :, :].bitcast(F32), op0=ALU.max,
                                               op1=ALU.subtract).then_inc(catT_lo_ready, 1)

            for g in range(AHEAD):
                low_group(0, g)
            for f in range(KO):
                dve.wait_ge(wo_hi_ready, f + 1)
                split_low(nc, wo_lo[:, f, :], wo_raw[:, f, :], wo_hi[:, f, :]).then_inc(wo_lo_ready, 1)
            dve.wait_ge(row_loaded, 16)
            dve.sem_inc(ln_step, 2 * LN)
            with dve.Fori(0, NT) as t:
                for g in range(NG):
                    low_group(t + (g + AHEAD) // NG, (g + AHEAD) % NG)
                step = [0]

                def link(ins):
                    step[0] += 1
                    ins.then_inc(ln_step, 1)
                    hold(dve, k.held, ln_step, (t + 2) * LN + step[0])

                dve.wait_ge(x2_stored, t * 16 + 16)
                dve.wait_ge(x2_scaled, t + 1)
                hold(dve, k.held, out_summed, t + 1)
                link(nc.vector.tensor_tensor(y[:, :].rearrange("p (s n) -> p s n", s=2),
                                             ps[0:T, bass.ds(3 + 2 * (t % 2), 2), 0:384],
                                             b_row[:, :].rearrange("p (s n) -> p s n", s=2), ALU.add))
                dve.wait_ge(x_loaded, 16 * t + 16)
                link(nc.vector.scalar_tensor_tensor(out=y[:, :], in0=y[:, :], scalar=0.0, in1=x_in[:, :], op0=ALU.max,
                                                    op1=ALU.add))
                link(nc.vector.bn_stats(stats[:, 0, :], y[:, 0:384]))
                link(nc.vector.bn_stats(stats[:, 1, :], y[:, 384:768]))
                link(nc.vector.bn_aggr(mean_var[:, :], stats[:, :, :]))
                dve.wait_ge(rstd_step, 2 * t + 2)
                nc.vector.tensor_scalar(y[:, :], y[:, :], mean_var[:, 0:1], rstd[:, :], ALU.subtract, ALU.mult
                                        ).then_inc(x2_ready, 1)

        @block.tensor
        def _(pe):
            pe.sem_inc(x2_scaled, 1)

            def turn_group(t, g):
                f, w = groups[g]
                pe.wait_ge(cat_loaded[g], 16 * t + 16)
                for j in range(w):
                    last = nc.tensor.transpose(ps[:, BANKS[g], j * T:(j + 1) * T], cat[g][:, j * 128:(j + 1) * 128],
                                               k.ident[0:T, 0:T])
                last.then_inc(cat_turned, 1)

            for g in range(AHEAD):
                turn_group(0, g)
            with pe.Fori(0, NT) as t:
                pe.wait_ge(ln_step, t * LN + 1)
                for g, (f0, w) in enumerate(groups):
                    ahead = g + AHEAD
                    if ahead == NG:
                        pe.wait_ge(catT_lo_ready, t * NG + NG)
                    turn_group(t + ahead // NG, ahead % NG)
                    pe.wait_ge(catT_lo_ready, t * NG + g + 1)
                    pe.wait_ge(wo_lo_ready, f0 + w)
                    for f in range(w):
                        for s in range(2):
                            cols = slice(s * 384, (s + 1) * 384)
                            last = three_passes(nc, ps[0:T, bass.ds(3 + s + 2 * (t % 2), 1), 0:384].rearrange(
                                "p o n -> p (o n)"), (catT_hi[g][:, f, :], catT_lo[g][:, f, :]),
                                (wo_hi[:, f0 + f, cols], wo_lo[:, f0 + f, cols]), f0 + f == 0, f0 + f == KO - 1)
                last.then_inc(out_summed, 1)


def convolve(nc, k, a, count_T, xs_raw, out):
    with ExitStack() as mem:
        def sb(name, shape, dt=F32):
            return mem.enter_context(nc.sbuf_tensor(name, shape, dt))

        P = 2 * T
        BANKS = KF // 2
        LN = 3
        xs_hi = sb("xs_hi", [T, NT, D], F32R)
        xs_lo = sb("xs_lo", [T, NT, D], F32R)
        w_raw, w_lo = raw_and_low(nc, mem, "gcn_w", KF)
        w_hi = sb("gcn_w_hi", [128, KF, D], F32R)
        agg_hi = sb("agg_hi", [128, KF, P], F32R)
        agg_lo = sb("agg_lo", [128, KF, P], F32R)
        chunk = sb("count_chunk", [T, NT, 2 * P], F32R)
        x2 = [sb(f"x2_in{j}", [T, D]) for j in range(2)]
        y = [sb(f"y_gcn{j}", [T, D]) for j in range(2)]
        b_rows = sb("gcn_b_rows", [T, 2, D])
        stats = [sb(f"gcn_stats{j}", [T, 2, 6]) for j in range(2)]
        mean_var = [sb(f"gcn_mean_var{j}", [T, 2]) for j in range(2)]
        rstd = [sb(f"gcn_rstd{j}", [T, 1]) for j in range(2)]
        ps = k.ps
        summed = ps[:, 0:BANKS, :].rearrange("p b (m n) -> p (b m) n", m=2)

        w_loaded = [k.sem(f"gcn_w_loaded{part}") for part in range(PARTS)]
        w_hi_ready = k.sem("gcn_w_hi_ready")
        w_lo_ready = k.sem("gcn_w_lo_ready")
        rows_loaded = k.sem("gcn_rows_loaded")
        xs_hi_ready = k.sem("xs_hi_ready")
        xs_lo_ready = k.sem("xs_lo_ready")
        chunk_ready = k.sem("chunk_ready")
        agg_summed = k.sem("agg_summed")
        agg_hi_ready = k.sem("agg_hi_ready")
        agg_lo_ready = k.sem("agg_lo_ready")
        gcn_summed = k.sem("gcn_summed")
        y_ready = k.sem("y_ready")
        xs_next = k.sem("xs_next")
        x2_loaded = [k.sem(f"x2_loaded{j}") for j in range(2)]
        x2_biased = k.sem("x2_biased")
        ln_step = k.sem("gcn_ln_step")
        rstd_step = k.sem("gcn_rstd_step")
        result_ready = k.sem("result_ready")
        out_stored = [k.sem(f"out_stored{j}") for j in range(2)]
        part_k = KF // PARTS
        block = mem.enter_context(nc.Block())

        @block.sync
        def _(sp):
            def load_weights(w):
                for part in range(PARTS):
                    sp.dma_start(w_raw[:, part * part_k:(part + 1) * part_k, :],
                                 w[part * part_k * 128:(part + 1) * part_k * 128, :].rearrange("(k p) n -> p k n", p=128)
                                 ).then_inc(w_loaded[part], 16)

            def load_x2(c, j):
                sp.dma_start(x2[j][:, :], k.x2_d[:, bass.ds(2 * c + j, 1), :].rearrange("p o n -> p (o n)")
                             ).then_inc(x2_loaded[j], 16)

            load_weights(a["W1"])
            for n, b in enumerate((a["b1"], a["b2"])):
                sp.dma_start(b_rows[:, n, :], b.rearrange("(o n) -> o n", o=1).to_broadcast([T, D])
                             ).then_inc(rows_loaded, 16)
            for j in range(2):
                load_x2(0, j)
                sp.sem_inc(out_stored[j], 16)
            sp.wait_ge(gcn_summed, NT)
            load_weights(a["W2"])
            with sp.Fori(0, PAIRS) as c:
                for j in range(2):
                    sp.wait_ge(y_ready, NT + 2 * c + 2 + j + 1)
                    load_x2((c + 1) % PAIRS, j)
                for j in range(2):
                    sp.wait_ge(result_ready, 2 * c + j + 1)
                    sp.dma_start(out[bass.ds(P * c + j * T, T), :], y[j][:, :]).then_inc(out_stored[j], 16)
            for j in range(2):
                sp.wait_ge(out_stored[j], 16 * PAIRS + 16)
                sp.wait_ge(x2_loaded[j], 16 * PAIRS + 16)

        @block.gpsimd
        def _(pool):
            def widen(n):
                hold(pool, k.held, agg_summed, BANKS * n + BANKS)
                nc.gpsimd.tensor_copy(chunk[:, :, bass.ds(P * (n % 2), P)], count_T[:, :, bass.ds(P * (n % PAIRS), P)]
                                      ).then_inc(chunk_ready, 1)

            widen(0)
            with pool.Fori(0, PAIRS) as c:
                widen(c + 1)
            pool.wait_ge(rows_loaded, 32)
            with pool.Fori(0, PAIRS) as c:
                widen(c + PAIRS + 1)
                for j in range(2):
                    pool.wait_ge(x2_loaded[j], 16 * c + 16)
                    nc.gpsimd.tensor_tensor(x2[j][:, :], x2[j][:, :], b_rows[:, 1, :], ALU.add).then_inc(x2_biased, 1)
                for j in range(2):
                    n = 2 * c + j
                    pool.wait_ge(ln_step, LN * n + LN)
                    nc.gpsimd.tensor_tensor(rstd[j][:, :], mean_var[j][:, 1:2], k.eps[0:T, :], ALU.add
                                            ).then_inc(rstd_step, 1)
                    pool.wait_ge(rstd_step, 2 * n + 1)
                    nc.gpsimd.tensor_tensor(rstd[j][:, :], rstd[j][:, :], k.neg_half[0:T, :], ALU.pow
                                            ).then_inc(rstd_step, 1)

        @block.scalar
        def _(act):
            def high_xs(t, layer):
                if layer:
                    act.wait_ge(xs_next, t + 3)
                nc.scalar.activation(xs_hi[:, t, :], xs_raw[:, t, :], ACT.Copy).then_inc(xs_hi_ready, 1)

            def high_weights(layer):
                for part in range(PARTS):
                    act.wait_ge(w_loaded[part], 16 * layer + 16)
                    ks = slice(part * part_k, (part + 1) * part_k)
                    nc.scalar.activation(w_hi[:, ks, :], w_raw[:, ks, :], ACT.Copy).then_inc(w_hi_ready, 1)

            def high_agg(n):
                for b in range(BANKS):
                    ms = slice(2 * b, 2 * b + 2)
                    act.wait_ge(agg_summed, BANKS * (n + 2) + b + 1)
                    nc.scalar.activation(agg_hi[:, ms, :], summed[:, ms, 0:P], ACT.Copy).then_inc(agg_hi_ready, 1)

            def activate(c, j):
                hold(act, k.held, y_ready, 2 * c + j + 3)
                nc.scalar.activation(xs_raw[:, bass.ds(2 * c + j, 1), :].rearrange("p o n -> p (o n)"), y[j][:, :],
                                     ACT.Relu, scale=k.dinv[:, bass.ds(2 * c + j, 1)]).then_inc(xs_next, 1)

            for t in range(NT):
                high_xs(t, 0)
            high_weights(0)
            act.sem_inc(xs_next, 2)
            with act.Fori(0, PAIRS - 1) as c:
                high_agg(c)
                for j in range(2):
                    activate(c, j)
            high_agg(PAIRS - 1)
            for t in range(NT - 2):
                high_xs(t, 1)
            for j in range(2):
                activate(PAIRS - 1, j)
                high_xs(NT - 2 + j, 1)
            high_weights(1)
            with act.Fori(PAIRS, 2 * PAIRS) as n:
                high_agg(n)

        @block.vector
        def _(dve):
            def low_xs(t, layer):
                dve.wait_ge(xs_hi_ready, layer * NT + t + 1)
                split_low(nc, xs_lo[:, t, :], xs_raw[:, t, :], xs_hi[:, t, :]).then_inc(xs_lo_ready, 1)

            def low_weights(layer):
                for part in range(PARTS):
                    dve.wait_ge(w_hi_ready, PARTS * layer + part + 1)
                    ks = slice(part * part_k, (part + 1) * part_k)
                    split_low(nc, w_lo[:, ks, :], w_raw[:, ks, :], w_hi[:, ks, :]).then_inc(w_lo_ready, 1)

            def low_agg(n):
                for b in range(BANKS):
                    ms = slice(2 * b, 2 * b + 2)
                    dve.wait_ge(agg_hi_ready, BANKS * n + b + 1)
                    split_low(nc, agg_lo[:, ms, :], summed[:, ms, 0:P], agg_hi[:, ms, :]).then_inc(agg_lo_ready, 1)

            def halves(x):
                return x.rearrange("p (s n) -> p s n", s=2)

            def add_row(n, t, j, row):
                hold(dve, k.held, gcn_summed, n + 1)
                nc.vector.scalar_tensor_tensor(
                    out=halves(y[j][:, :]), in0=ps[0:T, 3 + 2 * j:5 + 2 * j, 0:384], scalar=k.dinv[:, bass.ds(t, 1)],
                    in1=halves(row), op0=ALU.mult, op1=ALU.add).then_inc(y_ready, 1)

            def add_first(c, j):
                dve.wait_ge(xs_next, 2 * c + j + 1)
                add_row(2 * c + j, 2 * c + j, j, b_rows[:, 0, :])

            dve.sem_inc(y_ready, 2)
            for t in range(NT):
                low_xs(t, 0)
            low_weights(0)
            dve.wait_ge(rows_loaded, 32)
            with dve.Fori(0, PAIRS - 1) as c:
                low_agg(c)
                for j in range(2):
                    add_first(c, j)
            low_agg(PAIRS - 1)
            for t in range(NT - 4):
                low_xs(t, 1)
            add_first(PAIRS - 1, 0)
            for t in (NT - 4, NT - 3):
                low_xs(t, 1)
            add_first(PAIRS - 1, 1)
            for t in (NT - 2, NT - 1):
                low_xs(t, 1)
            low_weights(1)
            with dve.Fori(0, PAIRS) as c:
                low_agg(c + PAIRS)
                for j in range(2):
                    n = 2 * c + j
                    dve.wait_ge(out_stored[j], 16 * c + 16)
                    dve.wait_ge(x2_biased, n + 1)
                    add_row(n + NT, n, j, x2[j][:, :])
                    hold(dve, k.held, y_ready, n + NT + 3)
                    for s in range(2):
                        nc.vector.bn_stats(stats[j][:, s, :], y[j][:, s * 384:(s + 1) * 384]).then_inc(ln_step, 1)
                    hold(dve, k.held, ln_step, LN * n + 2)
                    nc.vector.bn_aggr(mean_var[j][:, :], stats[j][:, :, :]).then_inc(ln_step, 1)
                    dve.wait_ge(rstd_step, 2 * n + 2)
                    nc.vector.tensor_scalar(y[j][:, :], y[j][:, :], mean_var[j][:, 0:1], rstd[j][:, :],
                                            ALU.subtract, ALU.mult).then_inc(result_ready, 1)

        @block.tensor
        def _(pe):
            pe.sem_inc(agg_summed, 2 * BANKS)

            def turn(n, layer):
                pe.wait_ge(chunk_ready, n + 1)
                for m in range(KF):
                    cols = slice(m * 128, (m + 1) * 128)
                    for s in range(NT):
                        if m == 0:
                            pe.wait_ge(xs_lo_ready, layer * NT + s + 1)
                        counts_of = chunk[:, s, bass.ds(P * (n % 2), P)]
                        nc.tensor.matmul(summed[:, m, 0:P], xs_hi[:, s, cols], counts_of, start=s == 0, stop=False)
                        last = nc.tensor.matmul(summed[:, m, 0:P], xs_lo[:, s, cols], counts_of, start=False,
                                                stop=s == NT - 1)
                    if m % 2 == 1:
                        last.then_inc(agg_summed, 1)
                for j in range(2):
                    nodes = slice(j * T, (j + 1) * T)
                    pe.wait_ge(y_ready, 2 * n + j + 1)
                    for f in range(KF):
                        if j == 0 and f % 2 == 0:
                            pe.wait_ge(agg_lo_ready, BANKS * n + f // 2 + 1)
                            pe.wait_ge(w_lo_ready, PARTS * layer + f // part_k + 1)
                        for s in range(2):
                            cols = slice(s * 384, (s + 1) * 384)
                            last = three_passes(nc, ps[0:T, 3 + 2 * j + s, 0:384],
                                                (agg_hi[:, f, nodes], agg_lo[:, f, nodes]),
                                                (w_hi[:, f, cols], w_lo[:, f, cols]), f == 0, f == KF - 1)
                    last.then_inc(gcn_summed, 1)

            for layer in range(2):
                with pe.Fori(layer * PAIRS, (layer + 1) * PAIRS) as n:
                    turn(n, layer)


def program(nc, a, out, stages=6):
    with ExitStack() as ctx:
        k = Core(nc, ctx)

        def sb(name, shape, dt=F32, stack=ctx):
            return stack.enter_context(nc.sbuf_tensor(name, shape, dt))

        k.held = k.sem("held")
        k.ps = ctx.enter_context(nc.psum_tensor("ps", [128, 8, 512], F32))
        k.ident = sb("ident", [128, 128])
        k.zeros = sb("zeros", [128, SW], BF16)
        k.far = sb("far", [128, 1])
        k.eps = sb("eps", [128, 1])
        k.neg_half = sb("neg_half", [128, 1])
        k.deg = sb("deg", [T, NT])
        k.dinv = sb("dinv", [T, NT])
        k.src_term = sb("src_term", [T, HALL, NT])
        k.src_drop = sb("src_drop", [T, HALL, NT])
        k.w_att = sb("w_att", [128, LAYERS * KF, 2 * HEADS])
        k.ranges_row = sb("ranges_row", [1, 2 * NT], I32)
        k.h_d = k.dram("h_d", (T, HALL, NT, C))
        k.src_row_d = k.dram("src_row_d", (TERMS, N))
        k.lift_d = k.dram("lift_d", (2 * HALL, N))
        k.cat_d = k.dram("cat_d", (T, NT, HALL + 1, C))
        k.x2_d = k.dram("x2_d", (T, NT, D))
        count_T = sb("count_T", [T, NT, N], U16)
        with ExitStack() as early:
            k.x1_hi = sb("x1_hi", [128, KF, N], F32R, early)
            k.x1_lo = sb("x1_lo", [128, KF, N], F32R, early)
            with ExitStack() as edges:
                k.loop_strip = sb("loop_strip", [T, 2 * N + 2], BF16, edges)
                k.iota_i = sb("iota_i", [128, 3 * SW], I32, edges)
                k.iota_h = sb("iota_h", [128, 3 * SW], F16, edges)
                k.src_col = sb("src_col", [128, CCOLS], F32, edges)
                k.dst_col = sb("dst_col", [128, CCOLS], F32, edges)
                nodes_in(nc, k, a)
                k.no_edge = early.enter_context(nc.sbuf_tensor("no_edge", [T, NT, 3 * SW], BF16, side="right"))
                if stages >= 2:
                    counts(nc, k, a, count_T)
            if stages >= 3:
                heads_in(nc, k, a)
        with ExitStack() as weights:
            xs_raw = sb("xs_raw", [T, NT, D])
            wo_raw, wo_lo = raw_and_low(nc, weights, "wo", KO)
            if stages >= 4:
                attend(nc, k, a, count_T, wo_raw)
            if stages >= 5:
                combine(nc, k, a, wo_raw, wo_lo, xs_raw)
        if stages >= 6:
            convolve(nc, k, a, count_T, xs_raw, out)
        return k


def kernel(**inputs):
    import numpy as np
    import concourse.bacc as bacc
    from concourse.bass_utils import run_bass_kernel_spmd

    given = {n: np.asarray(v) for n, v in inputs.items()}
    gat = "L0_gnn_"
    turned = np.stack([given[f"{gat}W{i}"].T.reshape(KF, 128, KF // WP, WP * 128).transpose(2, 1, 0, 3)
                       for i in range(LAYERS)]).reshape(LAYERS * KF // WP, 128, KF, WP * 128)
    att = np.zeros((LAYERS, D, 2 * HEADS), np.float32)
    for i in range(LAYERS):
        for h in range(HEADS):
            att[i, h * C:(h + 1) * C, h] = given[f"{gat}a_src{i}"][h]
            att[i, h * C:(h + 1) * C, HEADS + h] = given[f"{gat}a_dst{i}"][h]
    arrays = {
        "x": given["x"], "src": given["src"], "dst": given["dst"],
        "W_ah": given[gat + "W_ah"], "b_ah_cols": given[gat + "b_ah"].reshape(KF, 128).T,
        "W_gat": np.stack([given[f"{gat}W{i}"] for i in range(LAYERS)]),
        "W_gat_turned": turned, "att": att.reshape(LAYERS, KF, 128, 2 * HEADS).transpose(2, 0, 1, 3),
        "b_gat": np.concatenate([given[f"{gat}b{i}"] for i in range(LAYERS)]),
        "W_out": given[gat + "W_out"], "b_out": given[gat + "b_out"],
        "W1": given["L1_gnn_W1"], "b1": given["L1_gnn_b1"],
        "W2": given["L1_gnn_W2"], "b2": given["L1_gnn_b2"],
    }
    nc = bacc.Bacc("TRN2", target_bir_lowering=False, num_devices=1)
    aps = {}
    for name, value in arrays.items():
        arrays[name] = np.ascontiguousarray(value)
        aps[name] = nc.dram_tensor(name, value.shape, mybir.dt.from_np(value.dtype), kind="ExternalInput").ap()
    out = nc.dram_tensor("out", (N, D), F32, kind="ExternalOutput").ap()
    program(nc, aps, out)
    return run_bass_kernel_spmd(nc, [arrays], core_ids=[0]).results[0]["out"]
```

```python
from contextlib import ExitStack

import concourse.bass as bass
from concourse import mybir

F32 = mybir.dt.float32
F32R = mybir.dt.float32r
BF16 = mybir.dt.bfloat16
F16 = mybir.dt.float16
I32 = mybir.dt.int32
U16 = mybir.dt.uint16
ALU = mybir.AluOpType
ACT = mybir.ActivationFunctionType
AX_X = mybir.AxisListType.X

N = 1250
T = 125
NT = N // T
PAIRS = NT // 2
D = 768
KF = D // 128
LAYERS = 3
HEADS = 4
C = D // HEADS
HALL = LAYERS * HEADS
TERMS = 2 * HALL
PARTS = KF
KO = LAYERS * D // 128
E = 41250
CHUNKS = -(-E // 128)
FULL = E // 128
CROWS = 3
CCOLS = CROWS * 128
PAD_NODE = 2000
CSTEP = 3
HOTS = 4
SW = 417
FAR = 1e30
NO_MAX = -3e38
EXP_CAP = 1e30
SLOPE = 0.2
EXACT = 4096
LN_EPS = 1e-5
HALF = N // 2
GT = NT // 2
RING = 4


def three_passes(nc, out, lhs, rhs, first, last):
    nc.tensor.matmul(out, lhs[0], rhs[0], start=first, stop=False)
    nc.tensor.matmul(out, lhs[0], rhs[1], start=False, stop=False)
    return nc.tensor.matmul(out, lhs[1], rhs[0], start=False, stop=last)


def hold(eng, held, semaphore, value):
    eng.wait_ge(semaphore, value)
    eng.sem_inc(held, 1)


class Core:

    def __init__(self, nc, ctx):
        self.nc, self.ctx = nc, ctx

    def sem(self, name):
        return self.ctx.enter_context(self.nc.semaphore(name))

    def dram(self, name, shape, dt=F32):
        return self.nc.dram_tensor(name, shape, dt, kind="Internal").ap()



def split_low(nc, out, whole, high):
    return nc.vector.tensor_tensor(out, whole, high.bitcast(F32), ALU.subtract)


def raw_and_low(nc, mem, name, feature_tiles):
    raw = mem.enter_context(nc.sbuf_tensor(f"{name}_raw", [128, feature_tiles, D], F32))
    low = nc.alloc_sbuf_tensor_at(f"{name}_lo", [128, feature_tiles, D], F32R,
                                  offset=nc.sbuf_base - feature_tiles * D * 4)
    return raw, low


def nodes_in(nc, k, a):
    with ExitStack() as mem:
        def sb(name, shape, dt=F32):
            return mem.enter_context(nc.sbuf_tensor(name, shape, dt))

        ones = sb("ones", [128, NT])
        tile_lo_i = sb("tile_lo_i", [NT, 1], I32)
        tile_lo = sb("tile_lo", [NT, 2])
        chunk_no = sb("chunk_no", [NT, 2, CCOLS])
        edge_i = sb("edge_i", [128, 2, CROWS, 128], I32)
        edge_f = sb("edge_f", [128, 2, CROWS, 128])
        span = sb("span", [128, 2, CROWS])
        span_diag = sb("span_diag", [128, 2, CROWS, 128])
        meets = sb("meets", [NT, 2, CCOLS])
        ranges = sb("ranges", [NT, 3])
        ranges_i = sb("ranges_i", [NT, 3], I32)
        w_raw = k.w_raw
        w_hi = sb("wah_hi", [128, KF, D], F32R)
        w_lo = sb("wah_lo", [128, KF, D], F32R)
        bias = sb("bah_col", [128, KF])
        x_in = sb("x_in", [T, 2, D])
        xT_hi = sb("xT_hi", [128, KF, 4 * T], F32R)
        xT_lo = sb("xT_lo", [128, KF, 4 * T], F32R)
        x1 = sb("x1_pair", [128, KF, 2 * T])
        ps = k.ps

        pads_set = k.sem("pads_set")
        fills = k.sem("fills")
        iota_ready = k.sem("iota_ready")
        consts_ready = k.sem("consts_ready")
        edges_loaded = k.sem("edges_loaded")
        weights_loaded = [k.sem(f"weights_loaded{f}") for f in range(KF)]
        bias_loaded = k.sem("bias_loaded")
        x_loaded = k.sem("x_loaded")
        vec_step = k.sem("vec_step")
        edges_float = k.sem("edges_float")
        edges_turned = k.sem("edges_turned")
        edges_taken = k.sem("edges_taken")
        diag_ready = k.sem("diag_ready")
        span_spread = k.sem("span_spread")
        ranges_ready = k.sem("ranges_ready")
        ranges_moved = k.sem("ranges_moved")
        wah_hi_ready = k.sem("wah_hi_ready")
        wah_lo_ready = k.sem("wah_lo_ready")
        x_turned = k.sem("x_turned")
        xT_hi_ready = k.sem("xT_hi_ready")
        xT_lo_ready = k.sem("xT_lo_ready")
        x1_summed = k.sem("x1_summed")
        x1_copied = k.sem("x1_copied")
        x1_lo_ready = k.sem("x1_lo_ready")

        turned = ps[:, 3:6, 0:4 * T]
        summed = ps[:, 0:3, :].rearrange("p b (m n) -> p (b m) n", m=2)

        block = mem.enter_context(nc.Block())
        x_pairs = a["x"].rearrange("(i j p) f -> p i j f", j=2, p=T)

        def slot(x, i):
            return x[:, :, bass.ds(2 * T * (i % 2), 2 * T)].rearrange("p (b k) n -> p b k n", k=2)

        def load_pair(sp, i):
            sp.dma_start(x_in[:, :, :], x_pairs[:, bass.ds(i, 1), :, :].rearrange("p i j f -> p (i j) f")
                         ).then_inc(x_loaded, 16)

        @block.sync
        def _(sp):
            load_pair(sp, 0)
            sp.wait_ge(pads_set, 1)
            for which, arr in ((0, a["src"]), (1, a["dst"])):
                rows = arr[0:FULL * 128].rearrange("(r f) -> r f", f=128)
                sp.dma_start(edge_i[:, which, 0:2, :],
                             rows[0:256, :].rearrange("(c p) f -> p c f", p=128)).then_inc(edges_loaded, 16)
                sp.dma_start(edge_i[0:FULL - 256, which, 2, :], rows[256:FULL, :]).then_inc(edges_loaded, 16)
                sp.dma_start(edge_i[FULL - 256:FULL - 255, which, 2, 0:E - FULL * 128],
                             arr[FULL * 128:E].rearrange("(r f) -> r f", r=1)).then_inc(edges_loaded, 16)
            with sp.Fori(1, PAIRS) as i:
                sp.wait_ge(x_turned, i)
                load_pair(sp, i)
            sp.wait_ge(ranges_ready, 1)
            for n in range(3):
                sp.dma_start(k.ranges_row[0:1, n * NT:(n + 1) * NT], ranges_i[:, n:n + 1]).then_inc(ranges_moved, 16)
            sp.wait_ge(ranges_moved, 48)

        @block.gpsimd
        def _(pool):
            nc.gpsimd.memset(edge_i[:, :, :, :], PAD_NODE).then_inc(pads_set, 1)
            nc.gpsimd.memset(k.ident[:, :], 0.0).then_inc(fills, 1)
            pool.wait_ge(fills, 1)
            nc.gpsimd.affine_select(out=k.ident[:, :], in_=k.ident[:, :], compare_op=ALU.not_equal, fill=1.0, base=0,
                                    pattern=[[-1, 128]], channel_multiplier=1).then_inc(consts_ready, 1)
            nc.gpsimd.memset(ones[:, :], 1.0).then_inc(consts_ready, 1)
            nc.gpsimd.iota(k.iota_i[:, :], pattern=[[1, 3 * SW]], base=0, channel_multiplier=0).then_inc(iota_ready, 1)
            nc.gpsimd.iota(tile_lo_i[:, :], pattern=[[0, 1]], base=0, channel_multiplier=T).then_inc(iota_ready, 1)
            nc.gpsimd.memset(k.loop_strip[:, :], 0.0).then_inc(fills, 1)
            pool.wait_ge(fills, 2)
            nc.gpsimd.affine_select(out=k.loop_strip[:, N:N + T], in_=k.loop_strip[:, N:N + T],
                                    compare_op=ALU.not_equal, fill=1.0, base=0, pattern=[[-1, T]],
                                    channel_multiplier=1)
            nc.gpsimd.memset(k.zeros[:, :], 0.0)
            nc.gpsimd.memset(k.far[:, :], FAR)
            nc.gpsimd.memset(k.eps[:, :], LN_EPS)
            nc.gpsimd.memset(k.neg_half[:, :], -0.5)

        @block.vector
        def _(dve):
            done = [0]

            def link(ins):
                done[0] += 1
                ins.then_inc(vec_step, 1)
                dve.wait_ge(vec_step, done[0])

            def split_x(i):
                dve.wait_ge(xT_hi_ready, i + 1)
                nc.vector.tensor_tensor(slot(xT_lo, i), turned.rearrange("p b (k n) -> p b k n", k=2),
                                        slot(xT_hi, i).bitcast(F32), ALU.subtract).then_inc(xT_lo_ready, 1)

            def split_x1(i):
                dve.wait_ge(x1_copied, (i + 2) * KF)
                nc.vector.tensor_tensor(k.x1_lo[:, :, bass.ds(2 * T * i, 2 * T)], x1[:, :, :],
                                        k.x1_hi[:, :, bass.ds(2 * T * i, 2 * T)].bitcast(F32),
                                        ALU.subtract).then_inc(x1_lo_ready, 1)

            split_x(0)
            for m in range(KF):
                cols = slice(m * 128, (m + 1) * 128)
                dve.wait_ge(wah_hi_ready, m + 1)
                split_low(nc, w_lo[:, :, cols], w_raw[:, :, cols], w_hi[:, :, cols]).then_inc(wah_lo_ready, 1)
            split_x(1)
            dve.wait_ge(edges_loaded, 96)
            nc.vector.tensor_copy(edge_f[:, :, :, :], edge_i[:, :, :, :]).then_inc(edges_float, 1)
            dve.wait_ge(edges_float, 1)
            link(nc.vector.tensor_reduce(span[:, 0, :], edge_f[:, 1, :, :], op=ALU.min, axis=AX_X))
            link(nc.vector.tensor_reduce(span[:, 1, :], edge_f[:, 1, :, :], op=ALU.max, axis=AX_X))
            dve.wait_ge(consts_ready, 2)
            for n in range(2):
                for c in range(CROWS):
                    last = nc.vector.tensor_scalar(span_diag[:, n, c, :], k.ident[:, :], span[:, n, c:c + 1], None,
                                                   ALU.mult)
            last.then_inc(diag_ready, 1)
            dve.wait_ge(iota_ready, 2)
            nc.vector.tensor_copy(k.iota_h[:, :], k.iota_i[:, :])
            link(nc.vector.tensor_copy(tile_lo[:, 0:1], tile_lo_i[:, :]))
            nc.vector.tensor_scalar(tile_lo[:, 1:2], tile_lo[:, 0:1], float(T), None, ALU.add)
            link(nc.vector.tensor_copy(chunk_no[:, 0, :], k.iota_i[0:NT, 0:CCOLS]))
            link(nc.vector.tensor_scalar(chunk_no[:, 1, :], chunk_no[:, 0, :], -1.0, CCOLS - 1.0, ALU.mult, ALU.add))
            dve.wait_ge(edges_turned, 1)
            nc.vector.tensor_copy(k.src_col[:, :], ps[:, 6, 0:CCOLS])
            nc.vector.tensor_copy(k.dst_col[:, :], ps[:, 7, 0:CCOLS]).then_inc(edges_taken, 1)
            split_x1(0)
            split_x(2)
            split_x1(1)
            dve.wait_ge(span_spread, 1)
            link(nc.vector.tensor_scalar(meets[:, 0, :], ps[0:NT, 6, 0:CCOLS], tile_lo[:, 1:2], None, ALU.is_lt))
            link(nc.vector.scalar_tensor_tensor(out=meets[:, 0, :], in0=ps[0:NT, 7, 0:CCOLS], scalar=tile_lo[:, 0:1],
                                                in1=meets[:, 0, :], op0=ALU.is_ge, op1=ALU.mult))
            link(nc.vector.tensor_tensor(meets[:, 1, :], meets[:, 0, :], chunk_no[:, 1, :], ALU.mult))
            link(nc.vector.tensor_tensor(meets[:, 0, :], meets[:, 0, :], chunk_no[:, 0, :], ALU.mult))
            link(nc.vector.tensor_reduce(ranges[:, 0:1], meets[:, 1, :], op=ALU.max, axis=AX_X))
            link(nc.vector.tensor_reduce(ranges[:, 1:2], meets[:, 0, :], op=ALU.max, axis=AX_X))
            link(nc.vector.tensor_scalar(ranges[:, 0:1], ranges[:, 0:1], -1.0, CCOLS - 1.0, ALU.mult, ALU.add))
            link(nc.vector.tensor_scalar(ranges[:, 0:1], ranges[:, 0:1], float(CHUNKS - 1), None, ALU.min))
            link(nc.vector.tensor_tensor(ranges[:, 1:2], ranges[:, 1:2], ranges[:, 0:1], ALU.max))
            link(nc.vector.tensor_scalar(ranges[:, 1:2], ranges[:, 1:2], 1.0, None, ALU.add))
            link(nc.vector.tensor_tensor(ranges[:, 2:3], ranges[:, 1:2], ranges[:, 0:1], ALU.subtract))
            nc.vector.tensor_copy(ranges_i[:, :], ranges[:, :]).then_inc(ranges_ready, 1)
            with dve.Fori(2, PAIRS - 1) as i:
                split_x(i + 1)
                split_x1(i)
            split_x1(PAIRS - 1)

        @block.tensor
        def _(pe):
            def turn_x(i):
                pe.wait_ge(x_loaded, (i + 1) * 16)
                for f in range(KF):
                    for j in range(2):
                        at = (f % 2) * 2 * T + j * T
                        last = nc.tensor.transpose(ps[:, 3 + f // 2, at:at + T], x_in[:, j, f * 128:(f + 1) * 128],
                                                   k.ident[0:T, 0:T])
                last.then_inc(x_turned, 1)

            pe.wait_ge(consts_ready, 2)
            turn_x(0)

            def multiply(i, first=False):
                pair = bass.ds(2 * T * (i % 2), 2 * T)
                for m in range(KF):
                    cols = slice(m * 128, (m + 1) * 128)
                    if m % 2 == 0:
                        pe.wait_ge(x1_copied, i * KF + m + 2)
                    if first:
                        pe.wait_ge(wah_lo_ready, m + 1)
                        if m == KF // 2:
                            turn_x(i + 1)
                    for f in range(KF):
                        last = three_passes(nc, summed[:, m, 0:2 * T], (w_hi[:, f, cols], w_lo[:, f, cols]),
                                            (xT_hi[:, f, pair], xT_lo[:, f, pair]), f == 0, f == KF - 1)
                    last.then_inc(x1_summed, 1)

            pe.sem_inc(x1_copied, KF)

            def turn_next_and_multiply(i):
                pe.wait_ge(xT_lo_ready, i + 1)
                turn_x(i + 1)
                multiply(i)

            pe.wait_ge(xT_lo_ready, 1)
            multiply(0, first=True)
            pe.wait_ge(edges_float, 1)
            for n in range(2):
                for c in range(CROWS):
                    last = nc.tensor.transpose(ps[:, 6 + n, c * 128:(c + 1) * 128], edge_f[:, n, c, :], k.ident[:, :])
            last.then_inc(edges_turned, 1)
            turn_next_and_multiply(1)
            pe.wait_ge(diag_ready, 1)
            pe.wait_ge(edges_taken, 1)
            for n in range(2):
                for c in range(CROWS):
                    last = nc.tensor.matmul(ps[0:NT, 6 + n, c * 128:(c + 1) * 128], ones[:, :], span_diag[:, n, c, :],
                                            start=True, stop=True)
            last.then_inc(span_spread, 1)
            with pe.Fori(2, PAIRS - 1) as i:
                turn_next_and_multiply(i)
            pe.wait_ge(xT_lo_ready, PAIRS)
            multiply(PAIRS - 1)

        @block.scalar
        def _(act):
            for m in range(KF):
                cols = slice(m * 128, (m + 1) * 128)
                act.dma_start(w_raw[:, :, cols], a["W_ah"].rearrange("(k p) n -> p k n", p=128)[:, :, cols]
                              ).then_inc(weights_loaded[m], 16)
            act.dma_start(bias[:, :], a["b_ah_cols"]).then_inc(bias_loaded, 16)

            def high_x(i):
                hold(act, k.held, x_turned, i + 1)
                nc.scalar.activation(slot(xT_hi, i), turned.rearrange("p b (k n) -> p b k n", k=2), ACT.Copy
                                     ).then_inc(xT_hi_ready, 1)

            high_x(0)
            for m in range(KF):
                cols = slice(m * 128, (m + 1) * 128)
                act.wait_ge(weights_loaded[m], 16)
                nc.scalar.activation(w_hi[:, :, cols], w_raw[:, :, cols], ACT.Copy).then_inc(wah_hi_ready, 1)
            act.wait_ge(bias_loaded, 16)

            def take_x1(i):
                for m in range(KF):
                    if m % 2 == 0:
                        act.wait_ge(x1_summed, i * KF + m + 2)
                    if m == 0:
                        act.wait_ge(x1_lo_ready, i + 1)
                    nc.scalar.activation(x1[:, m, :], summed[:, m, 0:2 * T], ACT.Relu, bias=bias[:, m:m + 1])
                    nc.scalar.activation(k.x1_hi[:, m, bass.ds(2 * T * i, 2 * T)], summed[:, m, 0:2 * T], ACT.Relu,
                                         bias=bias[:, m:m + 1]).then_inc(x1_copied, 1)

            act.sem_inc(x1_lo_ready, 1)
            with act.Fori(0, PAIRS - 1) as i:
                high_x(i + 1)
                take_x1(i)
            take_x1(PAIRS - 1)


def counts(nc, k, a, count_T):
    with ExitStack() as mem:
        def sb(name, shape, dt=F32):
            return mem.enter_context(nc.sbuf_tensor(name, shape, dt))

        src_hot = sb("src_hot", [128, HOTS, CSTEP, 3 * SW], BF16)
        dst_hot = sb("dst_hot", [128, HOTS, CSTEP, T], BF16)
        count_tile = sb("count_tile", [T, 2, 3, SW])
        att = sb("att_spread", [128, 2, D])
        weighted = sb("weighted", [128, 2, 2, D])
        root = sb("root", [T, NT])
        ps = k.ps
        acc = ps[0:T, 0:6, 0:SW]

        hots_ready = k.sem("hots_ready")
        hots_used = k.sem("hots_used")
        counts_summed = k.sem("counts_summed")
        counts_copied = k.sem("counts_copied")
        no_edge_ready = k.sem("no_edge_ready")
        counts_turned = k.sem("counts_turned")
        turned_copied = k.sem("turned_copied")
        deg_root = k.sem("deg_root")
        layer_loaded = k.sem("layer_loaded")
        weighted_ready = k.sem("weighted_ready")
        weighted_summed = k.sem("weighted_summed")
        most = NT * (CHUNKS // CSTEP + 2)
        GROUPS = ((0, 4, 6), (4, 4, 7), (8, 2, 6))

        block = mem.enter_context(nc.Block())

        def ring_slot(eng, n):
            return eng.snap((n - 1) % HOTS, min_val=0, max_val=HOTS - 1)

        @block.sync
        def _(sp):
            for n, l in enumerate(reversed(range(LAYERS))):
                if n:
                    sp.wait_ge(weighted_ready, KF * n)
                sp.dma_start(k.w_raw[:, :, :], a["W_gat"][l, :, :].rearrange("(k p) n -> p k n", p=128)
                             ).then_inc(layer_loaded, 16)
                sp.dma_start(att[:, :, :], a["att_rows"][l:l + 1, :, :].to_broadcast([128, 2, D])
                             ).then_inc(layer_loaded, 16)

        @block.gpsimd
        def _(pool):
            pool.sem_inc(weighted_summed, 2)
            with pool.Fori(0, LAYERS) as n:
                pool.wait_ge(layer_loaded, 32 * n + 32)
                for f in range(KF):
                    pool.wait_ge(weighted_summed, KF * n + f + 1)
                    nc.gpsimd.tensor_tensor(weighted[:, f % 2, :, :],
                                            k.w_raw[:, f, :].unsqueeze(1).to_broadcast([128, 2, D]), att[:, :, :],
                                            ALU.mult).then_inc(weighted_ready, 1)

        @block.vector
        def _(dve):
            made = nc.vector.alloc_register("made")
            nc.vector.reg_mov(made, 1)
            dve.sem_inc(hots_used, HOTS)
            with dve.Fori(0, NT) as t:
                first = nc.vector.value_load(k.ranges_row[0:1, bass.ds(t, 1)], min_val=0, max_val=CHUNKS)
                end = nc.vector.value_load(k.ranges_row[0:1, bass.ds(t + NT, 1)], min_val=1, max_val=CHUNKS + 1)
                tile_lo = nc.vector.snap(T * t, min_val=0, max_val=N - T)
                with dve.Fori(first, end, CSTEP) as c:
                    n = nc.vector.snap(made, min_val=1, max_val=most)
                    slot = ring_slot(nc.vector, n)
                    dve.wait_ge(hots_used, n)
                    for j in range(CSTEP):
                        nc.vector.tensor_scalar(src_hot[:, bass.ds(slot, 1), j, :].rearrange("p o n -> p (o n)"),
                                                k.iota_h[:, :], k.src_col[:, bass.ds(c + j, 1)], None, ALU.is_equal)
                    nc.vector.tensor_tensor(dst_hot[:, bass.ds(slot, 1), :, :].rearrange("p o c n -> p (o c) n"),
                                            k.iota_h[:, bass.ds(tile_lo, T)].unsqueeze(1).to_broadcast([128, CSTEP, T]),
                                            k.dst_col[:, bass.ds(c, CSTEP)].unsqueeze(2).to_broadcast([128, CSTEP, T]),
                                            ALU.is_equal).then_inc(hots_ready, 1)
                    nc.vector.reg_add(made, made, 1)
            dve.wait_ge(deg_root, 1)
            nc.vector.reciprocal(k.dinv[:, :], root[:, :])

        @block.tensor
        def _(pe):
            pe.sem_inc(counts_copied, 2)
            pe.sem_inc(turned_copied, 3)
            taken = nc.tensor.alloc_register("taken")
            nc.tensor.reg_mov(taken, 1)

            def open_tile(t, j):
                summed = acc[:, 3 * j:3 * j + 3, :]
                pe.wait_ge(counts_copied, t + 1)
                for s in range(3):
                    nc.tensor.matmul(summed[:, s, :], k.loop_strip[:, N:N + T],
                                     k.loop_strip[:, bass.ds(N - T * t + SW * s, SW)], start=True, stop=False)
                return nc.tensor.value_load(k.ranges_row[0:1, bass.ds(t + 2 * NT, 1)], min_val=1, max_val=CHUNKS)

            def sum_tile(chunks, j):
                summed = acc[:, 3 * j:3 * j + 3, :]
                with pe.Fori(0, chunks, CSTEP) as _:
                    n = nc.tensor.snap(taken, min_val=1, max_val=most)
                    slot = ring_slot(nc.tensor, n)
                    pe.wait_ge(hots_ready, n)
                    for i in range(CSTEP):
                        for s in range(3):
                            last = nc.tensor.matmul(
                                summed[:, s, :], dst_hot[:, bass.ds(slot, 1), i, :].rearrange("p o n -> p (o n)"),
                                src_hot[:, bass.ds(slot, 1), i, s * SW:(s + 1) * SW].rearrange("p o n -> p (o n)"),
                                start=False, stop=False)
                    last.then_inc(hots_used, 1)
                    nc.tensor.reg_add(taken, taken, 1)
                for s in range(3):
                    last = nc.tensor.matmul(summed[:, s, :], k.zeros[0:T, 0:T], k.zeros[0:T, :], start=False, stop=True)
                last.then_inc(counts_summed, 1)

            def turn_tile(t, j, groups):
                flat = count_tile[:, j, :, :].rearrange("p a b -> p (a b)")
                pe.wait_ge(counts_copied, t + 3)
                for g in groups:
                    s0, w, bank = GROUPS[g]
                    pe.wait_ge(turned_copied, 3 * t + (g + 1 if g < 2 else 4))
                    for s in range(w):
                        last = nc.tensor.transpose(ps[0:T, bank, s * T:(s + 1) * T],
                                                   flat[:, (s0 + s) * T:(s0 + s + 1) * T], k.ident[0:T, 0:T])
                    last.then_inc(counts_turned, 1)

            def turn_and_sum_next(t, j):
                turn_tile(t, j, (0, 1))
                chunks = open_tile(t + 2, j)
                turn_tile(t, j, (2,))
                sum_tile(chunks, j)

            sum_tile(open_tile(0, 0), 0)
            sum_tile(open_tile(1, 1), 1)
            with pe.Fori(0, NT // 2 - 1) as u:
                for j in range(2):
                    turn_and_sum_next(2 * u + j, j)
            for j in range(2):
                turn_tile(NT - 2 + j, j, (0, 1, 2))

        @block.scalar
        def _(act):
            act.sem_inc(no_edge_ready, 1)

            def take_tile(t):
                mine = count_tile[:, bass.ds(t % 2, 1), :, :].rearrange("p o a b -> p (o a) b")
                act.wait_ge(counts_summed, t + 1)
                hold(act, k.held, no_edge_ready, t + 1)
                nc.scalar.activation(mine, acc[:, bass.ds(3 * (t % 2), 3), :], ACT.Copy,
                                     accum_out=k.deg[:, bass.ds(t, 1)]).then_inc(counts_copied, 1)
                hold(act, k.held, counts_copied, t + 3)
                nc.scalar.activation(k.no_edge[:, bass.ds(t, 1), :].rearrange("p a (b c) -> p (a b) c", c=SW),
                                     mine, ACT.Relu, bias=k.far[0:T, :], scale=-FAR).then_inc(no_edge_ready, 1)

            def take_turned(t):
                for g, (s0, w, bank) in enumerate(GROUPS):
                    hold(act, k.held, counts_turned, 3 * t + g + 1)
                    nc.scalar.activation(count_T[:, s0:s0 + w, bass.ds(T * t, T)],
                                         ps[0:T, bank, 0:w * T].rearrange("p (a b) -> p a b", b=T), ACT.Copy
                                         ).then_inc(turned_copied, 1)

            def sum_weighted(piece, b):
                hold(act, k.held, weighted_ready, piece + 1)
                for s in range(2):
                    for h in range(HEADS):
                        mine = weighted[:, b, s, h * C:(h + 1) * C]
                        last = nc.scalar.activation(mine, mine, ACT.Copy,
                                                    accum_out=k.w_att[:, bass.ds(piece, 1), s * HEADS + h])
                last.then_inc(weighted_summed, 1)

            with act.Fori(0, NT - 1) as t:
                take_tile(t)
                for b in range(2):
                    sum_weighted(2 * t + b, b)
                take_turned(t)
            take_tile(NT - 1)
            take_turned(NT - 1)
            nc.scalar.activation(root[:, :], k.deg[:, :], ACT.Sqrt).then_inc(deg_root, 1)


def heads_in(nc, k, a):
    with ExitStack() as mem:
        def sb(name, shape, dt=F32):
            return mem.enter_context(nc.sbuf_tensor(name, shape, dt))

        w_hi = sb("w_hi", [128, KF, D], F32R)
        w_lo = sb("w_lo", [128, KF, D], F32R)
        wa_hi = sb("wa_hi", [128, KF, LAYERS, 2 * HEADS], F32R)
        wa_lo = sb("wa_lo", [128, KF, LAYERS, 2 * HEADS], F32R)
        h_out = [sb(f"h_out{b}", [T, D]) for b in range(2)]
        dst_term = sb("dst_term", [T, HALL, NT])
        rows = sb("term_rows", [TERMS, N])
        src_spread = [sb(f"src_spread{h}", [T, N]) for h in range(HEADS)]
        scores = [sb(f"scores{b}", [T, N], BF16) for b in range(2)]
        top = sb("top", [T, HEADS, NT])
        low = sb("low", [T, HEADS, NT])
        lifts = sb("lifts", [T, NT, TERMS])
        deg_top = sb("deg_top", [T, 1])
        all_top = sb("all_top", [1, 1])
        w_raw = k.w_raw
        ps = k.ps
        shares = [(0, 416, 4), (416, 416, 5), (832, N - 832, 6)]

        deg_step = k.sem("deg_step")
        wa_split = k.sem("wa_split")
        terms_summed = k.sem("terms_summed")
        rows_turned = k.sem("rows_turned")
        rows_copied = k.sem("rows_copied")
        rows_stored = k.sem("rows_stored")
        spread_loaded = [k.sem(f"spread_loaded{h}") for h in range(HEADS)]
        raw_loaded = k.sem("raw_loaded")
        w_hi_ready = k.sem("w_hi_ready")
        w_lo_ready = k.sem("w_lo_ready")
        h_summed = k.sem("h_summed")
        h_copied = k.sem("h_copied")
        h_stored = [k.sem(f"h_stored{b}") for b in range(2)]
        terms_taken = k.sem("terms_taken")
        maxima_step = k.sem("maxima_step")
        lift_step = k.sem("lift_step")
        LIFT = 5
        DEG_AT = NT * TERMS

        block = mem.enter_context(nc.Block())
        w_all = a["W_gat"].rearrange("l (k p) n -> p l k n", p=128)
        layer_maxima = NT * HEADS

        def w_att_of(l):
            at = (LAYERS - 1 - l) * KF
            return k.w_att[:, at:at + KF, :]

        part_k = KF // PARTS

        @block.sync
        def _(sp):
            def load_weights(l):
                sp.dma_start(w_raw[:, :, :], w_all[:, bass.ds(l, 1), :, :].rearrange("p l k n -> p (l k) n")
                             ).then_inc(raw_loaded, 16)

            def load_spread(l, h):
                sp.dma_start(src_spread[h][:, :], k.src_row_d[bass.ds(l * 2 * HEADS + h, 1), :].to_broadcast([T, N])
                             ).then_inc(spread_loaded[h], 16)

            sp.wait_ge(rows_stored, 16)
            for h in range(HEADS):
                load_spread(0, h)
            with sp.Fori(0, LAYERS - 1) as l:
                sp.wait_ge(w_lo_ready, PARTS * (l + 1))
                load_weights(l + 1)
                for h in range(HEADS):
                    sp.wait_ge(maxima_step, l * layer_maxima + (h + 1) * NT + 1)
                    load_spread(l + 1, h)

        @block.scalar
        def _(act):
            for l in range(LAYERS):
                nc.scalar.activation(wa_hi[:, :, l, :], w_att_of(l), ACT.Copy).then_inc(wa_split, 1)
            act.sem_inc(h_copied, 2)

            def high_weights():
                for part in range(PARTS):
                    ks = slice(part_k * part, part_k * (part + 1))
                    nc.scalar.activation(w_hi[:, ks, :], w_raw[:, ks, :], ACT.Copy).then_inc(w_hi_ready, 1)

            def multiply_layer(l):
                for t in range(NT):
                    act.wait_ge(h_summed, l * NT + t + 1)
                    act.wait_ge(h_stored[t % 2], (l * (NT // 2) + t // 2 + 1) * 16)
                    nc.scalar.activation(h_out[t % 2][:, :].rearrange("p (s n) -> p s n", s=2),
                                         ps[0:T, 2 * (t % 2):2 * (t % 2) + 2, 0:D // 2], ACT.Copy).then_inc(h_copied, 1)
                    act.wait_ge(h_copied, l * NT + t + 3)
                    act.dma_start(k.h_d[:, bass.ds(l * HEADS, HEADS), t, :],
                                  h_out[t % 2][:, :].rearrange("p (h c) -> p h c", c=C)).then_inc(h_stored[t % 2], 16)

            high_weights()
            for n, (at, w, bank) in enumerate(shares):
                act.wait_ge(terms_summed, n + 1)
                nc.scalar.activation(rows[:, at:at + w], ps[0:TERMS, bank, 0:w], ACT.Copy).then_inc(rows_copied, 1)
            act.wait_ge(rows_copied, 3)
            act.dma_start(k.src_row_d, rows[:, :]).then_inc(rows_stored, 16)
            act.sem_inc(h_stored[0], 16)
            act.sem_inc(h_stored[1], 16)
            with act.Fori(0, LAYERS - 1) as l:
                multiply_layer(l)
                act.wait_ge(raw_loaded, (l + 1) * 16)
                act.wait_ge(h_copied, (l + 1) * NT + 2)
                high_weights()
            multiply_layer(LAYERS - 1)
            for g, w in ((0, 4), (1, 4), (2, 2)):
                act.wait_ge(rows_turned, g + 2)
                nc.scalar.activation(rows[:, 4 * g * T:(4 * g + w) * T], ps[0:TERMS, 4 + g, 0:w * T],
                                     ACT.Copy).then_inc(rows_copied, 1)
            act.wait_ge(rows_copied, 6)
            act.dma_start(k.lift_d, rows[:, :]).then_inc(rows_stored, 16)
            act.wait_ge(rows_stored, 32)
            for b in range(2):
                act.wait_ge(h_stored[b], (LAYERS * (NT // 2) + 1) * 16)

        @block.vector
        def _(dve):
            nc.vector.tensor_reduce(deg_top[:, :], k.deg[:, :], op=ALU.max, axis=AX_X).then_inc(deg_step, 1)
            dve.wait_ge(wa_split, LAYERS)
            for l in range(LAYERS):
                last = split_low(nc, wa_lo[:, :, l, :], w_att_of(l), wa_hi[:, :, l, :])
            last.then_inc(wa_split, 1)

            def low_weights(l):
                for part in range(PARTS):
                    ks = slice(part_k * part, part_k * (part + 1))
                    dve.wait_ge(w_hi_ready, PARTS * l + part + 1)
                    split_low(nc, w_lo[:, ks, :], w_raw[:, ks, :], w_hi[:, ks, :]).then_inc(w_lo_ready, 1)

            low_weights(0)
            dve.wait_ge(rows_turned, 1)
            by_head = ps[0:T, 7, 0:NT * TERMS].rearrange("p (t l s h) -> p l s h t", t=NT, l=LAYERS, s=2)

            def all_heads(x):
                return x.rearrange("p (l h) t -> p l h t", l=LAYERS)

            nc.vector.tensor_copy(all_heads(k.src_term[:, :, :]), by_head[:, :, 0, :, :])
            nc.vector.tensor_scalar(all_heads(k.src_drop[:, :, :]), by_head[:, :, 0, :, :], SLOPE - 1.0, None, ALU.mult)
            nc.vector.tensor_copy(all_heads(dst_term[:, :, :]), by_head[:, :, 1, :, :]).then_inc(terms_taken, 1)
            nc.vector.tensor_reduce(all_top[:, :], ps[0:1, 7, DEG_AT:DEG_AT + T], op=ALU.max, axis=AX_X
                                    ).then_inc(deg_step, 1)
            dve.wait_ge(deg_step, 2)
            nc.vector.tensor_scalar(all_top[:, :], all_top[:, :], float(EXACT), None, ALU.is_gt).then_inc(deg_step, 1)
            dve.wait_ge(deg_step, 3)
            nc.vector.tensor_copy(k.large_counts[:, :], all_top[:, :])
            dve.sem_inc(maxima_step, 1)
            dve.wait_ge(terms_taken, 1)

            def take_maxima(l):
                for h in range(HEADS):
                    dve.wait_ge(spread_loaded[h], (l + 1) * 16)
                    for t in range(NT):
                        n = h * NT + t
                        hold(dve, k.held, maxima_step, l * layer_maxima + max(n, 1))
                        nc.vector.tensor_tensor_reduce(
                            out=scores[n % 2][:, :], in0=src_spread[h][:, :], in1=k.no_edge[:, t, 0:N], scale=1.0,
                            scalar=NO_MAX, op0=ALU.subtract, op1=ALU.max,
                            accum_out=top[:, h, t:t + 1]).then_inc(maxima_step, 1)
                dve.wait_ge(maxima_step, (l + 1) * layer_maxima + 1)
                chain = [0]

                def link(ins):
                    chain[0] += 1
                    ins.then_inc(lift_step, 1)
                    dve.wait_ge(lift_step, l * LIFT + chain[0])

                mine = dst_term[:, bass.ds(l * HEADS, HEADS), :]
                link(nc.vector.tensor_tensor(top[:, :, :], top[:, :, :], mine, ALU.add))
                link(nc.vector.tensor_scalar(low[:, :, :], top[:, :, :], SLOPE, None, ALU.mult))
                link(nc.vector.tensor_tensor(top[:, :, :], top[:, :, :], low[:, :, :], ALU.max))
                pairs = lifts[:, :, bass.ds(l * 2 * HEADS, 2 * HEADS)].rearrange("p t (h u) -> p h u t", u=2)
                link(nc.vector.tensor_tensor(pairs[:, :, 0, :], mine, top[:, :, :], ALU.subtract))
                link(nc.vector.scalar_tensor_tensor(out=pairs[:, :, 1, :], in0=mine, scalar=SLOPE,
                                                    in1=top[:, :, :], op0=ALU.mult, op1=ALU.subtract))

            with dve.Fori(0, LAYERS - 1) as l:
                take_maxima(l)
                low_weights(l + 1)
            take_maxima(LAYERS - 1)

        @block.tensor
        def _(pe):
            pe.wait_ge(wa_split, LAYERS + 1)
            for at, w, bank in shares:
                for f in range(KF):
                    nodes = slice(at, at + w)
                    last = three_passes(nc, ps[0:TERMS, bank, 0:w],
                                        (wa_hi[:, f, :, :].rearrange("p l h -> p (l h)"),
                                         wa_lo[:, f, :, :].rearrange("p l h -> p (l h)")),
                                        (k.x1_hi[:, f, nodes], k.x1_lo[:, f, nodes]), f == 0, f == KF - 1)
                last.then_inc(terms_summed, 1)
            pe.wait_ge(rows_copied, len(shares))
            for t in range(NT):
                last = nc.tensor.transpose(ps[0:T, 7, t * TERMS:(t + 1) * TERMS], rows[:, t * T:(t + 1) * T],
                                           k.ident[0:TERMS, 0:TERMS])
            pe.wait_ge(deg_step, 1)
            last = nc.tensor.transpose(ps[0:1, 7, DEG_AT:DEG_AT + T], deg_top[:, :], k.ident[0:T, 0:T])
            last.then_inc(rows_turned, 1)
            with pe.Fori(0, LAYERS) as l:
                for t in range(NT):
                    pe.wait_ge(h_copied, l * NT + t + 1)
                    for f in range(KF):
                        if t == 0 and f % part_k == 0:
                            pe.wait_ge(w_lo_ready, PARTS * l + f // part_k + 1)
                        for s in range(2):
                            nodes = slice(t * T, (t + 1) * T)
                            cols = slice(s * D // 2, (s + 1) * D // 2)
                            last = three_passes(nc, ps[0:T, 2 * (t % 2) + s, 0:D // 2],
                                                (k.x1_hi[:, f, nodes], k.x1_lo[:, f, nodes]),
                                                (w_hi[:, f, cols], w_lo[:, f, cols]), f == 0, f == KF - 1)
                    last.then_inc(h_summed, 1)
            pe.wait_ge(lift_step, LIFT * LAYERS)
            for t in range(NT):
                last = nc.tensor.transpose(ps[0:TERMS, 4 + t // 4, (t % 4) * T:(t % 4 + 1) * T], lifts[:, t, :],
                                           k.ident[0:T, 0:T])
                if t % 4 == 3 or t == NT - 1:
                    last.then_inc(rows_turned, 1)


def attend(nc, k, a, count_T, wo_raw):
    with ExitStack() as mem:
        def sb(name, shape, dt=F32):
            return mem.enter_context(nc.sbuf_tensor(name, shape, dt))

        lift = [sb(f"lift{q}", [T, 2, N]) for q in range(2)]
        h_in = [sb(f"h_in{q}", [T, NT, C + 1]) for q in range(2)]
        score = [sb(f"score{r}", [T, HALF]) for r in range(RING)]
        weight = [sb(f"weight{r}", [T, HALF]) for r in range(RING)]
        sums = [sb(f"sums{g}", [T, GT, C + 1]) for g in range(2)]
        inverse = [sb(f"inverse{g}", [T, GT, 1]) for g in range(2)]
        normed = [sb(f"normed{g}", [T, GT, C]) for g in range(2)]
        bias = sb("gat_bias", [T, HALL + 1, C])
        ps = k.ps
        banks = [ps[0:T, 3 * g:3 * g + 3, :].rearrange("p b (m n) -> p (b m) n", m=2) for g in range(2)]

        wo_loaded = k.sem("wo_loaded")
        bias_loaded = k.sem("gat_bias_loaded")
        lift_loaded = [[k.sem(f"lift_loaded{q}_{g}") for g in range(2)] for q in range(2)]
        h_loaded = [[k.sem(f"h_loaded{q}_{g}") for g in range(2)] for q in range(2)]
        ones_set = k.sem("ones_set")
        score_ready = k.sem("score_ready")
        exp_ready = k.sem("exp_ready")
        weight_ready = k.sem("weight_ready")
        weight_used = k.sem("weight_used")
        sums_copied = k.sem("sums_copied")
        norm_step = k.sem("norm_step")
        biased = k.sem("biased")
        cat_stored = [k.sem(f"cat_stored{g}") for g in range(2)]

        PAIR = 4 * NT
        GROUPS = 4
        block = mem.enter_context(nc.Block())

        def group_of(i):
            return i // NT % 2, i % NT, i // (2 * NT)

        @block.sync
        def _(sp):
            def load_head(head, q):
                for g in range(2):
                    cols = slice(g * HALF, (g + 1) * HALF)
                    tiles = slice(g * GT, (g + 1) * GT)
                    sp.dma_start(lift[q][:, :, cols], k.lift_d[bass.ds(2 * head, 2), cols].rearrange(
                        "(o u) n -> o u n", o=1).to_broadcast([T, 2, HALF])).then_inc(lift_loaded[q][g], 16)
                    sp.dma_start(h_in[q][:, tiles, 0:C], k.h_d[:, bass.ds(head, 1), tiles, :].rearrange(
                        "p o t c -> p (o t) c")).then_inc(h_loaded[q][g], 16)

            load_head(0, 0)
            sp.wait_ge(h_loaded[0][1], 16)
            load_head(1, 1)
            sp.dma_start(bias[:, 1:, :], a["b_gat"].rearrange("(o h c) -> o h c", o=1, c=C).to_broadcast([T, HALL, C])
                         ).then_inc(bias_loaded, 16)
            sp.wait_ge(h_loaded[1][1], 16)
            sp.dma_start(wo_raw[:, :, :], a["W_out"].rearrange("(k p) n -> p k n", p=128)).then_inc(wo_loaded, 16)
            sp.sem_inc(cat_stored[0], 16)
            sp.sem_inc(cat_stored[1], 16)

            def store(n, g, slot):
                sp.wait_ge(biased, n + 1)
                sp.dma_start(k.cat_d[:, g * GT:(g + 1) * GT, bass.ds(slot, 1), :].rearrange("p t o c -> p t (o c)"),
                             normed[g][:, :, :]).then_inc(cat_stored[g], 16)

            def store_group(p, gg):
                store(p * GROUPS + gg, (gg + 1) % 2, 2 * p + (gg + 1) // 2)

            with sp.Fori(0, HALL // 2 - 1) as p:
                for gg in range(GROUPS):
                    store_group(p, gg)
                    if gg >= 2:
                        q = gg - 2
                        sp.wait_ge(weight_used, p * PAIR + 2 * NT * (q + 1) + RING)
                        load_head(2 * (p + 1) + q, q)
            sp.sem_inc(lift_loaded[0][0], 16)
            for gg in range(GROUPS):
                store_group(HALL // 2 - 1, gg)
            store(2 * HALL, 1, HALL)
            sp.wait_ge(wo_loaded, 16)
            for g in range(2):
                sp.wait_ge(cat_stored[g], (HALL + 1 + g) * 16)

        @block.vector
        def _(dve):
            dve.sem_inc(weight_ready, RING)
            dve.sem_inc(weight_used, RING - 1)
            dve.sem_inc(norm_step, 6)

            def make_score(p, i):
                g, s, q = group_of(i)
                cols = slice(g * HALF, (g + 1) * HALF)
                if s == 0:
                    dve.wait_ge(lift_loaded[q][g], (p + 1) * 16)
                head = 2 * (p % (HALL // 2)) + q
                dve.wait_ge(weight_ready, p * PAIR + i + 1)
                nc.vector.scalar_tensor_tensor(out=score[i % RING][:, :], in0=lift[q][:, 1, cols],
                                               scalar=k.src_drop[:, bass.ds(head, 1), s], in1=lift[q][:, 0, cols],
                                               op0=ALU.add, op1=ALU.max).then_inc(score_ready, 1)

            def normalise(n, g, before):
                dve.wait_ge(sums_copied, n + 2)
                base = 6 + 3 * n
                nc.vector.tensor_scalar(inverse[g][:, :, :], sums[g][:, :, C:C + 1], 1e-16, None,
                                        ALU.add).then_inc(norm_step, 1)
                dve.wait_ge(norm_step, base + 1)
                nc.vector.reciprocal(inverse[g][:, :, :], inverse[g][:, :, :]).then_inc(norm_step, 1)
                dve.wait_ge(norm_step, base + 2)
                dve.wait_ge(cat_stored[g], before * 16 + 16)
                nc.vector.tensor_tensor(normed[g][:, :, :], sums[g][:, :, 0:C],
                                        inverse[g][:, :, :].to_broadcast([T, GT, C]), ALU.mult).then_inc(norm_step, 1)

            make_score(0, 0)
            with dve.Fori(0, HALL // 2) as p:
                for i in range(PAIR):
                    g, s, q = group_of(i)
                    make_score(p + (i + 1) // PAIR, (i + 1) % PAIR)
                    dve.wait_ge(exp_ready, p * PAIR + i + 1)
                    dve.wait_ge(weight_used, p * PAIR + i + 1)
                    nc.vector.scalar_tensor_tensor(out=weight[i % RING][:, :], in0=score[i % RING][:, :], scalar=EXP_CAP,
                                                   in1=count_T[:, s, g * HALF:(g + 1) * HALF], op0=ALU.min,
                                                   op1=ALU.mult).then_inc(weight_ready, 1)
                    if s == 6:
                        gg = i // NT
                        normalise(p * GROUPS + gg, (gg + 1) % 2, 2 * p + gg // 2)
            normalise(2 * HALL, 1, HALL)

        @block.scalar
        def _(act):
            act.sem_inc(sums_copied, 1)

            def copy_sums(n, g):
                act.wait_ge(weight_used, n * NT + RING)
                act.wait_ge(norm_step, 3 * n + 3)
                nc.scalar.activation(sums[g][:, :, :], banks[g][:, 0:GT, 0:C + 1], ACT.Copy).then_inc(sums_copied, 1)

            with act.Fori(0, HALL // 2) as p:
                for i in range(PAIR):
                    g, s, q = group_of(i)
                    hold(act, k.held, score_ready, p * PAIR + i + 1)
                    nc.scalar.activation(score[i % RING][:, :], score[i % RING][:, :], ACT.Exp,
                                         bias=k.src_term[:, bass.ds(2 * p + q, 1), s]).then_inc(exp_ready, 1)
                    if s == 3:
                        gg = i // NT
                        copy_sums(p * GROUPS + gg, (gg + 1) % 2)
            copy_sums(2 * HALL, 1)

        @block.tensor
        def _(pe):
            for b in range(3):
                for half in range(2):
                    last = nc.tensor.matmul(ps[0:T, 3 + b, half * 256:(half + 1) * 256], k.zeros[0:T, 0:T],
                                            k.zeros[0:T, 0:256], start=True, stop=True)
            last.then_inc(weight_used, 1)
            pe.wait_ge(ones_set, 2)
            with pe.Fori(0, HALL // 2) as p:
                for i in range(PAIR):
                    g, s, q = group_of(i)
                    if s == 0:
                        pe.wait_ge(sums_copied, p * GROUPS + i // NT + 1)
                    pe.wait_ge(weight_ready, p * PAIR + i + 1 + RING)
                    if g == 0 and s % GT == 0:
                        pe.wait_ge(h_loaded[q][s // GT], (p + 1) * 16)
                    for t in range(GT):
                        last = nc.tensor.matmul(banks[g][:, t, 0:C + 1], weight[i % RING][:, t * T:(t + 1) * T],
                                                h_in[q][:, s, :], start=(s == 0 and t % 2 == 0), stop=(s == NT - 1),
                                                skip_group_check=True)
                    last.then_inc(weight_used, 1)

        @block.gpsimd
        def _(pool):
            for q in range(2):
                nc.gpsimd.memset(h_in[q][:, :, C:C + 1], 1.0).then_inc(ones_set, 1)
            nc.gpsimd.memset(bias[:, 0:1, :], 0.0).then_inc(ones_set, 1)
            pool.wait_ge(ones_set, 3)
            pool.wait_ge(bias_loaded, 16)

            def add_bias(n, g, slot):
                hold(pool, k.held, norm_step, 3 * n + 9)
                nc.gpsimd.tensor_tensor(normed[g][:, :, :], normed[g][:, :, :],
                                        bias[:, bass.ds(slot, 1), :].to_broadcast([T, GT, C]), ALU.add
                                        ).then_inc(biased, 1)

            with pool.Fori(0, HALL // 2) as p:
                for gg in range(GROUPS):
                    add_bias(p * GROUPS + gg, (gg + 1) % 2, 2 * p + (gg + 1) // 2)
            add_bias(2 * HALL, 1, HALL)


def combine(nc, k, a, wo_raw, wo_lo, xs_raw):
    with ExitStack() as mem:
        def sb(name, shape, dt=F32):
            return mem.enter_context(nc.sbuf_tensor(name, shape, dt))

        groups = [(f, min(4, KO - f)) for f in range(0, KO, 4)]
        NG = len(groups)
        BANKS = (0, 1, 2, 7, 0)
        AHEAD = 2
        WHILE_LOADED = 6
        LN = 5
        wo_hi = sb("wo_hi", [128, KO, D], F32R)
        cat = [sb(f"cat{g}", [T, w * 128]) for g, (f, w) in enumerate(groups)]
        catT_hi = [sb(f"catT_hi{g}", [128, w, T], F32R) for g, (f, w) in enumerate(groups)]
        catT_lo = [sb(f"catT_lo{g}", [128, w, T], F32R) for g, (f, w) in enumerate(groups)]
        x_in = sb("x_res", [T, D])
        y = sb("y_pre", [T, D])
        stats = sb("stats", [T, 2, 6])
        mean_var = sb("mean_var", [T, 2])
        rstd = sb("rstd", [T, 1])
        b_row = sb("b_out_row", [T, D])
        ps = k.ps

        wo_hi_ready = k.sem("wo_hi_ready")
        wo_lo_ready = k.sem("wo_lo_ready")
        row_loaded = k.sem("b_out_loaded")
        cat_loaded = [k.sem(f"cat_loaded{g}") for g in range(NG)]
        x_loaded = k.sem("x_res_loaded")
        cat_turned = k.sem("cat_turned")
        catT_hi_ready = k.sem("catT_hi_ready")
        catT_lo_ready = k.sem("catT_lo_ready")
        out_summed = k.sem("out_summed")
        ln_step = k.sem("ln_step")
        rstd_step = k.sem("rstd_step")
        x2_ready = k.sem("x2_ready")
        x2_scaled = k.sem("x2_scaled")
        x2_stored = k.sem("x2_stored")
        block = mem.enter_context(nc.Block())

        def turned(g):
            w = groups[g][1]
            return ps[:, BANKS[g], 0:w * T].rearrange("p (k n) -> p k n", n=T)

        @block.sync
        def _(sp):
            def load_cat(t, g):
                f, w = groups[g]
                sp.dma_start(cat[g][:, :], k.cat_d[:, bass.ds(t, 1), 1:, :].rearrange("p o h c -> p (o h c)")[
                    :, f * 128:(f + w) * 128]).then_inc(cat_loaded[g], 16)

            def load_x(t):
                sp.dma_start(x_in[:, :], a["x"][bass.ds(t * T, T), :]).then_inc(x_loaded, 16)

            for g in range(NG):
                load_cat(0, g)
            load_x(0)
            sp.dma_start(b_row[:, :], a["b_out"].rearrange("(o n) -> o n", o=1).to_broadcast([T, D])
                         ).then_inc(row_loaded, 16)
            sp.sem_inc(x2_stored, 16)
            with sp.Fori(0, NT) as t:
                after = (t + 1) % NT
                for g in range(NG):
                    sp.wait_ge(cat_turned, t * NG + g + 1)
                    load_cat(after, g)
                sp.wait_ge(ln_step, (t + 2) * LN + 2)
                load_x(after)
                sp.wait_ge(x2_ready, t + 1)
                sp.dma_start(k.x2_d[:, bass.ds(t, 1), :].rearrange("p o n -> p (o n)"), y[:, :]).then_inc(x2_stored, 16)
            sp.wait_ge(x2_stored, NT * 16 + 16)
            for g in range(NG):
                sp.wait_ge(cat_loaded[g], NT * 16 + 16)
            sp.wait_ge(x_loaded, NT * 16 + 16)

        @block.gpsimd
        def _(pool):
            with pool.Fori(0, NT) as t:
                pool.wait_ge(ln_step, (t + 2) * LN + LN)
                nc.gpsimd.tensor_tensor(rstd[:, :], mean_var[:, 1:2], k.eps[0:T, :], ALU.add).then_inc(rstd_step, 1)
                pool.wait_ge(rstd_step, 2 * t + 1)
                nc.gpsimd.tensor_tensor(rstd[:, :], rstd[:, :], k.neg_half[0:T, :], ALU.pow).then_inc(rstd_step, 1)
                hold(pool, k.held, x2_ready, t + 1)
                nc.gpsimd.tensor_tensor(xs_raw[:, bass.ds(t, 1), :].rearrange("p o n -> p (o n)"), y[:, :],
                                        k.dinv[:, bass.ds(t, 1)].to_broadcast([T, D]), ALU.mult).then_inc(x2_scaled, 1)

        @block.scalar
        def _(act):
            def high_group(t, g):
                act.wait_ge(cat_turned, t * NG + g + 1)
                nc.scalar.activation(catT_hi[g][:, :, :], turned(g), ACT.Relu).then_inc(catT_hi_ready, 1)

            def high_weights(first, end):
                for f in range(first, end):
                    nc.scalar.activation(wo_hi[:, f, :], wo_raw[:, f, :], ACT.Copy).then_inc(wo_hi_ready, 1)

            high_weights(0, WHILE_LOADED)
            for g in range(AHEAD):
                high_group(0, g)
            high_weights(WHILE_LOADED, KO)
            with act.Fori(0, NT) as t:
                for g in range(NG):
                    high_group(t + (g + AHEAD) // NG, (g + AHEAD) % NG)

        @block.vector
        def _(dve):
            def low_group(t, g):
                dve.wait_ge(catT_hi_ready, t * NG + g + 1)
                nc.vector.scalar_tensor_tensor(out=catT_lo[g][:, :, :], in0=turned(g), scalar=0.0,
                                               in1=catT_hi[g][:, :, :].bitcast(F32), op0=ALU.max,
                                               op1=ALU.subtract).then_inc(catT_lo_ready, 1)

            def low_weights(first, end):
                for f in range(first, end):
                    dve.wait_ge(wo_hi_ready, f + 1)
                    split_low(nc, wo_lo[:, f, :], wo_raw[:, f, :], wo_hi[:, f, :]).then_inc(wo_lo_ready, 1)

            low_weights(0, WHILE_LOADED)
            for g in range(AHEAD):
                low_group(0, g)
            low_weights(WHILE_LOADED, KO)
            dve.wait_ge(row_loaded, 16)
            with dve.Fori(0, NT) as t:
                for g in range(NG):
                    low_group(t + (g + AHEAD) // NG, (g + AHEAD) % NG)
                step = [0]

                def link(ins):
                    step[0] += 1
                    ins.then_inc(ln_step, 1)
                    hold(dve, k.held, ln_step, (t + 2) * LN + step[0])

                dve.wait_ge(x2_stored, t * 16 + 16)
                dve.wait_ge(x2_scaled, t + 1)
                hold(dve, k.held, out_summed, t + 1)
                link(nc.vector.tensor_tensor(y[:, :].rearrange("p (s n) -> p s n", s=2),
                                             ps[0:T, bass.ds(3 + 2 * (t % 2), 2), 0:384],
                                             b_row[:, :].rearrange("p (s n) -> p s n", s=2), ALU.add))
                dve.wait_ge(x_loaded, 16 * t + 16)
                link(nc.vector.scalar_tensor_tensor(out=y[:, :], in0=y[:, :], scalar=0.0, in1=x_in[:, :], op0=ALU.max,
                                                    op1=ALU.add))
                link(nc.vector.bn_stats(stats[:, 0, :], y[:, 0:384]))
                link(nc.vector.bn_stats(stats[:, 1, :], y[:, 384:768]))
                link(nc.vector.bn_aggr(mean_var[:, :], stats[:, :, :]))
                dve.wait_ge(rstd_step, 2 * t + 2)
                nc.vector.tensor_scalar(y[:, :], y[:, :], mean_var[:, 0:1], rstd[:, :], ALU.subtract, ALU.mult
                                        ).then_inc(x2_ready, 1)

        @block.tensor
        def _(pe):
            pe.sem_inc(x2_scaled, 1)
            pe.sem_inc(ln_step, 2 * LN)

            def turn_group(t, g):
                f, w = groups[g]
                pe.wait_ge(cat_loaded[g], 16 * t + 16)
                for j in range(w):
                    last = nc.tensor.transpose(ps[:, BANKS[g], j * T:(j + 1) * T], cat[g][:, j * 128:(j + 1) * 128],
                                               k.ident[0:T, 0:T])
                last.then_inc(cat_turned, 1)

            for g in range(AHEAD):
                turn_group(0, g)
            with pe.Fori(0, NT) as t:
                pe.wait_ge(ln_step, t * LN + 1)
                for g, (f0, w) in enumerate(groups):
                    ahead = g + AHEAD
                    if ahead == NG:
                        pe.wait_ge(catT_lo_ready, t * NG + NG)
                    turn_group(t + ahead // NG, ahead % NG)
                    pe.wait_ge(catT_lo_ready, t * NG + g + 1)
                    pe.wait_ge(wo_lo_ready, f0 + w)
                    for f in range(w):
                        for s in range(2):
                            cols = slice(s * 384, (s + 1) * 384)
                            last = three_passes(nc, ps[0:T, bass.ds(3 + s + 2 * (t % 2), 1), 0:384].rearrange(
                                "p o n -> p (o n)"), (catT_hi[g][:, f, :], catT_lo[g][:, f, :]),
                                (wo_hi[:, f0 + f, cols], wo_lo[:, f0 + f, cols]), f0 + f == 0, f0 + f == KO - 1)
                last.then_inc(out_summed, 1)


def convolve(nc, k, a, count_T, xs_raw, out):
    with ExitStack() as mem:
        def sb(name, shape, dt=F32):
            return mem.enter_context(nc.sbuf_tensor(name, shape, dt))

        P = 2 * T
        BANKS = KF // 2
        LN = 3
        xs_hi = sb("xs_hi", [T, NT, D], F32R)
        xs_lo = sb("xs_lo", [T, NT, D], F32R)
        w_raw, w_lo = raw_and_low(nc, mem, "gcn_w", KF)
        w_hi = sb("gcn_w_hi", [128, KF, D], F32R)
        agg_hi = sb("agg_hi", [128, KF, P], F32R)
        agg_lo = sb("agg_lo", [128, KF, P], F32R)
        chunk = sb("count_chunk", [T, NT, 2 * P], F32R)
        chunk_whole = nc.alloc_sbuf_tensor_at("count_chunk_whole", [T, NT, 2 * P], F32,
                                              offset=nc.sbuf_base - NT * 2 * P * 4)
        x2 = [sb(f"x2_in{j}", [T, D]) for j in range(2)]
        y = [sb(f"y_gcn{j}", [T, D]) for j in range(2)]
        b_rows = sb("gcn_b_rows", [T, 2, D])
        stats = [sb(f"gcn_stats{j}", [T, 2, 6]) for j in range(2)]
        mean_var = [sb(f"gcn_mean_var{j}", [T, 2]) for j in range(2)]
        rstd = [sb(f"gcn_rstd{j}", [T, 1]) for j in range(2)]
        ps = k.ps
        summed = ps[:, 0:BANKS, :].rearrange("p b (m n) -> p (b m) n", m=2)

        w_loaded = [k.sem(f"gcn_w_loaded{part}") for part in range(PARTS)]
        w_hi_ready = k.sem("gcn_w_hi_ready")
        w_lo_ready = k.sem("gcn_w_lo_ready")
        rows_loaded = k.sem("gcn_rows_loaded")
        xs_hi_ready = k.sem("xs_hi_ready")
        xs_lo_ready = k.sem("xs_lo_ready")
        first_widened = k.sem("first_widened")
        chunk_ready = k.sem("chunk_ready")
        agg_summed = k.sem("agg_summed")
        agg_hi_ready = k.sem("agg_hi_ready")
        agg_lo_ready = k.sem("agg_lo_ready")
        gcn_summed = k.sem("gcn_summed")
        y_ready = k.sem("y_ready")
        xs_next = k.sem("xs_next")
        x2_loaded = [k.sem(f"x2_loaded{j}") for j in range(2)]
        x2_biased = k.sem("x2_biased")
        ln_step = k.sem("gcn_ln_step")
        rstd_step = k.sem("gcn_rstd_step")
        result_ready = k.sem("result_ready")
        out_stored = [k.sem(f"out_stored{j}") for j in range(2)]
        part_k = KF // PARTS
        block = mem.enter_context(nc.Block())

        def load_path(eng):
            return eng.value_load(k.large_counts[0:1, 0:1], min_val=0, max_val=1)

        @block.sync
        def _(sp):
            def load_weights(w):
                for part in range(PARTS):
                    sp.dma_start(w_raw[:, part * part_k:(part + 1) * part_k, :],
                                 w[part * part_k * 128:(part + 1) * part_k * 128, :].rearrange("(k p) n -> p k n", p=128)
                                 ).then_inc(w_loaded[part], 16)

            def load_x2(c, j):
                sp.dma_start(x2[j][:, :], k.x2_d[:, bass.ds(2 * c + j, 1), :].rearrange("p o n -> p (o n)")
                             ).then_inc(x2_loaded[j], 16)

            load_weights(a["W1"])
            for n, b in enumerate((a["b1"], a["b2"])):
                sp.dma_start(b_rows[:, n, :], b.rearrange("(o n) -> o n", o=1).to_broadcast([T, D])
                             ).then_inc(rows_loaded, 16)
            for j in range(2):
                load_x2(0, j)
                sp.sem_inc(out_stored[j], 16)
            sp.wait_ge(gcn_summed, NT)
            load_weights(a["W2"])
            with sp.Fori(0, PAIRS) as c:
                for j in range(2):
                    sp.wait_ge(y_ready, NT + 2 * c + 2 + j + 1)
                    load_x2((c + 1) % PAIRS, j)
                for j in range(2):
                    sp.wait_ge(result_ready, 2 * c + j + 1)
                    sp.dma_start(out[bass.ds(P * c + j * T, T), :], y[j][:, :]).then_inc(out_stored[j], 16)
            for j in range(2):
                sp.wait_ge(out_stored[j], 16 * PAIRS + 16)
                sp.wait_ge(x2_loaded[j], 16 * PAIRS + 16)

        @block.gpsimd
        def _(pool):
            large = load_path(nc.gpsimd)

            def widen(n):
                hold(pool, k.held, agg_summed, BANKS * n + BANKS)
                for path, to in enumerate((chunk, chunk_whole)):
                    with pool.If(large < 1 if path == 0 else large > 0):
                        nc.gpsimd.tensor_copy(to[:, :, bass.ds(P * (n % 2), P)],
                                              count_T[:, :, bass.ds(P * (n % PAIRS), P)]).then_inc(chunk_ready, 1)

            for path, to in enumerate((chunk, chunk_whole)):
                with pool.If(large < 1 if path == 0 else large > 0):
                    for s in range(NT):
                        nc.gpsimd.tensor_copy(to[:, s, 0:P], count_T[:, s, 0:P]).then_inc(first_widened, 1)
            with pool.Fori(0, PAIRS) as c:
                widen(c + 1)
            pool.wait_ge(rows_loaded, 32)
            with pool.Fori(0, PAIRS) as c:
                widen(c + PAIRS + 1)
                for j in range(2):
                    pool.wait_ge(x2_loaded[j], 16 * c + 16)
                    nc.gpsimd.tensor_tensor(x2[j][:, :], x2[j][:, :], b_rows[:, 1, :], ALU.add).then_inc(x2_biased, 1)
                for j in range(2):
                    n = 2 * c + j
                    pool.wait_ge(ln_step, LN * n + LN)
                    nc.gpsimd.tensor_tensor(rstd[j][:, :], mean_var[j][:, 1:2], k.eps[0:T, :], ALU.add
                                            ).then_inc(rstd_step, 1)
                    pool.wait_ge(rstd_step, 2 * n + 1)
                    nc.gpsimd.tensor_tensor(rstd[j][:, :], rstd[j][:, :], k.neg_half[0:T, :], ALU.pow
                                            ).then_inc(rstd_step, 1)

        @block.scalar
        def _(act):
            def high_xs(t, layer):
                if layer:
                    act.wait_ge(xs_next, t + 3)
                nc.scalar.activation(xs_hi[:, t, :], xs_raw[:, t, :], ACT.Copy).then_inc(xs_hi_ready, 1)

            def high_weights(layer):
                for part in range(PARTS):
                    act.wait_ge(w_loaded[part], 16 * layer + 16)
                    ks = slice(part * part_k, (part + 1) * part_k)
                    nc.scalar.activation(w_hi[:, ks, :], w_raw[:, ks, :], ACT.Copy).then_inc(w_hi_ready, 1)

            def high_agg(n):
                for b in range(BANKS):
                    ms = slice(2 * b, 2 * b + 2)
                    act.wait_ge(agg_summed, BANKS * (n + 2) + b + 1)
                    nc.scalar.activation(agg_hi[:, ms, :], summed[:, ms, 0:P], ACT.Copy).then_inc(agg_hi_ready, 1)

            def activate(c, j):
                hold(act, k.held, y_ready, 2 * c + j + 3)
                nc.scalar.activation(xs_raw[:, bass.ds(2 * c + j, 1), :].rearrange("p o n -> p (o n)"), y[j][:, :],
                                     ACT.Relu, scale=k.dinv[:, bass.ds(2 * c + j, 1)]).then_inc(xs_next, 1)

            for t in range(NT):
                high_xs(t, 0)
            high_weights(0)
            act.sem_inc(xs_next, 2)
            with act.Fori(0, PAIRS - 1) as c:
                high_agg(c)
                for j in range(2):
                    activate(c, j)
            high_agg(PAIRS - 1)
            for t in range(NT - 2):
                high_xs(t, 1)
            for j in range(2):
                activate(PAIRS - 1, j)
                high_xs(NT - 2 + j, 1)
            high_weights(1)
            with act.Fori(PAIRS, 2 * PAIRS) as n:
                high_agg(n)

        @block.vector
        def _(dve):
            def low_xs(t, layer):
                dve.wait_ge(xs_hi_ready, layer * NT + t + 1)
                split_low(nc, xs_lo[:, t, :], xs_raw[:, t, :], xs_hi[:, t, :]).then_inc(xs_lo_ready, 1)

            def low_weights(layer):
                for part in range(PARTS):
                    dve.wait_ge(w_hi_ready, PARTS * layer + part + 1)
                    ks = slice(part * part_k, (part + 1) * part_k)
                    split_low(nc, w_lo[:, ks, :], w_raw[:, ks, :], w_hi[:, ks, :]).then_inc(w_lo_ready, 1)

            def low_agg(n):
                for b in range(BANKS):
                    ms = slice(2 * b, 2 * b + 2)
                    dve.wait_ge(agg_hi_ready, BANKS * n + b + 1)
                    split_low(nc, agg_lo[:, ms, :], summed[:, ms, 0:P], agg_hi[:, ms, :]).then_inc(agg_lo_ready, 1)

            def halves(x):
                return x.rearrange("p (s n) -> p s n", s=2)

            def add_row(n, t, j, row):
                hold(dve, k.held, gcn_summed, n + 1)
                nc.vector.scalar_tensor_tensor(
                    out=halves(y[j][:, :]), in0=ps[0:T, 3 + 2 * j:5 + 2 * j, 0:384], scalar=k.dinv[:, bass.ds(t, 1)],
                    in1=halves(row), op0=ALU.mult, op1=ALU.add).then_inc(y_ready, 1)

            def add_first(c, j):
                dve.wait_ge(xs_next, 2 * c + j + 1)
                add_row(2 * c + j, 2 * c + j, j, b_rows[:, 0, :])

            dve.sem_inc(y_ready, 2)
            for t in range(NT):
                low_xs(t, 0)
            low_weights(0)
            dve.wait_ge(rows_loaded, 32)
            with dve.Fori(0, PAIRS - 1) as c:
                low_agg(c)
                for j in range(2):
                    add_first(c, j)
            low_agg(PAIRS - 1)
            for t in range(NT - 4):
                low_xs(t, 1)
            add_first(PAIRS - 1, 0)
            for t in (NT - 4, NT - 3):
                low_xs(t, 1)
            add_first(PAIRS - 1, 1)
            for t in (NT - 2, NT - 1):
                low_xs(t, 1)
            low_weights(1)
            with dve.Fori(0, PAIRS) as c:
                low_agg(c + PAIRS)
                for j in range(2):
                    n = 2 * c + j
                    dve.wait_ge(out_stored[j], 16 * c + 16)
                    dve.wait_ge(x2_biased, n + 1)
                    add_row(n + NT, n, j, x2[j][:, :])
                    hold(dve, k.held, y_ready, n + NT + 3)
                    for s in range(2):
                        nc.vector.bn_stats(stats[j][:, s, :], y[j][:, s * 384:(s + 1) * 384]).then_inc(ln_step, 1)
                    hold(dve, k.held, ln_step, LN * n + 2)
                    nc.vector.bn_aggr(mean_var[j][:, :], stats[j][:, :, :]).then_inc(ln_step, 1)
                    dve.wait_ge(rstd_step, 2 * n + 2)
                    nc.vector.tensor_scalar(y[j][:, :], y[j][:, :], mean_var[j][:, 0:1], rstd[j][:, :],
                                            ALU.subtract, ALU.mult).then_inc(result_ready, 1)

        @block.tensor
        def _(pe):
            pe.sem_inc(agg_summed, 2 * BANKS)

            large = load_path(nc.tensor)

            def both_paths(sums, *given):
                with pe.If(large < 1):
                    sums(xs_hi, xs_lo, chunk, *given)
                with pe.If(large > 0):
                    sums(xs_hi.bitcast(F32), xs_lo.bitcast(F32), chunk_whole, *given)

            def sum_first(hi, lo, chunk):
                for s in range(NT):
                    pe.wait_ge(first_widened, s + 1)
                    pe.wait_ge(xs_lo_ready, s + 1)
                    for m in range(KF):
                        cols = slice(m * 128, (m + 1) * 128)
                        nc.tensor.matmul(summed[:, m, 0:P], hi[:, s, cols], chunk[:, s, 0:P],
                                         start=s == 0 and m % 2 == 0, stop=False, skip_group_check=True)
                        last = nc.tensor.matmul(summed[:, m, 0:P], lo[:, s, cols], chunk[:, s, 0:P], start=False,
                                                stop=s == NT - 1, skip_group_check=True)
                        if s == NT - 1 and m % 2 == 1:
                            last.then_inc(agg_summed, 1)

            def sum_turn(hi, lo, chunk, n, layer):
                pe.wait_ge(chunk_ready, n)
                for m in range(KF):
                    cols = slice(m * 128, (m + 1) * 128)
                    for s in range(NT):
                        if m == 0:
                            pe.wait_ge(xs_lo_ready, layer * NT + s + 1)
                        counts_of = chunk[:, s, bass.ds(P * (n % 2), P)]
                        nc.tensor.matmul(summed[:, m, 0:P], hi[:, s, cols], counts_of, start=s == 0, stop=False)
                        last = nc.tensor.matmul(summed[:, m, 0:P], lo[:, s, cols], counts_of, start=False,
                                                stop=s == NT - 1)
                    if m % 2 == 1:
                        last.then_inc(agg_summed, 1)

            def multiply(n, layer):
                for j in range(2):
                    nodes = slice(j * T, (j + 1) * T)
                    pe.wait_ge(y_ready, 2 * n + j + 1)
                    for f in range(KF):
                        if j == 0 and f % 2 == 0:
                            pe.wait_ge(agg_lo_ready, BANKS * n + f // 2 + 1)
                            pe.wait_ge(w_lo_ready, PARTS * layer + f // part_k + 1)
                        for s in range(2):
                            cols = slice(s * 384, (s + 1) * 384)
                            last = three_passes(nc, ps[0:T, 3 + 2 * j + s, 0:384],
                                                (agg_hi[:, f, nodes], agg_lo[:, f, nodes]),
                                                (w_hi[:, f, cols], w_lo[:, f, cols]), f == 0, f == KF - 1)
                    last.then_inc(gcn_summed, 1)

            both_paths(sum_first)
            multiply(0, 0)
            for layer, first in ((0, 1), (1, PAIRS)):
                with pe.Fori(first, (layer + 1) * PAIRS) as n:
                    both_paths(sum_turn, n, layer)
                    multiply(n, layer)


def program(nc, a, out, stages=6):
    with ExitStack() as ctx:
        k = Core(nc, ctx)

        def sb(name, shape, dt=F32, stack=ctx):
            return stack.enter_context(nc.sbuf_tensor(name, shape, dt))

        k.held = k.sem("held")
        k.ps = ctx.enter_context(nc.psum_tensor("ps", [128, 8, 512], F32))
        k.ident = sb("ident", [128, 128])
        k.zeros = sb("zeros", [128, SW], BF16)
        k.far = sb("far", [128, 1])
        k.eps = sb("eps", [128, 1])
        k.neg_half = sb("neg_half", [128, 1])
        k.deg = sb("deg", [T, NT])
        k.dinv = sb("dinv", [T, NT])
        k.src_term = sb("src_term", [T, HALL, NT])
        k.src_drop = sb("src_drop", [T, HALL, NT])
        k.large_counts = sb("large_counts", [1, 1], I32)
        k.w_att = sb("w_att", [128, LAYERS * KF, 2 * HEADS])
        k.ranges_row = sb("ranges_row", [1, 3 * NT], I32)
        k.h_d = k.dram("h_d", (T, HALL, NT, C))
        k.src_row_d = k.dram("src_row_d", (TERMS, N))
        k.lift_d = k.dram("lift_d", (2 * HALL, N))
        k.cat_d = k.dram("cat_d", (T, NT, HALL + 1, C))
        k.x2_d = k.dram("x2_d", (T, NT, D))
        count_T = sb("count_T", [T, NT, N], U16)
        with ExitStack() as early:
            k.x1_hi = sb("x1_hi", [128, KF, N], F32R, early)
            k.x1_lo = sb("x1_lo", [128, KF, N], F32R, early)
            k.w_raw = sb("w_raw", [128, KF, D], F32, early)
            with ExitStack() as edges:
                k.loop_strip = sb("loop_strip", [T, 2 * N + 2], BF16, edges)
                k.iota_i = sb("iota_i", [128, 3 * SW], I32, edges)
                k.iota_h = sb("iota_h", [128, 3 * SW], F16, edges)
                k.src_col = sb("src_col", [128, CCOLS], F32, edges)
                k.dst_col = sb("dst_col", [128, CCOLS], F16, edges)
                nodes_in(nc, k, a)
                k.no_edge = early.enter_context(nc.sbuf_tensor("no_edge", [T, NT, 3 * SW], BF16, side="right"))
                if stages >= 2:
                    counts(nc, k, a, count_T)
            if stages >= 3:
                heads_in(nc, k, a)
        with ExitStack() as weights:
            xs_raw = sb("xs_raw", [T, NT, D])
            wo_raw, wo_lo = raw_and_low(nc, weights, "wo", KO)
            if stages >= 4:
                attend(nc, k, a, count_T, wo_raw)
            if stages >= 5:
                combine(nc, k, a, wo_raw, wo_lo, xs_raw)
        if stages >= 6:
            convolve(nc, k, a, count_T, xs_raw, out)
        return k


def kernel(**inputs):
    import numpy as np
    import concourse.bacc as bacc
    from concourse.bass_utils import run_bass_kernel_spmd

    given = {n: np.asarray(v) for n, v in inputs.items()}
    gat = "L0_gnn_"
    arrays = {
        "x": given["x"], "src": given["src"], "dst": given["dst"],
        "W_ah": given[gat + "W_ah"], "b_ah_cols": given[gat + "b_ah"].reshape(KF, 128).T,
        "W_gat": np.stack([given[f"{gat}W{i}"] for i in range(LAYERS)]),
        "att_rows": np.stack([np.stack([given[f"{gat}a_src{i}"].reshape(D), given[f"{gat}a_dst{i}"].reshape(D)])
                              for i in range(LAYERS)]),
        "b_gat": np.concatenate([given[f"{gat}b{i}"] for i in range(LAYERS)]),
        "W_out": given[gat + "W_out"], "b_out": given[gat + "b_out"],
        "W1": given["L1_gnn_W1"], "b1": given["L1_gnn_b1"],
        "W2": given["L1_gnn_W2"], "b2": given["L1_gnn_b2"],
    }
    nc = bacc.Bacc("TRN2", target_bir_lowering=False, num_devices=1)
    aps = {}
    for name, value in arrays.items():
        arrays[name] = np.ascontiguousarray(value)
        aps[name] = nc.dram_tensor(name, value.shape, mybir.dt.from_np(value.dtype), kind="ExternalInput").ap()
    out = nc.dram_tensor("out", (N, D), F32, kind="ExternalOutput").ap()
    program(nc, aps, out)
    return run_bass_kernel_spmd(nc, [arrays], core_ids=[0]).results[0]["out"]
```
